# Optimizing a Trainium2 kernel written in Bass

```python
import numpy as np
import jax
import jax.numpy as jnp

def _softmax(x, axis=-1):
    return jax.nn.softmax(x, axis=axis)

def _gelu(x):
    return jax.nn.gelu(x, approximate=True)

def _silu(x):
    return jax.nn.silu(x)

def _sigmoid(x):
    return jax.nn.sigmoid(x)

def _layernorm(x, axis=-1, eps=1e-05):
    m = jnp.mean(x, axis=axis, keepdims=True)
    v = jnp.var(x, axis=axis, keepdims=True)
    return (x - m) / jnp.sqrt(v + eps)

def _scatter_add(tgt, idx, src, axis=0):
    return tgt.at[idx].add(src)

def _segment_sum(src, seg, n):
    return jax.ops.segment_sum(src, seg, n)
kernel_name = 'mk_seq_postln_d2_jaxref_r8_bb2138'

def setup_inputs(seed: int=0):
    np.random.seed(seed)
    _w = jnp.asarray

    def _L0_attn_setup():
        import jax, jax.numpy as jnp
        import numpy as np
        B, S, D = (4, 256, 128)
        key = jax.random.key(seed)
        k1, k2 = jax.random.split(key)
        x = jax.random.normal(k1, (B, S, D), dtype=jnp.float32)
        W = jax.random.normal(k2, (2 * D, D), dtype=jnp.float32) * 0.02
        return {'x': x, 'W': W}
    _L0_attn_in = _L0_attn_setup()

    def _L0_ffn_setup():
        import jax, jax.numpy as jnp
        import numpy as np
        DIM = 128

        def _reference_tuple_inner(x, W_r, W_k, W_v, mu_r, mu_k):
            B, T, C = x.shape
            x_prev = jnp.concatenate([jnp.zeros((B, 1, C), x.dtype), x[:, :-1, :]], axis=1)
            xr = mu_r * x + (1.0 - mu_r) * x_prev
            xk = mu_k * x + (1.0 - mu_k) * x_prev
            r = jax.nn.sigmoid(jnp.einsum('btc,dc->btd', xr, W_r))
            k = jnp.einsum('btc,dc->btd', xk, W_k)
            k_act = jnp.square(jax.nn.relu(k))
            out = r * jnp.einsum('btc,dc->btd', k_act, W_v)
            new_state = x[:, -1, :]
            return (out, new_state)
        key = jax.random.key(seed)
        ks = jax.random.split(key, 6)
        B, T, C = (8, 256, DIM)
        x = jax.random.normal(ks[0], (B, T, C), dtype=jnp.float32)
        s = 1.0 / np.sqrt(C)
        W_r = jax.random.uniform(ks[1], (C, C), jnp.float32, -s, s)
        W_k = jax.random.uniform(ks[2], (C, C), jnp.float32, -s, s)
        W_v = jax.random.uniform(ks[3], (C, C), jnp.float32, -s, s)
        mu_r = jax.random.uniform(ks[4], (C,), jnp.float32)
        mu_k = jax.random.uniform(ks[5], (C,), jnp.float32)
        return {'x': x, 'W_r': W_r, 'W_k': W_k, 'W_v': W_v, 'mu_r': mu_r, 'mu_k': mu_k}
    _L0_ffn_in = _L0_ffn_setup()

    def _L1_attn_setup():
        import jax, jax.numpy as jnp
        import numpy as np
        key = jax.random.key(seed)
        B, L, D, N = (2, 256, 128, 16)
        ks = jax.random.split(key, 8)
        s = 1.0 / np.sqrt(D)
        A_log = jnp.log(jnp.broadcast_to(jnp.arange(1, N + 1, dtype=jnp.float32), (D, N)))
        return {'x': jax.random.normal(ks[0], (B, L, D), jnp.float32), 'Wz': jax.random.normal(ks[1], (D, D), jnp.float32) * s, 'bz': jnp.zeros((D,), jnp.float32), 'Wx': jax.random.normal(ks[2], (D, D), jnp.float32) * s, 'bx': jnp.zeros((D,), jnp.float32), 'WB': jax.random.normal(ks[3], (D, N), jnp.float32) * s, 'bB': jnp.zeros((N,), jnp.float32), 'WC': jax.random.normal(ks[4], (D, N), jnp.float32) * s, 'bC': jnp.zeros((N,), jnp.float32), 'Wdt': jax.random.normal(ks[5], (D, D), jnp.float32) * s, 'bdt': jnp.zeros((D,), jnp.float32), 'A_log': A_log, 'Wout': jax.random.normal(ks[6], (D, D), jnp.float32) * s, 'bout': jnp.zeros((D,), jnp.float32)}
    _L1_attn_in = _L1_attn_setup()

    def _L1_ffn_setup():
        import jax, jax.numpy as jnp
        import numpy as np
        GROUP = 16
        EPS = 1e-05

        def _dequant(q, scale):
            w = q.astype(jnp.float32) / 7.5 - 1.0
            return w * jnp.repeat(scale, GROUP, axis=1)

        def _qlora_linear(x, q, scale, bias, la, lb):
            w = _dequant(q, scale)
            base = jnp.einsum('btd,od->bto', x, w) + bias
            lora = jnp.einsum('btr,or->bto', jnp.einsum('btd,rd->btr', x, la), lb)
            return base + lora

        def _layernorm(x, g, b):
            mu = jnp.mean(x, axis=-1, keepdims=True)
            var = jnp.mean(jnp.square(x - mu), axis=-1, keepdims=True)
            return (x - mu) * jax.lax.rsqrt(var + EPS) * g + b
        key = jax.random.key(seed)
        ks = jax.random.split(key, 6)
        D, R, B, T = (128, 32, 8, 512)
        x = jax.random.normal(ks[0], (B, T, D), dtype=jnp.float32)
        qweights = jax.random.randint(ks[1], (6, D, D), 0, 16, dtype=jnp.int32)
        scales = jax.random.uniform(ks[2], (6, D, D // GROUP), dtype=jnp.float32)
        biases = jax.random.normal(ks[3], (6, D), dtype=jnp.float32) * 0.02
        lora_a = jax.random.normal(ks[4], (6, R, D), dtype=jnp.float32) * 0.02
        lora_b = jax.random.normal(ks[5], (6, D, R), dtype=jnp.float32) * 0.02
        ln_gamma = jnp.ones((3, D), dtype=jnp.float32)
        ln_beta = jnp.zeros((3, D), dtype=jnp.float32)
        return {'x': x, 'qweights': qweights, 'scales': scales, 'biases': biases, 'lora_a': lora_a, 'lora_b': lora_b, 'ln_gamma': ln_gamma, 'ln_beta': ln_beta}
    _L1_ffn_in = _L1_ffn_setup()
    _d = {'L0_attn_x': _L0_attn_in['x'], 'L0_attn_W': _L0_attn_in['W'], 'L0_ffn_W_r': _L0_ffn_in['W_r'], 'L0_ffn_W_k': _L0_ffn_in['W_k'], 'L0_ffn_W_v': _L0_ffn_in['W_v'], 'L0_ffn_mu_r': _L0_ffn_in['mu_r'], 'L0_ffn_mu_k': _L0_ffn_in['mu_k'], 'L1_attn_Wz': _L1_attn_in['Wz'], 'L1_attn_bz': _L1_attn_in['bz'], 'L1_attn_Wx': _L1_attn_in['Wx'], 'L1_attn_bx': _L1_attn_in['bx'], 'L1_attn_WB': _L1_attn_in['WB'], 'L1_attn_bB': _L1_attn_in['bB'], 'L1_attn_WC': _L1_attn_in['WC'], 'L1_attn_bC': _L1_attn_in['bC'], 'L1_attn_Wdt': _L1_attn_in['Wdt'], 'L1_attn_bdt': _L1_attn_in['bdt'], 'L1_attn_A_log': _L1_attn_in['A_log'], 'L1_attn_Wout': _L1_attn_in['Wout'], 'L1_attn_bout': _L1_attn_in['bout'], 'L1_ffn_qweights': _L1_ffn_in['qweights'], 'L1_ffn_scales': _L1_ffn_in['scales'], 'L1_ffn_biases': _L1_ffn_in['biases'], 'L1_ffn_lora_a': _L1_ffn_in['lora_a'], 'L1_ffn_lora_b': _L1_ffn_in['lora_b'], 'L1_ffn_ln_gamma': _L1_ffn_in['ln_gamma'], 'L1_ffn_ln_beta': _L1_ffn_in['ln_beta']}
    _x0 = _d['L0_attn_x']
    _d['L0_attn_x'] = jax.random.normal(jax.random.fold_in(jax.random.key(seed), 1), (8, 1024, 128), dtype=_x0.dtype)
    del _x0
    return _d

def reference(L0_attn_x, L0_attn_W, L0_ffn_W_r, L0_ffn_W_k, L0_ffn_W_v, L0_ffn_mu_r, L0_ffn_mu_k, L1_attn_Wz, L1_attn_bz, L1_attn_Wx, L1_attn_bx, L1_attn_WB, L1_attn_bB, L1_attn_WC, L1_attn_bC, L1_attn_Wdt, L1_attn_bdt, L1_attn_A_log, L1_attn_Wout, L1_attn_bout, L1_ffn_qweights, L1_ffn_scales, L1_ffn_biases, L1_ffn_lora_a, L1_ffn_lora_b, L1_ffn_ln_gamma, L1_ffn_ln_beta):

    def _L0_attn_ref(x, W):
        import jax, jax.numpy as jnp
        import numpy as np
        B, S, D = (4, 256, 128)
        d = x.shape[-1]
        kv = x @ W.T
        K, V = (kv[..., :d], kv[..., d:])
        n = x.shape[-2]
        causal = jnp.tril(jnp.ones((n, n), dtype=bool))
        mask = jnp.where(causal, jnp.float32(0.0), -jnp.inf).astype(x.dtype)
        scores = jnp.einsum('bqd,bkd->bqk', x, K) + mask
        attn = jax.nn.softmax(scores, axis=-1)
        return x + jnp.einsum('bqk,bkd->bqd', attn, V)

    def _L0_ffn_ref(x, W_r, W_k, W_v, mu_r, mu_k):
        import jax, jax.numpy as jnp
        import numpy as np
        DIM = 128

        def _reference_tuple_inner(x, W_r, W_k, W_v, mu_r, mu_k):
            B, T, C = x.shape
            x_prev = jnp.concatenate([jnp.zeros((B, 1, C), x.dtype), x[:, :-1, :]], axis=1)
            xr = mu_r * x + (1.0 - mu_r) * x_prev
            xk = mu_k * x + (1.0 - mu_k) * x_prev
            r = jax.nn.sigmoid(jnp.einsum('btc,dc->btd', xr, W_r))
            k = jnp.einsum('btc,dc->btd', xk, W_k)
            k_act = jnp.square(jax.nn.relu(k))
            out = r * jnp.einsum('btc,dc->btd', k_act, W_v)
            new_state = x[:, -1, :]
            return (out, new_state)
        return _reference_tuple_inner(x, W_r, W_k, W_v, mu_r, mu_k)[0]

    def _L1_attn_ref(x, Wz, bz, Wx, bx, WB, bB, WC, bC, Wdt, bdt, A_log, Wout, bout):
        import jax, jax.numpy as jnp
        import numpy as np
        B, L, D = x.shape
        N = A_log.shape[1]
        z = jax.nn.sigmoid(x @ Wz + bz)
        x_ssm = x @ Wx + bx
        Bm = x @ WB + bB
        C = x @ WC + bC
        dt = jax.nn.softplus(x @ Wdt + bdt)
        A = -jnp.exp(A_log)
        A_bar = jnp.exp(dt[..., None] * A)
        x_db = x_ssm[..., None] * (dt[..., None] * Bm[..., None, :])
        a_scan = jnp.transpose(A_bar, (1, 0, 2, 3))
        x_scan = jnp.transpose(x_db, (1, 0, 2, 3))
        c_scan = jnp.transpose(C, (1, 0, 2))

        def ssm_step(h, inp):
            a_t, x_t, c_t = inp
            h_new = a_t * h + x_t
            y_t = jnp.einsum('bdn,bn->bd', h_new, c_t)
            return (h_new, y_t)
        h0 = jnp.zeros((B, D, N), x.dtype)
        _, y_ssm = jax.lax.scan(ssm_step, h0, (a_scan, x_scan, c_scan))
        y_ssm = jnp.transpose(y_ssm, (1, 0, 2))
        y = y_ssm * z
        return y @ Wout + bout

    def _L1_ffn_ref(x, qweights, scales, biases, lora_a, lora_b, ln_gamma, ln_beta):
        import jax, jax.numpy as jnp
        import numpy as np
        GROUP = 16
        EPS = 1e-05

        def _dequant(q, scale):
            w = q.astype(jnp.float32) / 7.5 - 1.0
            return w * jnp.repeat(scale, GROUP, axis=1)

        def _qlora_linear(x, q, scale, bias, la, lb):
            w = _dequant(q, scale)
            base = jnp.einsum('btd,od->bto', x, w) + bias
            lora = jnp.einsum('btr,or->bto', jnp.einsum('btd,rd->btr', x, la), lb)
            return base + lora

        def _layernorm(x, g, b):
            mu = jnp.mean(x, axis=-1, keepdims=True)
            var = jnp.mean(jnp.square(x - mu), axis=-1, keepdims=True)
            return (x - mu) * jax.lax.rsqrt(var + EPS) * g + b
        h = x
        for blk in range(3):
            i0, i1 = (2 * blk, 2 * blk + 1)
            y = _qlora_linear(h, qweights[i0], scales[i0], biases[i0], lora_a[i0], lora_b[i0])
            y = _layernorm(y, ln_gamma[blk], ln_beta[blk])
            y = jax.nn.gelu(y, approximate=False)
            y = _qlora_linear(y, qweights[i1], scales[i1], biases[i1], lora_a[i1], lora_b[i1])
            h = y + h
        return h
    x = L0_attn_x
    x = _layernorm(x + _L0_attn_ref(x, L0_attn_W), axis=-1)
    x = _layernorm(x + _L0_ffn_ref(x, L0_ffn_W_r, L0_ffn_W_k, L0_ffn_W_v, L0_ffn_mu_r, L0_ffn_mu_k), axis=-1)
    x = _layernorm(x + _L1_attn_ref(x, L1_attn_Wz, L1_attn_bz, L1_attn_Wx, L1_attn_bx, L1_attn_WB, L1_attn_bB, L1_attn_WC, L1_attn_bC, L1_attn_Wdt, L1_attn_bdt, L1_attn_A_log, L1_attn_Wout, L1_attn_bout), axis=-1)
    x = _layernorm(x + _L1_ffn_ref(x, L1_ffn_qweights, L1_ffn_scales, L1_ffn_biases, L1_ffn_lora_a, L1_ffn_lora_b, L1_ffn_ln_gamma, L1_ffn_ln_beta), axis=-1)
    return x

_drawn_inputs = setup_inputs


def setup_inputs(seed=0):
    import zlib

    import numpy as np

    out = dict(_drawn_inputs(seed))
    spreads = {'L1_attn_bz': (0.0, 0.1),
     'L1_attn_bx': (0.0, 0.1),
     'L1_attn_bB': (0.0, 0.1),
     'L1_attn_bC': (0.0, 0.1),
     'L1_attn_bdt': (0.0, 0.1),
     'L1_attn_bout': (0.0, 0.1),
     'L1_ffn_ln_gamma': (1.0, 0.2),
     'L1_ffn_ln_beta': (0.0, 0.1)}
    factors = {'L0_ffn_mu_r': 3.182,
     'L1_ffn_biases': 5.156,
     'L1_ffn_lora_a': 5.109,
     'L1_ffn_lora_b': 5.223}
    for name, (base, spread) in spreads.items():
        noise = np.random.default_rng([zlib.crc32(name.encode()), seed]).standard_normal(out[name].shape)
        drawn = base * np.exp(spread * noise) if base else spread * noise
        out[name] = jnp.asarray(drawn.astype(out[name].dtype))
    for name, factor in factors.items():
        out[name] = (out[name] * factor).astype(out[name].dtype)
    return out
```

```python
from contextlib import ExitStack

import concourse.bass as bass
from concourse import mybir

F32 = mybir.dt.float32
BF16 = mybir.dt.bfloat16
I32 = mybir.dt.int32
ALU = mybir.AluOpType
ACT = mybir.ActivationFunctionType
AX = mybir.AxisListType

P = 128
BATCH = 8
T = 1024
CH = T // P
HALF = 512
HC = HALF // P
N = 16
EPS = 1e-5
MASKED = -1e30


def wait(eng, sem, value):
    if not (isinstance(value, int) and value <= 0):
        eng.wait_ge(sem, value)


def settle(eng, settled):
    eng.sem_inc(settled, 1)


def chunk(c):
    return slice(c * P, (c + 1) * P)


def half(h):
    return slice(h * HALF, (h + 1) * HALF)


def groups(q):
    first = q if q < HC else HC + 2 * (q - HC)
    return [(first + g, g * HC, min(HC, q + 1 - g * HC)) for g in range(1 + (q >= HC))]


GROUPS = groups(CH - 1)[-1][0] + 1


def attention_phase(nc, d, keep):
    with ExitStack() as ctx:
        def sb(name, shape, dt=F32):
            return ctx.enter_context(nc.sbuf_tensor(name + "_sb", shape, dt))

        def ps(name, cols):
            return ctx.enter_context(nc.psum_tensor(name, [P, cols], F32))

        def sem(name):
            return ctx.enter_context(nc.semaphore(name))

        ident, x_all = keep["ident"], keep["x_all"]
        w_key, w_val = sb("w_key", [P, P]), sb("w_val", [P, P])
        w_r, w_k, w_v = sb("w_r", [P, P]), sb("w_k", [P, P]), sb("w_v", [P, P])
        mu = sb("mu", [P, 2])
        mask32, mask, ident16 = sb("mask32", [P, P]), sb("mask", [P, P], BF16), sb("ident16", [P, P], BF16)
        minus_half = sb("a_minus_half", [P, CH])
        xin, xx = sb("xin", [P, CH, P]), sb("xx", [P, CH, P])
        xT, kT, val = sb("xT", [P, T]), sb("kT", [P, T]), sb("val", [P, CH, P])
        probs, probsT = sb("probs", [P, 2, T]), sb("probsT", [P, 2, T])
        negmax, rowsum, rinv = sb("negmax", [P, 2]), sb("rowsum", [P, CH]), sb("rinv", [P, 2])
        att, stats, mv = sb("att", [P, CH, P]), sb("stats", [P, CH, 6]), sb("mv", [P, CH, 2])
        var_eps, rstd = sb("var_eps", [P, CH]), sb("rstd", [P, CH])
        x1 = sb("x1", [P, CH, P])
        x1T, diff = sb("x1T", [P, 1 + T]), sb("diff", [P, T])
        xk, xr = sb("xk", [P, T]), sb("xr", [P, T])
        relu, kact = sb("relu", [P, T]), sb("kact", [P, T])
        gate, mixed = sb("gate", [P, T]), sb("mixed", [P, CH, P])
        stats2, mv2 = sb("stats2", [P, CH, 6]), sb("mv2", [P, CH, 2])
        var_eps2, rstd2 = sb("var_eps2", [P, CH]), sb("rstd2", [P, CH])
        score = [ps("score0", T), ps("score1", T)]
        turn = [ps("turn0", HALF), ps("turn1", HALF)]
        pv, mix = ps("pv", HALF), ps("mix", HALF)

        weights_in = sem("weights_in")
        pool_settled, dve_settled = sem("a_pool_settled"), sem("a_dve_settled")
        minus_made = sem("minus_made")
        zero_made = sem("zero_made")
        consts = sem("consts")
        x_in = sem("x_in")
        xx_made = sem("xx_made")
        xT_ready = sem("xT_ready")
        xT_copied = sem("xT_copied")
        k_ready = sem("k_ready")
        k_copied = sem("k_copied")
        v_ready = sem("v_ready")
        v_copied = sem("v_copied")
        scored = sem("scored")
        max_found = sem("max_found")
        exp_done = sem("exp_done")
        turned = sem("turned")
        even_copied = sem("even_copied")
        odd_copied = sem("odd_copied")
        pv_done = sem("pv_done")
        inverted = sem("inverted")
        combined = sem("combined")
        summed = sem("summed")
        mv_ready = sem("mv_ready")
        veps_ready = sem("veps_ready")
        rstd_ready = sem("rstd_ready")
        x1_ready = sem("x1_ready")
        x1T_ready = sem("x1T_ready")
        x1T_copied = sem("x1T_copied")
        diff_ready = sem("diff_ready")
        xk_ready = sem("xk_ready")
        km_ready = sem("km_ready")
        relu_done = sem("relu_done")
        kact_ready = sem("kact_ready")
        r_ready = sem("r_ready")
        gate_ready = sem("gate_ready")
        vm_ready = sem("vm_ready")
        gated = sem("gated")
        mixed_ready = sem("mixed_ready")
        summed2 = sem("summed2")
        mv2_ready = sem("mv2_ready")
        veps2_ready = sem("veps2_ready")
        rstd2_ready = sem("rstd2_ready")
        x2_ready = sem("x2_ready")
        block = ctx.enter_context(nc.Block())

        x_dram = d["L0_attn_x"].rearrange("b (c p) d -> p b c d", p=P)
        weights = [(ident[:], d["ident"]), (w_key[:], d["w_key"]), (w_val[:], d["w_val"]), (mask32[:], d["mask"]),
                   (w_r[:], d["w_r"]), (w_k[:], d["w_k"]), (w_v[:], d["w_v"]), (mu[:], d["mu"])]

        @block.sync
        def _(sp):
            sp.dma_start(xin[:], x_dram[:, 0]).then_inc(x_in, 16)
            for dst, src in weights:
                sp.dma_start(dst, src).then_inc(weights_in, 16)
            with sp.Fori(1, BATCH) as i:
                wait(sp, xT_ready, 2 * i)
                wait(sp, xx_made, i)
                sp.dma_start(xin[:], x_dram[:, bass.ds(i, 1)].rearrange("p b c d -> p (b c) d")).then_inc(x_in, 16)

        @block.gpsimd
        def _(pool):
            pool.memset(minus_half[:], -0.5).then_inc(minus_made, 1)
            pool.memset(x1T[:, 0:1], 0.0).then_inc(zero_made, 1)
            pool.wait_ge(minus_made, 1)
            pool.wait_ge(zero_made, 1)

            def double(i):
                pool.wait_ge(x_in, 16 * i + 16)
                wait(pool, combined, CH * i)
                settle(pool, pool_settled)
                pool.tensor_scalar(xx[:], xin[:], 2.0, 0.0, ALU.mult, ALU.add).then_inc(xx_made, 1)

            def mix_inputs(b):
                pool.wait_ge(x1T_copied, 2 * b + 2)
                wait(pool, xk_ready, 2 * b)
                pool.tensor_tensor(diff[:], x1T[:, 1:1 + T], x1T[:, 0:T], ALU.subtract).then_inc(diff_ready, 1)
                for h in range(2):
                    pool.wait_ge(relu_done, 2 * b + h + 1)
                    wait(pool, vm_ready, 2 * b)
                    pool.tensor_tensor(kact[:, half(h)], relu[:, half(h)], relu[:, half(h)],
                                       ALU.mult).then_inc(kact_ready, 1)

            def inverse_std(b, mean_var, ready, ve, made, out, done, used):
                pool.wait_ge(ready, CH * b + CH)
                settle(pool, pool_settled)
                pool.tensor_scalar(ve[:], mean_var[:, :, 1], 1.0, EPS, ALU.mult, ALU.add).then_inc(made, 1)
                pool.wait_ge(made, b + 1)
                wait(pool, used, CH * b)
                pool.tensor_tensor(out[:], ve[:], minus_half[:], ALU.pow).then_inc(done, 1)

            def iteration(i, attend, channel):
                if attend:
                    double(i)
                if channel:
                    mix_inputs(i - 1)
                    inverse_std(i - 1, mv2, mv2_ready, var_eps2, veps2_ready, rstd2, rstd2_ready, x2_ready)
                if attend:
                    inverse_std(i, mv, mv_ready, var_eps, veps_ready, rstd, rstd_ready, x1_ready)

            iteration(0, True, False)
            iteration(1, True, True)
            with pool.Fori(2, BATCH) as i:
                iteration(i, True, True)
            iteration(BATCH, False, True)

        @block.tensor
        def _(pe):
            def transpose_x(i):
                pe.wait_ge(x_in, 16 * i + 16)
                for h in range(2):
                    wait(pe, odd_copied if h else even_copied, GROUPS // 2 * i)
                    for c in range(HC):
                        mm = pe.transpose(turn[h][:, chunk(c)], xin[:, HC * h + c, :], ident[:])
                    mm.then_inc(xT_ready, 1)

            def keys_values(i):
                for h in range(2):
                    pe.wait_ge(xT_copied, 2 * i + h + 1)
                    if h == 0:
                        wait(pe, exp_done, CH * i - 1)
                    pe.matmul(score[0][:, half(h)], w_key[:], xT[:, half(h)], start=True, stop=True).then_inc(k_ready, 1)
                wait(pe, exp_done, CH * i)
                for h in range(2):
                    for c in range(HC):
                        mm = pe.matmul(score[1][:, chunk(HC * h + c)], xT[:, chunk(HC * h + c)], w_val[:],
                                       start=True, stop=True)
                    mm.then_inc(v_ready, 1)

            def scores(i, q):
                if q < 2:
                    pe.wait_ge(v_copied if q else k_copied, 2 * i + 2)
                else:
                    pe.wait_ge(exp_done, CH * i + q - 1)
                s = score[q % 2]
                for lo in range(0, q * P, HALF):
                    hi = min(lo + HALF, q * P)
                    pe.matmul(s[:, lo:hi], xT[:, chunk(q)], kT[:, lo:hi], start=True, stop=True)
                pe.matmul(s[:, chunk(q)], xT[:, chunk(q)], kT[:, chunk(q)], start=True, stop=False)
                pe.matmul(s[:, chunk(q)], ident16[:], mask[:], start=False, stop=True).then_inc(scored, 1)

            def transpose_probs(i, q):
                pe.wait_ge(exp_done, CH * i + q + 1)
                for g, first, blocks in groups(q):
                    if g < 2:
                        pe.wait_ge(xT_copied, 2 * i + 2)
                    else:
                        pe.wait_ge(odd_copied if g % 2 else even_copied, GROUPS // 2 * i + g // 2)
                    for k in range(blocks):
                        mm = pe.transpose(turn[g % 2][:, chunk(k)], probs[:, q % 2, chunk(first + k)], ident[:])
                    mm.then_inc(turned, 1)

            def weigh_values(i, q):
                for g, _, _ in groups(q):
                    pe.wait_ge(odd_copied if g % 2 else even_copied, GROUPS // 2 * i + g // 2 + 1)
                wait(pe, combined, CH * i + q)
                for k in range(q + 1):
                    mm = pe.matmul(pv[:, 0:P], probsT[:, q % 2, chunk(k)], val[:, k, :], start=k == 0, stop=k == q)
                mm.then_inc(pv_done, 1)

            def channel_piece(b, n):
                h = n % 2
                if n < 2:
                    if h:
                        pe.wait_ge(x1T_copied, 2 * b + 1)
                    else:
                        pe.wait_ge(x1_ready, CH * b + CH)
                        wait(pe, gated, 2 * b)
                    for c in range(HC):
                        mm = pe.transpose(mix[:, chunk(c)], x1[:, HC * h + c, :], ident[:])
                    mm.then_inc(x1T_ready, 1)
                elif n < 4:
                    pe.wait_ge(xk_ready, 2 * b + 1)
                    if h:
                        pe.wait_ge(relu_done, 2 * b + 1)
                    else:
                        pe.wait_ge(x1T_copied, 2 * b + 2)
                    pe.matmul(mix[:], w_k[:], xk[:, half(h)], start=True, stop=True).then_inc(km_ready, 1)
                elif n < 6:
                    pe.wait_ge(xk_ready, 2 * b + 2)
                    if h:
                        pe.wait_ge(gate_ready, 2 * b + 1)
                    else:
                        pe.wait_ge(relu_done, 2 * b + 2)
                    for c in range(HC):
                        mm = pe.matmul(mix[:, chunk(c)], xr[:, chunk(HC * h + c)], w_r[:], start=True, stop=True)
                    mm.then_inc(r_ready, 1)
                else:
                    pe.wait_ge(kact_ready, 2 * b + h + 1)
                    if h:
                        pe.wait_ge(gated, 2 * b + 1)
                    else:
                        pe.wait_ge(gate_ready, 2 * b + 2)
                    for c in range(HC):
                        mm = pe.matmul(mix[:, chunk(c)], kact[:, chunk(HC * h + c)], w_v[:], start=True, stop=True)
                    mm.then_inc(vm_ready, 1)

            def iteration(i, attend, channel):
                if attend:
                    transpose_x(i)
                    keys_values(i)
                for s in range(CH + 2):
                    if attend and s < CH:
                        scores(i, s)
                    if attend and s >= 2:
                        weigh_values(i, s - 2)
                    if attend and 1 <= s <= CH:
                        transpose_probs(i, s - 1)
                    if channel and s < 8:
                        channel_piece(i - 1, s)

            pe.wait_ge(weights_in, 16 * len(weights))
            pe.wait_ge(consts, 2)
            iteration(0, True, False)
            iteration(1, True, True)
            with pe.Fori(2, BATCH) as i:
                iteration(i, True, True)
            iteration(BATCH, False, True)

        @block.scalar
        def _(act):
            def iteration(i, attend, channel):
                b = i - 1
                if attend:
                    for h in range(2):
                        act.wait_ge(xT_ready, 2 * i + h + 1)
                        act.activation(xT[:, half(h)], turn[h][:], ACT.Copy).then_inc(xT_copied, 1)
                    for h in range(2):
                        act.wait_ge(k_ready, 2 * i + h + 1)
                        act.activation(kT[:, half(h)], score[0][:, half(h)], ACT.Copy).then_inc(k_copied, 1)
                for s in range(CH + 1):
                    if attend and s < CH:
                        act.wait_ge(max_found, CH * i + s + 1)
                        if s >= 2:
                            act.wait_ge(turned, GROUPS * i + groups(s - 2)[-1][0] + 1)
                        else:
                            wait(act, turned, GROUPS * (i - 1) + groups(CH - 2 + s)[-1][0] + 1)
                        wait(act, combined, CH * (i - 1) + s + 1)
                        act.activation(probs[:, s % 2, 0:(s + 1) * P], score[s % 2][:, 0:(s + 1) * P], ACT.Exp,
                                       bias=negmax[:, s % 2:s % 2 + 1],
                                       accum_out=rowsum[:, s:s + 1]).then_inc(exp_done, 1)
                    if attend and s >= 1:
                        for g, first, blocks in groups(s - 1):
                            if g % 2 == 0:
                                act.wait_ge(turned, GROUPS * i + g + 1)
                                wait(act, pv_done, CH * i + s - 2)
                                act.activation(probsT[:, (s - 1) % 2, first * P:(first + blocks) * P],
                                               turn[0][:, 0:blocks * P], ACT.Copy).then_inc(even_copied, 1)
                    if channel and s < 6:
                        h = s % 2
                        if s < 2:
                            act.wait_ge(x1T_ready, 2 * b + h + 1)
                            wait(act, xk_ready, 2 * b)
                            act.activation(x1T[:, 1 + h * HALF:1 + (h + 1) * HALF], mix[:],
                                           ACT.Copy).then_inc(x1T_copied, 1)
                        elif s < 4:
                            act.wait_ge(km_ready, 2 * b + h + 1)
                            wait(act, kact_ready, 2 * b)
                            act.activation(relu[:, half(h)], mix[:], ACT.Relu).then_inc(relu_done, 1)
                        else:
                            act.wait_ge(r_ready, 2 * b + h + 1)
                            wait(act, gated, 2 * b)
                            act.activation(gate[:, half(h)], mix[:], ACT.Tanh, scale=0.5).then_inc(gate_ready, 1)

            iteration(0, True, False)
            iteration(1, True, True)
            with act.Fori(2, BATCH) as i:
                iteration(i, True, True)
            iteration(BATCH, False, True)

        @block.vector
        def _(dve):
            def find_max(i, q):
                dve.wait_ge(scored, CH * i + q + 1)
                dve.tensor_reduce(negmax[:, q % 2:q % 2 + 1], score[q % 2][:, 0:(q + 1) * P], AX.X, ALU.max,
                                  negate=True).then_inc(max_found, 1)

            def combine(i, q):
                dve.wait_ge(pv_done, CH * i + q + 1)
                dve.wait_ge(inverted, CH * i + q + 1)
                dve.wait_ge(xx_made, i + 1)
                dve.scalar_tensor_tensor(out=att[:, q, :], in0=pv[:, 0:P], scalar=rinv[:, q % 2:q % 2 + 1],
                                         in1=xx[:, q, :], op0=ALU.mult, op1=ALU.add).then_inc(combined, 1)

            def invert(i, q):
                dve.wait_ge(exp_done, CH * i + q + 1)
                dve.reciprocal(rinv[:, q % 2:q % 2 + 1], rowsum[:, q:q + 1]).then_inc(inverted, 1)

            def copy_odd(i, q):
                for g, first, blocks in groups(q):
                    if g % 2:
                        dve.wait_ge(turned, GROUPS * i + g + 1)
                        wait(dve, pv_done, CH * i + q - 1)
                        dve.tensor_copy(probsT[:, q % 2, first * P:(first + blocks) * P],
                                        turn[1][:, 0:blocks * P]).then_inc(odd_copied, 1)

            def sum_up(i, q):
                dve.wait_ge(combined, CH * i + q + 1)
                dve.bn_stats(stats[:, q, :], att[:, q, :]).then_inc(summed, 1)

            def mix_inputs(b):
                dve.wait_ge(diff_ready, b + 1)
                wait(dve, km_ready, 2 * b)
                wait(dve, r_ready, 2 * b)
                for out, m in ((xk, 1), (xr, 0)):
                    dve.scalar_tensor_tensor(out=out[:], in0=diff[:], scalar=mu[:, m:m + 1], in1=x1T[:, 0:T],
                                             op0=ALU.mult, op1=ALU.add).then_inc(xk_ready, 1)

            def apply_gate(b, h):
                dve.wait_ge(gate_ready, 2 * b + h + 1)
                dve.wait_ge(vm_ready, 2 * b + h + 1)
                dve.scalar_tensor_tensor(out=gate[:, half(h)], in0=gate[:, half(h)], scalar=1.0, in1=mix[:],
                                         op0=ALU.add, op1=ALU.mult).then_inc(gated, 1)

            def add_x1(b, h):
                dve.wait_ge(gated, 2 * b + h + 1)
                cs = slice(HC * h, HC * h + HC)
                dve.scalar_tensor_tensor(out=mixed[:, cs, :].rearrange("p c d -> p (c d)"), in0=gate[:, half(h)],
                                         scalar=0.5, in1=x1[:, cs, :].rearrange("p c d -> p (c d)"),
                                         op0=ALU.mult, op1=ALU.add).then_inc(mixed_ready, 1)

            def sum_up2(b, h):
                dve.wait_ge(mixed_ready, 2 * b + h + 1)
                for c in range(HC * h, HC * h + HC):
                    dve.bn_stats(stats2[:, c, :], mixed[:, c, :]).then_inc(summed2, 1)

            def aggregate(b, sums, done, out, ready):
                dve.wait_ge(done, CH * b + CH)
                settle(dve, dve_settled)
                for c in range(CH):
                    dve.bn_aggr(out[:, c, :], sums[:, c, :]).then_inc(ready, 1)

            def normalise(out, src, mean_var, r, ready):
                for c in range(CH):
                    dve.tensor_scalar(out[:, c, :], src[:, c, :], mean_var[:, c, 0:1], r[:, c:c + 1],
                                      ALU.subtract, ALU.mult).then_inc(ready, 1)

            def iteration(i, attend, channel):
                b = i - 1
                if attend:
                    for h in range(2):
                        dve.wait_ge(v_ready, 2 * i + h + 1)
                        dve.tensor_copy(val[:, HC * h:HC * h + HC, :].rearrange("p c d -> p (c d)"),
                                        score[1][:, half(h)]).then_inc(v_copied, 1)
                for s in range(CH + 2):
                    if attend:
                        if s < CH:
                            find_max(i, s)
                        if 1 <= s <= CH:
                            invert(i, s - 1)
                        if s >= 2:
                            combine(i, s - 2)
                        if 1 <= s <= CH:
                            copy_odd(i, s - 1)
                        if s >= 2:
                            sum_up(i, s - 2)
                    if channel:
                        if s == 2:
                            mix_inputs(b)
                        if s in (6, 7):
                            apply_gate(b, s - 6)
                            add_x1(b, s - 6)
                        if s in (7, 8):
                            sum_up2(b, s - 7)
                        if s == 8:
                            aggregate(b, stats2, summed2, mv2, mv2_ready)
                        if s == 9:
                            dve.wait_ge(rstd2_ready, b + 1)
                            normalise(x_all[:, bass.ds(b, 1)].rearrange("p b c d -> p (b c) d")
                                      if not isinstance(b, int) else x_all[:, b], mixed, mv2, rstd2, x2_ready)
                if attend:
                    aggregate(i, stats, summed, mv, mv_ready)
                    dve.wait_ge(rstd_ready, i + 1)
                    wait(dve, x1T_ready, 2 * i)
                    normalise(x1, att, mv, rstd, x1_ready)

            dve.wait_ge(weights_in, 16 * len(weights))
            dve.tensor_copy(mask[:], mask32[:]).then_inc(consts, 1)
            dve.tensor_copy(ident16[:], ident[:]).then_inc(consts, 1)
            iteration(0, True, False)
            iteration(1, True, True)
            with dve.Fori(2, BATCH) as i:
                iteration(i, True, True)
            iteration(BATCH, False, True)


def at(i, n):
    return i + n // N, n % N


def step_count(i, n):
    return N * i + n


def ssm_phase(nc, d, keep):
    with ExitStack() as ctx:
        def sb(name, shape, dt=F32):
            return ctx.enter_context(nc.sbuf_tensor(name + "_sb", shape, dt))

        def ps(name, cols):
            return ctx.enter_context(nc.psum_tensor(name, [P, cols], F32))

        def sem(name):
            return ctx.enter_context(nc.semaphore(name))

        ident, x_all = keep["ident"], keep["x_all"]
        K3 = 3 * 2 * N
        w_dt, w_x, w_z, w_out = sb("w_dt", [P, P]), sb("w_x", [P, P]), sb("w_z", [P, P]), sb("w_out", [P, P])
        w_bc, b_bc = sb("w_bc", [P, K3]), sb("b_bc", [K3, 1])
        b_dt, b_x, a_log = sb("b_dt", [P, 1]), sb("b_x", [P, 1]), sb("a_log", [P, N])
        a_pos, a_neg = sb("a_pos", [P, N]), sb("a_neg", [P, N])
        pick32, pick = sb("pick32", [K3, 2 * N]), sb("pick", [K3, 2 * N, P], BF16)
        rows32 = sb("rows32", [K3, 2, P])
        rows, ones = sb("rows", [K3, 2, P], BF16), sb("ones", [K3, P], BF16)
        minus_half = sb("s_minus_half", [P, CH])
        x2, x2T = sb("x2", [P, CH, P]), sb("x2T", [P, T])
        dt, u, bc = sb("dt", [P, 2, T]), sb("u", [P, 2, T]), sb("bc", [K3, 2, T], BF16)
        mag, soft, bc32, rest = sb("mag", [P, T]), sb("soft", [P, T]), sb("bc32", [K3, T]), sb("rest", [K3, T])
        z = sb("z", [P, 2, T])
        a, bn, xb = sb("a", [P, 2, T]), sb("bn", [P, 2, T]), sb("xb", [P, 2, T])
        h, hc = sb("h", [P, 4, T]), sb("hc", [P, 2, T])
        yz, yzT, res = sb("yz", [P, T]), sb("yzT", [P, T]), sb("res", [P, CH, P])
        stats, mv = sb("s_stats", [P, CH, 6]), sb("s_mv", [P, CH, 2])
        var_eps, rstd = sb("s_var_eps", [P, CH]), sb("s_rstd", [P, CH])
        b_bank = [ps("b_bank0", HALF), ps("b_bank1", HALF)]
        c_bank = [ps("c_bank0", HALF), ps("c_bank1", HALF)]
        side = [ps("side0", HALF), ps("side1", HALF)]
        y = ps("y", T)

        weights_in = sem("weights_in2")
        a_made = sem("a_made")
        rows_made = sem("rows_made")
        pool_settled, dve_settled, act_settled = sem("s_pool_settled"), sem("s_dve_settled"), sem("s_act_settled")
        rows_clear = sem("rows_clear")
        pool_const = sem("pool_const")
        consts = sem("consts2")
        x2_in = sem("x2_in")
        x2T_ready = sem("x2T_ready")
        x2T_copied = sem("x2T_copied")
        dt_raw = sem("dt_raw")
        mag_done = sem("mag_done")
        relu_dt = sem("relu_dt")
        soft_exp = sem("soft_exp")
        soft_ln = sem("soft_ln")
        dt_ready = sem("dt_ready")
        xs_ready = sem("xs_ready")
        u_ready = sem("u_ready")
        bc_raw = sem("bc_raw")
        bc_high = sem("bc_high")
        bc_step = sem("bc_step")
        z_raw = sem("z_raw")
        z_ready = sem("z_ready")
        b_ready = sem("b_ready")
        b_copied = sem("b_copied")
        a_ready = sem("a_ready")
        xb_ready = sem("xb_ready")
        scanned = sem("scanned")
        c_ready = sem("c_ready")
        hc_ready = sem("hc_ready")
        summed_y = sem("summed_y")
        yz_ready = sem("yz_ready")
        yzT_ready = sem("yzT_ready")
        yzT_copied = sem("yzT_copied")
        out_ready = sem("out_ready")
        res_ready = sem("res_ready")
        summed = sem("s_summed")
        mv_ready = sem("s_mv_ready")
        veps_ready = sem("s_veps_ready")
        rstd_ready = sem("s_rstd_ready")
        x3_ready = sem("x3_ready")
        block = ctx.enter_context(nc.Block())

        def rows_of(b):
            if isinstance(b, int):
                return x_all[:, b]
            return x_all[:, bass.ds(b, 1)].rearrange("p b c d -> p (b c) d")

        def slot(buf, b):
            if isinstance(b, int):
                return buf[:, b % 2]
            return buf[:, bass.ds(b % 2, 1)].rearrange("p b t -> p (b t)")

        weights = [(w_dt[:], d["w_dt"]), (w_x[:], d["w_x"]), (w_z[:], d["w_z"]), (w_out[:], d["w_out"]),
                   (w_bc[:], d["w_bc"]), (b_bc[:], d["b_bc"]), (b_dt[:], d["b_dt"]), (b_x[:], d["b_x"]),
                   (a_log[:], d["a_log"]), (pick32[:], d["pick"])] + [
                       (rows32[32 * k:32 * k + 1], d["rows"]) for k in range(3)]

        @block.sync
        def _(sp):
            sp.dma_start(x2[:], x_all[:, 0]).then_inc(x2_in, 16)
            sp.wait_ge(rows_clear, 1)
            for dst, src in weights:
                sp.dma_start(dst, src).then_inc(weights_in, 16)
            with sp.Fori(1, BATCH) as i:
                wait(sp, x2T_ready, 2 * i)
                sp.dma_start(x2[:], rows_of(i)).then_inc(x2_in, 16)

        @block.gpsimd
        def _(pool):
            def scale_b(i, n):
                g = step_count(*at(i, n))
                b = at(i, n)[0]
                if at(i, n)[1] == 0:
                    pool.wait_ge(u_ready, 2 * b + 2)
                pool.wait_ge(b_copied, 2 * g + 2)
                wait(pool, scanned, g - 1)
                settle(pool, pool_settled)
                pool.tensor_tensor(xb[:, n % 2, :], slot(u, b), bn[:, n % 2, :], ALU.mult).then_inc(xb_ready, 1)

            def inverse_std(b):
                pool.wait_ge(mv_ready, CH * b + CH)
                settle(pool, pool_settled)
                pool.tensor_scalar(var_eps[:], mv[:, :, 1], 1.0, EPS, ALU.mult, ALU.add).then_inc(veps_ready, 1)
                pool.wait_ge(veps_ready, b + 1)
                wait(pool, x3_ready, CH * b)
                pool.tensor_tensor(rstd[:], var_eps[:], minus_half[:], ALU.pow).then_inc(rstd_ready, 1)

            def iteration(i, scan, finish, more):
                for n in range(N):
                    if scan and (more or n + 2 < N):
                        scale_b(i, n + 2)
                    if finish and n == 13:
                        inverse_std(i - 1)

            pool.memset(rows32[:], 0.0).then_inc(rows_clear, 1)
            pool.memset(minus_half[:], -0.5).then_inc(pool_const, 1)
            pool.wait_ge(pool_const, 1)
            for n in range(2):
                scale_b(0, n)
            iteration(0, True, False, True)
            iteration(1, True, True, True)
            with pool.Fori(2, BATCH - 1) as i:
                iteration(i, True, True, True)
            iteration(BATCH - 1, True, True, False)
            iteration(BATCH, False, True, False)

        @block.tensor
        def _(pe):
            def spread_b(i, n):
                b, k = at(i, n)
                g = step_count(b, k)
                if k == 0:
                    pe.wait_ge(bc_step, 4 * b + 4)
                for f in range(2):
                    wait(pe, b_copied, 2 * g + f - 1)
                    pe.matmul(b_bank[f][:], pick[:, k, :], slot(bc, b)[:, half(f)], start=True,
                              stop=True).then_inc(b_ready, 1)

            def spread_c(i, n):
                g = step_count(i, n)
                for f in range(2):
                    wait(pe, hc_ready, 2 * g + f - 1)
                    pe.matmul(c_bank[f][:], pick[:, N + n, :], slot(bc, i)[:, half(f)], start=True,
                              stop=True).then_inc(c_ready, 1)

            def sum_states(i, n):
                b, k = at(i, n)
                g = step_count(b, k)
                pe.wait_ge(hc_ready, 2 * g + 2)
                if k == 0:
                    wait(pe, yz_ready, 2 * b)
                for c in range(CH):
                    mm = pe.matmul(y[:, chunk(c)], hc[:, k % 2, chunk(c)], ident[:], is_transpose=True,
                                   start=k == 0 and c % HC == 0, stop=k == N - 1, skip_group_check=True)
                mm.then_inc(summed_y, 1)

            def prepare(b, n):
                if n == 0:
                    pe.wait_ge(x2_in, 16 * b + 16)
                    wait(pe, res_ready, 2 * (b - 2))
                    wait(pe, z_ready, 2 * b)
                    for f in range(2):
                        for c in range(HC):
                            mm = pe.transpose(side[f][:, chunk(c)], x2[:, HC * f + c, :], ident[:])
                        mm.then_inc(x2T_ready, 1)
                elif n in (1, 2):
                    f = n - 1
                    pe.wait_ge(x2T_copied, 2 * b + f + 1)
                    pe.matmul(side[f][:], w_dt[:], x2T[:, half(f)], start=True, stop=True).then_inc(dt_raw, 1)
                elif n in (3, 4):
                    f = n - 3
                    pe.wait_ge(mag_done, 2 * b + f + 1)
                    pe.wait_ge(relu_dt, 2 * b + f + 1)
                    pe.matmul(side[f][:], w_x[:], x2T[:, half(f)], start=True, stop=True).then_inc(xs_ready, 1)
                elif n in (5, 6):
                    f = n - 5
                    pe.wait_ge(u_ready, 2 * b + f + 1)
                    pe.matmul(side[f][0:K3, :], w_bc[:], x2T[:, half(f)], start=True, stop=True).then_inc(bc_raw, 1)
                elif n in (8, 9):
                    f = n - 8
                    if f == 0:
                        pe.wait_ge(bc_high, 4 * b + 4)
                    wait(pe, yzT_copied, 2 * (b - 2) + f + 1)
                    for c in range(HC):
                        pe.matmul(side[f][:, chunk(c)], x2T[:, chunk(HC * f + c)], w_z[:], start=True, stop=False)
                        mm = pe.matmul(side[f][:, chunk(c)], ones[:], rows[:, 0, :], start=False, stop=True)
                    mm.then_inc(z_raw, 1)

            def finish(b, n, last):
                if n == 7:
                    pe.wait_ge(yz_ready, 2 * b + 2)
                    wait(pe, res_ready, 2 * b)
                    if not last:
                        pe.wait_ge(bc_high, 4 * (b + 2) + 4)
                    for f in range(2):
                        for c in range(HC):
                            mm = pe.transpose(side[f][:, chunk(c)], yz[:, chunk(HC * f + c)], ident[:])
                        mm.then_inc(yzT_ready, 1)
                elif n in (10, 11):
                    f = n - 10
                    pe.wait_ge(yzT_copied, 2 * b + f + 1)
                    if not last:
                        pe.wait_ge(z_ready, 2 * (b + 2) + f + 1)
                    for c in range(HC):
                        pe.matmul(side[f][:, chunk(c)], yzT[:, chunk(HC * f + c)], w_out[:], start=True, stop=False)
                        mm = pe.matmul(side[f][:, chunk(c)], ones[:], rows[:, 1, :], start=False, stop=True)
                    mm.then_inc(out_ready, 1)

            def iteration(i, scan, done, more):
                for n in range(N):
                    if scan:
                        spread_c(i, n)
                        if more or n + 3 < N:
                            spread_b(i, n + 3)
                    if more:
                        prepare(i + 1, n)
                    if done:
                        finish(i - 1, n, not more)
                    if (scan and n >= 1) or (done and n == 0):
                        sum_states(i, n - 1)

            pe.wait_ge(weights_in, 16 * len(weights))
            pe.wait_ge(consts, 3)
            pe.wait_ge(rows_made, 5)
            for n in range(N):
                prepare(0, n)
            for n in range(3):
                spread_b(0, n)
            iteration(0, True, False, True)
            iteration(1, True, True, True)
            with pe.Fori(2, BATCH - 1) as i:
                iteration(i, True, True, True)
            iteration(BATCH - 1, True, True, False)
            iteration(BATCH, False, True, False)

        @block.scalar
        def _(act):
            def copy_b(i, n):
                g = step_count(*at(i, n))
                for f in range(2):
                    act.wait_ge(b_ready, 2 * g + f + 1)
                    if f == 0:
                        wait(act, xb_ready, g - 1)
                    act.activation(bn[:, n % 2, half(f)], b_bank[f][:], ACT.Copy).then_inc(b_copied, 1)

            def decay(i, n):
                b, k = at(i, n)
                g = step_count(b, k)
                if k == 0:
                    act.wait_ge(dt_ready, b + 1)
                wait(act, scanned, g - 1)
                settle(act, act_settled)
                act.activation(a[:, n % 2, :], slot(dt, b), ACT.Exp, scale=a_neg[:, k:k + 1]).then_inc(a_ready, 1)

            def prepare(b, n):
                if n == 0:
                    for f in range(2):
                        act.wait_ge(x2T_ready, 2 * b + f + 1)
                        wait(act, z_raw, 2 * b)
                        act.activation(x2T[:, half(f)], side[f][:], ACT.Copy).then_inc(x2T_copied, 1)
                elif n in (1, 2):
                    f = n - 1
                    act.wait_ge(dt_raw, 2 * b + f + 1)
                    act.activation(mag[:, half(f)], side[f][:], ACT.Abs, bias=b_dt[:]).then_inc(mag_done, 1)
                    if f:
                        act.wait_ge(mag_done, 2 * b + 2)
                        act.activation(soft[:], mag[:], ACT.Exp, scale=-1.0).then_inc(soft_exp, 1)
                        act.wait_ge(soft_exp, b + 1)
                        act.activation(mag[:], soft[:], ACT.Ln, bias=1.0).then_inc(soft_ln, 1)
                elif n in (5, 6):
                    f = n - 5
                    act.wait_ge(bc_raw, 2 * b + f + 1)
                    wait(act, bc_step, 4 * b)
                    act.activation(bc32[:, half(f)], side[f][0:K3, :], ACT.Identity,
                                   bias=b_bc[:]).then_inc(bc_high, 1)
                    act.activation(slot(bc, b)[:, half(f)], side[f][0:K3, :], ACT.Identity,
                                   bias=b_bc[:]).then_inc(bc_high, 1)
                elif n == 9:
                    act.wait_ge(z_raw, 2 * b + 2)
                    wait(act, yz_ready, 2 * (b - 1))
                    settle(act, act_settled)
                    for f in range(2):
                        act.activation(slot(z, b)[:, half(f)], side[f][:], ACT.Sigmoid).then_inc(z_ready, 1)
                    act.preload_act_table_set("natural_log_exp_and_others")

            def finish(b, n):
                if n == 7:
                    for f in range(2):
                        act.wait_ge(yzT_ready, 2 * b + f + 1)
                        wait(act, out_ready, 2 * b)
                        act.activation(yzT[:, half(f)], side[f][:], ACT.Copy).then_inc(yzT_copied, 1)

            def iteration(i, scan, done, more):
                for n in range(N):
                    if scan and (more or n + 3 < N):
                        copy_b(i, n + 3)
                    if scan and (more or n + 2 < N):
                        decay(i, n + 2)
                    if more:
                        prepare(i + 1, n)
                    if done:
                        finish(i - 1, n)

            act.preload_act_table_set("natural_log_exp_and_others")
            act.wait_ge(weights_in, 16 * len(weights))
            act.activation(a_pos[:], a_log[:], ACT.Exp).then_inc(a_made, 1)
            for n in range(N):
                prepare(0, n)
            act.wait_ge(a_made, 2)
            for n in range(3):
                copy_b(0, n)
                if n < 2:
                    decay(0, n)
            iteration(0, True, False, True)
            iteration(1, True, True, True)
            with act.Fori(2, BATCH - 1) as i:
                iteration(i, True, True, True)
            iteration(BATCH - 1, True, True, False)
            iteration(BATCH, False, True, False)

        @block.vector
        def _(dve):
            def scan_state(i, n):
                b, k = at(i, n)
                g = step_count(b, k)
                dve.wait_ge(a_ready, g + 1)
                dve.wait_ge(xb_ready, g + 1)
                wait(dve, hc_ready, 2 * (g - 3))
                dve.tensor_tensor_scan(h[:, n % 4, :], a[:, n % 2, :], xb[:, n % 2, :], 0.0, ALU.mult,
                                       ALU.add).then_inc(scanned, 1)

            def times_c(i, n):
                g = step_count(i, n)
                dve.wait_ge(scanned, g + 1)
                wait(dve, summed_y, g - 1)
                for f in range(2):
                    dve.wait_ge(c_ready, 2 * g + f + 1)
                    dve.tensor_tensor(hc[:, n % 2, half(f)], h[:, n % 4, half(f)], c_bank[f][:],
                                      ALU.mult).then_inc(hc_ready, 1)

            def prepare(b, n):
                if n in (1, 2):
                    f = n - 1
                    dve.wait_ge(mag_done, 2 * b + f + 1)
                    wait(dve, xb_ready, N * (b - 1))
                    dve.tensor_scalar(slot(dt, b)[:, half(f)], side[f][:], b_dt[:], 0.0, ALU.add,
                                      ALU.max).then_inc(relu_dt, 1)
                elif n == 3:
                    dve.wait_ge(soft_ln, b + 1)
                    dve.wait_ge(relu_dt, 2 * b + 2)
                    dve.tensor_tensor(slot(dt, b), slot(dt, b), mag[:], ALU.add).then_inc(dt_ready, 1)
                    dve.wait_ge(dt_ready, b + 1)
                if n in (3, 4):
                    f = n - 3
                    dve.wait_ge(xs_ready, 2 * b + f + 1)
                    dve.scalar_tensor_tensor(out=slot(u, b)[:, half(f)], in0=side[f][:], scalar=b_x[:],
                                             in1=slot(dt, b)[:, half(f)], op0=ALU.add,
                                             op1=ALU.mult).then_inc(u_ready, 1)
                elif n == 7:
                    dve.wait_ge(bc_high, 4 * b + 4)
                    dve.tensor_tensor(rest[:], bc32[:], slot(bc, b), ALU.subtract).then_inc(bc_step, 1)
                elif n == 8:
                    dve.wait_ge(bc_step, 4 * b + 1)
                    dve.tensor_copy(slot(bc, b)[32:64], rest[32:64]).then_inc(bc_step, 1)
                    dve.tensor_copy(slot(bc, b)[64:96], rest[64:96]).then_inc(bc_step, 1)
                elif n == 9:
                    dve.wait_ge(bc_step, 4 * b + 3)
                    dve.tensor_tensor(slot(bc, b)[64:96], rest[64:96], slot(bc, b)[64:96],
                                      ALU.subtract).then_inc(bc_step, 1)

            def finish(b, n):
                if n == 0:
                    dve.wait_ge(summed_y, N * b + N)
                    dve.wait_ge(z_ready, 2 * b + 2)
                    for f in range(2):
                        dve.tensor_tensor(yz[:, half(f)], y[:, half(f)], slot(z, b)[:, half(f)],
                                          ALU.mult).then_inc(yz_ready, 1)
                elif n in (10, 11):
                    f = n - 10
                    dve.wait_ge(out_ready, 2 * b + f + 1)
                    dve.tensor_tensor(res[:, HC * f:HC * f + HC, :].rearrange("p c d -> p (c d)"), side[f][:],
                                      rows_of(b)[:, HC * f:HC * f + HC, :].rearrange("p c d -> p (c d)"),
                                      ALU.add).then_inc(res_ready, 1)
                elif n == 12:
                    dve.wait_ge(res_ready, 2 * b + 2)
                    for c in range(CH):
                        dve.bn_stats(stats[:, c, :], res[:, c, :]).then_inc(summed, 1)
                elif n == 13:
                    dve.wait_ge(summed, CH * b + CH)
                    settle(dve, dve_settled)
                    for c in range(CH):
                        dve.bn_aggr(mv[:, c, :], stats[:, c, :]).then_inc(mv_ready, 1)
                elif n == 15:
                    dve.wait_ge(rstd_ready, b + 1)
                    for c in range(CH):
                        dve.tensor_scalar(rows_of(b)[:, c, :], res[:, c, :], mv[:, c, 0:1], rstd[:, c:c + 1],
                                          ALU.subtract, ALU.mult).then_inc(x3_ready, 1)

            def iteration(i, scan, done, more):
                for n in range(N):
                    if scan and (more or n + 1 < N):
                        scan_state(i, n + 1)
                    if scan:
                        times_c(i, n)
                    if more:
                        prepare(i + 1, n)
                    if done:
                        finish(i - 1, n)

            dve.memset(ones[:], 1.0).then_inc(consts, 1)
            dve.wait_ge(weights_in, 16 * len(weights))
            for r in range(2):
                dve.tensor_copy(pick[:, N * r:N * r + N, :],
                                pick32[:, N * r:N * r + N].unsqueeze(2).broadcast_to([K3, N, P])).then_inc(consts, 1)
            dve.wait_ge(a_made, 1)
            dve.tensor_scalar(a_neg[:], a_pos[:], -1.0, None, ALU.mult).then_inc(a_made, 1)
            dve.tensor_copy(rows[:], rows32[:]).then_inc(rows_made, 1)
            dve.wait_ge(rows_made, 1)
            dve.tensor_tensor(rows32[:], rows32[:], rows[:], ALU.subtract).then_inc(rows_made, 1)
            dve.wait_ge(rows_made, 2)
            dve.tensor_copy(rows[32:64], rows32[32:64]).then_inc(rows_made, 1)
            dve.tensor_copy(rows[64:96], rows32[64:96]).then_inc(rows_made, 1)
            dve.wait_ge(rows_made, 4)
            dve.tensor_tensor(rows[64:96], rows32[64:96], rows[64:96], ALU.subtract).then_inc(rows_made, 1)
            for n in range(N):
                prepare(0, n)
            scan_state(0, 0)
            iteration(0, True, False, True)
            iteration(1, True, True, True)
            with dve.Fori(2, BATCH - 1) as i:
                iteration(i, True, True, True)
            iteration(BATCH - 1, True, True, False)
            iteration(BATCH, False, True, False)


def ffn_phase(nc, d, keep):
    BLOCKS, LANES, RANK, LINEARS = 3, 4, 32, 6
    PAIRS = BATCH // 2
    with ExitStack() as ctx:
        def sb(name, shape, dt=F32):
            return ctx.enter_context(nc.sbuf_tensor(name + "_sb", shape, dt))

        def ps(name, cols):
            return ctx.enter_context(nc.psum_tensor(name, [P, cols], F32))

        def sem(name):
            return ctx.enter_context(nc.semaphore(name))

        ident, x_all = keep["ident"], keep["x_all"]
        q, scale, w = sb("q", [P, LINEARS, P], I32), sb("scale", [P, LINEARS, P]), sb("w", [P, LINEARS, P])
        lora_a, lora_b = sb("lora_a", [RANK, LINEARS, P]), sb("lora_b", [RANK, LINEARS, P])
        gamma, beta = sb("gamma", [P, BLOCKS]), sb("beta", [P, BLOCKS])
        rows32 = sb("f_rows32", [96, LINEARS, P])
        rows, ones = sb("f_rows", [96, LINEARS, P], BF16), sb("f_ones", [96, P], BF16)
        minus_half = sb("f_minus_half", [P, HC])

        def lanes(name, *shape):
            return [sb(f"{name}{n}", [P, *shape]) for n in range(LANES)]

        h_in, h_a, h_b, hx = lanes("h_in", HC, P), lanes("h_a", HC, P), lanes("h_b", HC, P), lanes("hx", HC, P)
        hT, yn, gT = lanes("hT", HALF), lanes("yn", HC, P), lanes("gT", HALF)
        fin, out = lanes("fin", HC, P), lanes("out", HC, P)
        stats, mv = lanes("f_stats", HC, 6), lanes("f_mv", HC, 2)
        var_eps, rstd = lanes("f_var_eps", HC), lanes("f_rstd", HC)
        stats2, mv2 = lanes("g_stats", HC, 6), lanes("g_mv", HC, 2)
        var_eps2, rstd2 = lanes("g_var_eps", HC), lanes("g_rstd", HC)
        turn = [ps(f"f_turn{n}", HALF) for n in range(LANES)]
        lin = [ps(f"lin{n}", HALF) for n in range(LANES)]

        weights_in = sem("weights_in3")
        pool_settled, dve_settled = sem("f_pool_settled"), sem("f_dve_settled")
        rows_clear = sem("f_rows_clear")
        pool_const = sem("f_pool_const")
        consts = sem("f_consts")
        dequant = sem("dequant")
        lora = sem("lora")
        rows_made = sem("f_rows_made")
        h_loaded = sem("h_loaded")
        hT_ready = sem("hT_ready")
        hT_copied = sem("hT_copied")
        lin0_ready = sem("lin0_ready")
        summed = sem("f_summed")
        mv_ready = sem("f_mv_ready")
        veps_ready = sem("f_veps_ready")
        rstd_ready = sem("f_rstd_ready")
        normed = sem("normed")
        ynT_ready = sem("ynT_ready")
        gelu_done = sem("gelu_done")
        lin1_ready = sem("lin1_ready")
        res_ready = sem("f_res_ready")
        hx_ready = sem("hx_ready")
        summed2 = sem("g_summed")
        mv2_ready = sem("g_mv_ready")
        veps2_ready = sem("g_veps_ready")
        rstd2_ready = sem("g_rstd_ready")
        out_ready = sem("f_out_ready")
        stored = sem("stored")
        block = ctx.enter_context(nc.Block())

        def batches(j):
            if isinstance(j, int):
                return x_all[:, 2 * j:2 * j + 2]
            return x_all[:, bass.ds(2 * j, 2)]

        def lane_rows(j, n):
            return batches(j)[:, n // 2, HC * (n % 2):HC * (n % 2) + HC, :]

        def count(j, k, n):
            return BLOCKS * LANES * j + LANES * k + n + 1

        weights = [(q[:], d["q"]), (scale[:], d["scale"]), (lora_a[:], d["lora_a"]), (lora_b[:], d["lora_b"]),
                   (gamma[:], d["gamma"]), (beta[:], d["beta"])] + [
                       (rows32[32 * r:32 * r + 1], d["biases"]) for r in range(3)]
        out_dram = d["out"].rearrange("(j e) (f c p) d -> j e f p c d", e=2, f=2, p=P)

        @block.sync
        def _(sp):
            def load(j):
                for n in range(LANES):
                    sp.dma_start(h_in[n][:], lane_rows(j, n)).then_inc(h_loaded, 16)

            load(0)
            sp.wait_ge(rows_clear, 1)
            for dst, src in weights:
                sp.dma_start(dst, src).then_inc(weights_in, 16)

            def pair(j, more):
                if more:
                    sp.wait_ge(res_ready, count(j, 0, LANES - 1))
                    load(j + 1)
                for n in range(LANES):
                    sp.wait_ge(out_ready, HC * (LANES * j + n + 1))
                    dst = out_dram[j:j + 1] if isinstance(j, int) else out_dram[bass.ds(j, 1)]
                    sp.dma_start(dst[:, n // 2, n % 2].rearrange("j p c d -> (j p) c d"), out[n][:]).then_inc(stored, 16)

            with sp.Fori(0, PAIRS - 1) as j:
                pair(j, True)
            pair(PAIRS - 1, False)
            sp.wait_ge(stored, 16 * LANES * PAIRS)

        @block.gpsimd
        def _(pool):
            pool.memset(rows32[:], 0.0).then_inc(rows_clear, 1)
            pool.memset(minus_half[:], -0.5).then_inc(pool_const, 1)
            pool.wait_ge(pool_const, 1)

            def pair(j):
                for k in range(BLOCKS):
                    for n in range(LANES):
                        c = count(j, k, n)
                        pool.wait_ge(mv_ready, HC * c)
                        settle(pool, pool_settled)
                        pool.tensor_scalar(var_eps[n][:], mv[n][:, :, 1], 1.0, EPS, ALU.mult,
                                           ALU.add).then_inc(veps_ready, 1)
                        pool.wait_ge(veps_ready, c)
                        pool.tensor_tensor(rstd[n][:], var_eps[n][:], minus_half[:], ALU.pow).then_inc(rstd_ready, 1)
                    if k == 1:
                        for n in range(LANES):
                            pool.wait_ge(res_ready, count(j, 1, n))
                            settle(pool, pool_settled)
                            pool.tensor_tensor(hx[n][:], h_b[n][:], lane_rows(j, n), ALU.add).then_inc(hx_ready, 1)
                for n in range(LANES):
                    c = LANES * j + n + 1
                    pool.wait_ge(mv2_ready, HC * c)
                    settle(pool, pool_settled)
                    pool.tensor_scalar(var_eps2[n][:], mv2[n][:, :, 1], 1.0, EPS, ALU.mult,
                                       ALU.add).then_inc(veps2_ready, 1)
                    pool.wait_ge(veps2_ready, c)
                    pool.tensor_tensor(rstd2[n][:], var_eps2[n][:], minus_half[:], ALU.pow).then_inc(rstd2_ready, 1)

            with pool.Fori(0, PAIRS) as j:
                pair(j)

        @block.tensor
        def _(pe):
            def linear(n, src, i):
                for c in range(HC):
                    pe.matmul(lin[n][:, chunk(c)], src[n][:, chunk(c)], w[:, i, :], start=True, stop=False)
                    mm = pe.matmul(lin[n][:, chunk(c)], ones[:], rows[:, i, :], start=False, stop=True)
                return mm

            def pair(j):
                for k in range(BLOCKS):
                    for n in range(LANES):
                        if k:
                            pe.wait_ge(res_ready, count(j, k - 1, n))
                        else:
                            pe.wait_ge(h_loaded, 16 * LANES * (j + 1))
                        for c in range(HC):
                            mm = pe.transpose(turn[n][:, chunk(c)], (h_in, h_a, h_b)[k][n][:, c, :], ident[:])
                        mm.then_inc(hT_ready, 1)
                    for n in range(LANES):
                        pe.wait_ge(hT_copied, count(j, k, n))
                        wait(pe, res_ready, count(j, k - 1, n))
                        linear(n, hT, 2 * k).then_inc(lin0_ready, 1)
                    for n in range(LANES):
                        pe.wait_ge(normed, HC * count(j, k, n))
                        for c in range(HC):
                            mm = pe.transpose(turn[n][:, chunk(c)], yn[n][:, c, :], ident[:])
                        mm.then_inc(ynT_ready, 1)
                    for n in range(LANES):
                        pe.wait_ge(gelu_done, count(j, k, n))
                        linear(n, gT, 2 * k + 1).then_inc(lin1_ready, 1)

            pe.wait_ge(weights_in, 16 * len(weights))
            for i in range(LINEARS):
                mm = pe.matmul(turn[i // HC][:, chunk(i % HC)], lora_a[:, i, :], lora_b[:, i, :], start=True, stop=True)
                if i in (HC - 1, LINEARS - 1):
                    mm.then_inc(lora, 1)
            pe.wait_ge(consts, 1)
            pe.wait_ge(rows_made, 5)
            pe.wait_ge(dequant, 4)
            pair(0)
            with pe.Fori(1, PAIRS) as j:
                pair(j)

        @block.scalar
        def _(act):
            def pair(j):
                for k in range(BLOCKS):
                    for n in range(LANES):
                        act.wait_ge(hT_ready, count(j, k, n))
                        act.activation(hT[n][:], turn[n][:], ACT.Copy).then_inc(hT_copied, 1)
                    for n in range(LANES):
                        act.wait_ge(ynT_ready, count(j, k, n))
                        act.activation(gT[n][:], turn[n][:], ACT.Gelu, bias=beta[:, k:k + 1],
                                       scale=gamma[:, k:k + 1]).then_inc(gelu_done, 1)

            act.preload_act_table_set("gelu_and_others")
            act.wait_ge(weights_in, 16 * len(weights))
            with act.Fori(0, PAIRS) as j:
                pair(j)

        @block.vector
        def _(dve):
            def flat(x):
                return x[:].rearrange("p c d -> p (c d)")

            def pair(j):
                for k in range(BLOCKS):
                    for n in range(LANES + 1):
                        if n < LANES:
                            c = count(j, k, n)
                            dve.wait_ge(lin0_ready, c)
                            for s in range(HC):
                                dve.bn_stats(stats[n][:, s, :], lin[n][:, chunk(s)]).then_inc(summed, 1)
                        if n:
                            dve.wait_ge(summed, HC * count(j, k, n - 1))
                            settle(dve, dve_settled)
                            for s in range(HC):
                                dve.bn_aggr(mv[n - 1][:, s, :], stats[n - 1][:, s, :]).then_inc(mv_ready, 1)
                    for n in range(LANES):
                        dve.wait_ge(rstd_ready, count(j, k, n))
                        for s in range(HC):
                            dve.tensor_scalar(yn[n][:, s, :], lin[n][:, chunk(s)], mv[n][:, s, 0:1], rstd[n][:, s:s + 1],
                                              ALU.subtract, ALU.mult).then_inc(normed, 1)
                    for n in range(LANES):
                        dve.wait_ge(lin1_ready, count(j, k, n))
                        if k == 1:
                            wait(dve, hx_ready, LANES * (j - 1) + n + 1)
                        if k == 2:
                            dve.wait_ge(hx_ready, LANES * j + n + 1)
                        dve.tensor_tensor(flat((h_a, h_b, fin)[k][n]), lin[n][:], flat((h_in, h_a, hx)[k][n]),
                                          ALU.add).then_inc(res_ready, 1)
                for n in range(LANES + 1):
                    if n < LANES:
                        dve.wait_ge(res_ready, count(j, BLOCKS - 1, n))
                        for s in range(HC):
                            dve.bn_stats(stats2[n][:, s, :], fin[n][:, s, :]).then_inc(summed2, 1)
                    if n:
                        dve.wait_ge(summed2, HC * (LANES * j + n))
                        settle(dve, dve_settled)
                        for s in range(HC):
                            dve.bn_aggr(mv2[n - 1][:, s, :], stats2[n - 1][:, s, :]).then_inc(mv2_ready, 1)
                for n in range(LANES):
                    dve.wait_ge(rstd2_ready, LANES * j + n + 1)
                    wait(dve, stored, 16 * LANES * j)
                    for s in range(HC):
                        dve.tensor_scalar(out[n][:, s, :], fin[n][:, s, :], mv2[n][:, s, 0:1], rstd2[n][:, s:s + 1],
                                          ALU.subtract, ALU.mult).then_inc(out_ready, 1)

            dve.memset(ones[:], 1.0).then_inc(consts, 1)
            dve.wait_ge(weights_in, 16 * len(weights))
            dve.tensor_scalar(w[:], q[:], 1.0 / 7.5, -1.0, ALU.mult, ALU.add).then_inc(dequant, 1)
            dve.wait_ge(dequant, 1)
            dve.tensor_tensor(w[:], w[:], scale[:], ALU.mult).then_inc(dequant, 1)
            dve.wait_ge(dequant, 2)
            for r, cols in enumerate((slice(0, HC), slice(HC, LINEARS))):
                dve.wait_ge(lora, r + 1)
                size = (cols.stop - cols.start) * P
                dve.tensor_tensor(w[:, cols, :].rearrange("p c d -> p (c d)"), turn[r][:, 0:size],
                                  w[:, cols, :].rearrange("p c d -> p (c d)"), ALU.add).then_inc(dequant, 1)
            dve.tensor_copy(rows[:], rows32[:]).then_inc(rows_made, 1)
            dve.wait_ge(rows_made, 1)
            dve.tensor_tensor(rows32[:], rows32[:], rows[:], ALU.subtract).then_inc(rows_made, 1)
            dve.wait_ge(rows_made, 2)
            dve.tensor_copy(rows[32:64], rows32[32:64]).then_inc(rows_made, 1)
            dve.tensor_copy(rows[64:96], rows32[64:96]).then_inc(rows_made, 1)
            dve.wait_ge(rows_made, 4)
            dve.tensor_tensor(rows[64:96], rows32[64:96], rows[64:96], ALU.subtract).then_inc(rows_made, 1)
            pair(0)
            with dve.Fori(1, PAIRS) as j:
                pair(j)


def build(nc, d):
    with ExitStack() as ctx:
        keep = {
            "ident": ctx.enter_context(nc.sbuf_tensor("ident_sb", [P, P], F32)),
            "x_all": ctx.enter_context(nc.sbuf_tensor("x_all", [P, BATCH, CH, P], F32)),
        }
        attention_phase(nc, d, keep)
        ssm_phase(nc, d, keep)
        ffn_phase(nc, d, keep)


def lay_out(np, inputs):
    tr = np.ascontiguousarray
    w = inputs["L0_attn_W"]
    return {
        "L0_attn_x": tr(inputs["L0_attn_x"]),
        "ident": np.eye(P, dtype=np.float32),
        "mask": np.triu(np.full((P, P), MASKED, np.float32), 1),
        "w_key": tr(w[:P].T), "w_val": tr(w[P:].T),
        "w_r": tr(inputs["L0_ffn_W_r"].T), "w_k": tr(inputs["L0_ffn_W_k"].T), "w_v": tr(inputs["L0_ffn_W_v"].T),
        "w_dt": tr(inputs["L1_attn_Wdt"]), "w_x": tr(inputs["L1_attn_Wx"]), "w_z": tr(inputs["L1_attn_Wz"]),
        "w_out": tr(inputs["L1_attn_Wout"]),
        "w_bc": tr(np.concatenate([inputs["L1_attn_WB"], inputs["L1_attn_WC"]] * 3, 1)),
        "b_bc": tr(np.concatenate([inputs["L1_attn_bB"], inputs["L1_attn_bC"]] * 3)[:, None]),
        "b_dt": tr(inputs["L1_attn_bdt"][:, None]), "b_x": tr(inputs["L1_attn_bx"][:, None]),
        "a_log": tr(inputs["L1_attn_A_log"]),
        "pick": np.concatenate([np.eye(2 * N, dtype=np.float32)] * 3),
        "rows": tr(np.stack([inputs["L1_attn_bz"], inputs["L1_attn_bout"]])[None]),
        "q": tr(inputs["L1_ffn_qweights"].transpose(2, 0, 1)),
        "scale": tr(np.repeat(inputs["L1_ffn_scales"], P // inputs["L1_ffn_scales"].shape[2], axis=2).transpose(2, 0, 1)),
        "lora_a": tr(inputs["L1_ffn_lora_a"].transpose(1, 0, 2)),
        "lora_b": tr(inputs["L1_ffn_lora_b"].transpose(2, 0, 1)),
        "biases": tr(inputs["L1_ffn_biases"][None]),
        "gamma": tr(inputs["L1_ffn_ln_gamma"].T), "beta": tr(inputs["L1_ffn_ln_beta"].T),
        "mu": tr(np.stack([inputs["L0_ffn_mu_r"], inputs["L0_ffn_mu_k"]], 1)),
    }


def kernel(**inputs):
    import numpy as np
    import concourse.bacc as bacc
    from concourse.bass_utils import run_bass_kernel_spmd

    nc = bacc.Bacc("TRN2", target_bir_lowering=False, num_devices=1)
    arrays = lay_out(np, {name: np.asarray(a) for name, a in inputs.items()})
    dram = {name: nc.dram_tensor(name, a.shape, mybir.dt.from_np(a.dtype), kind="ExternalInput").ap()
            for name, a in arrays.items()}
    dram["out"] = nc.dram_tensor("out", (BATCH, T, P), F32, kind="ExternalOutput").ap()
    build(nc, dram)
    r = run_bass_kernel_spmd(nc, [arrays], core_ids=[0])
    return r.results[0]["out"]
```

```python
from contextlib import ExitStack

import concourse.bass as bass
from concourse import mybir

F32 = mybir.dt.float32
BF16 = mybir.dt.bfloat16
I32 = mybir.dt.int32
ALU = mybir.AluOpType
ACT = mybir.ActivationFunctionType
AX = mybir.AxisListType

P = 128
BATCH = 8
T = 1024
CH = T // P
HALF = 512
HC = HALF // P
N = 16
EPS = 1e-5
MASKED = -1e30


def wait(eng, sem, value):
    if not (isinstance(value, int) and value <= 0):
        eng.wait_ge(sem, value)


def settle(eng, settled):
    eng.sem_inc(settled, 1)


def chunk(c):
    return slice(c * P, (c + 1) * P)


def half(h):
    return slice(h * HALF, (h + 1) * HALF)


def groups(q):
    first = q if q < HC else HC + 2 * (q - HC)
    return [(first + g, g * HC, min(HC, q + 1 - g * HC)) for g in range(1 + (q >= HC))]


THIRDS = (range(0, 3), range(3, 6), range(6, 8))
GROUPS = groups(CH - 1)[-1][0] + 1


def attention_phase(nc, d, keep):
    with ExitStack() as ctx:
        def sb(name, shape, dt=F32):
            return ctx.enter_context(nc.sbuf_tensor(name + "_sb", shape, dt))

        def ps(name, cols):
            return ctx.enter_context(nc.psum_tensor(name, [P, cols], F32))

        def sem(name):
            return ctx.enter_context(nc.semaphore(name))

        ident, x_all = keep["ident"], keep["x_all"]
        w_key, w_val = sb("w_key", [P, P]), sb("w_val", [P, P])
        w_r, w_k, w_v = sb("w_r", [P, P]), sb("w_k", [P, P]), sb("w_v", [P, P])
        mu = sb("mu", [P, 2])
        mask32, mask, ident16 = sb("mask32", [P, P]), sb("mask", [P, P], BF16), sb("ident16", [P, P], BF16)
        minus_half = sb("a_minus_half", [P, CH])
        xin, xx = sb("xin", [P, CH, P]), sb("xx", [P, CH, P])
        xT, kT, val = sb("xT", [P, T]), sb("kT", [P, T]), sb("val", [P, CH, P])
        probs, probsT = sb("probs", [P, 2, T]), sb("probsT", [P, 2, T])
        negmax, rowsum, rinv = sb("negmax", [P, 2]), sb("rowsum", [P, CH]), sb("rinv", [P, 2])
        att, stats, mv = sb("att", [P, CH, P]), sb("stats", [P, CH, 6]), sb("mv", [P, CH, 2])
        var_eps, rstd, shift = sb("var_eps", [P, CH]), sb("rstd", [P, CH]), sb("shift", [P, CH])
        x1 = sb("x1", [P, CH, P])
        x1T, diff = sb("x1T", [P, 1 + T]), sb("diff", [P, T])
        xk, xr = sb("xk", [P, T]), sb("xr", [P, T])
        relu, kact = sb("relu", [P, T]), sb("kact", [P, T])
        gate, mixed = sb("gate", [P, T]), sb("mixed", [P, CH, P])
        stats2, mv2 = sb("stats2", [P, CH, 6]), sb("mv2", [P, CH, 2])
        var_eps2, rstd2 = sb("var_eps2", [P, CH]), sb("rstd2", [P, CH])
        score = [ps("score0", T), ps("score1", T)]
        turn = [ps("turn0", HALF), ps("turn1", HALF)]
        pv, mix = ps("pv", HALF), ps("mix", HALF)

        weights_in = sem("weights_in")
        pool_settled, dve_settled = sem("a_pool_settled"), sem("a_dve_settled")
        minus_made = sem("minus_made")
        zero_made = sem("zero_made")
        consts = sem("consts")
        x_in = sem("x_in")
        xx_made = sem("xx_made")
        xT_ready = sem("xT_ready")
        xT_copied = sem("xT_copied")
        k_ready = sem("k_ready")
        k_copied = sem("k_copied")
        v_ready = sem("v_ready")
        v_copied = sem("v_copied")
        scored = sem("scored")
        max_found = sem("max_found")
        exp_done = sem("exp_done")
        turned = sem("turned")
        even_copied = sem("even_copied")
        odd_copied = sem("odd_copied")
        pv_done = sem("pv_done")
        inverted = sem("inverted")
        combined = sem("combined")
        summed = sem("summed")
        mv_ready = sem("mv_ready")
        veps_ready = sem("veps_ready")
        rstd_ready = sem("rstd_ready")
        shift_part = sem("shift_part")
        x1_ready = sem("x1_ready")
        x1T_ready = sem("x1T_ready")
        x1T_copied = sem("x1T_copied")
        diff_ready = sem("diff_ready")
        xk_ready = sem("xk_ready")
        km_ready = sem("km_ready")
        relu_done = sem("relu_done")
        kact_ready = sem("kact_ready")
        r_ready = sem("r_ready")
        gate_ready = sem("gate_ready")
        vm_ready = sem("vm_ready")
        gated = sem("gated")
        mixed_ready = sem("mixed_ready")
        summed2 = sem("summed2")
        mv2_ready = sem("mv2_ready")
        veps2_ready = sem("veps2_ready")
        rstd2_ready = sem("rstd2_ready")
        x2_ready = sem("x2_ready")
        block = ctx.enter_context(nc.Block())

        x_dram = d["L0_attn_x"].rearrange("b (c p) d -> p b c d", p=P)
        weights = [(ident[:], d["ident"]), (w_key[:], d["w_key"]), (w_val[:], d["w_val"]), (mask32[:], d["mask"]),
                   (w_r[:], d["w_r"]), (w_k[:], d["w_k"]), (w_v[:], d["w_v"]), (mu[:], d["mu"])]

        @block.sync
        def _(sp):
            sp.dma_start(xin[:], x_dram[:, 0]).then_inc(x_in, 16)
            for dst, src in weights:
                sp.dma_start(dst, src).then_inc(weights_in, 16)
            with sp.Fori(1, BATCH) as i:
                wait(sp, xT_ready, 2 * i)
                wait(sp, xx_made, i)
                sp.dma_start(xin[:], x_dram[:, bass.ds(i, 1)].rearrange("p b c d -> p (b c) d")).then_inc(x_in, 16)

        @block.gpsimd
        def _(pool):
            pool.memset(minus_half[:], -0.5).then_inc(minus_made, 1)
            pool.memset(x1T[:, 0:1], 0.0).then_inc(zero_made, 1)
            pool.wait_ge(minus_made, 1)
            pool.wait_ge(zero_made, 1)

            def double(i):
                pool.wait_ge(x_in, 16 * i + 16)
                wait(pool, combined, CH * i)
                settle(pool, pool_settled)
                pool.tensor_scalar(xx[:], xin[:], 2.0, 0.0, ALU.mult, ALU.add).then_inc(xx_made, 1)

            def mix_inputs(b):
                pool.wait_ge(x1T_copied, 2 * b + 2)
                wait(pool, xk_ready, 2 * b)
                pool.tensor_tensor(diff[:], x1T[:, 1:1 + T], x1T[:, 0:T], ALU.subtract).then_inc(diff_ready, 1)
                for h in range(2):
                    pool.wait_ge(relu_done, 2 * b + h + 1)
                    wait(pool, vm_ready, 2 * b)
                    pool.tensor_tensor(kact[:, half(h)], relu[:, half(h)], relu[:, half(h)],
                                       ALU.mult).then_inc(kact_ready, 1)

            def inverse_std(b, mean_var, ready, ve, made, out, done, used):
                pool.wait_ge(ready, CH * b + CH)
                settle(pool, pool_settled)
                pool.tensor_scalar(ve[:], mean_var[:, :, 1], 1.0, EPS, ALU.mult, ALU.add).then_inc(made, 1)
                pool.wait_ge(made, b + 1)
                wait(pool, used, CH * b)
                pool.tensor_tensor(out[:], ve[:], minus_half[:], ALU.pow).then_inc(done, 1)

            def normalise_x1(i):
                pool.wait_ge(rstd_ready, i + 1)
                pool.tensor_tensor(shift[:], mv[:, :, 0], rstd[:], ALU.mult).then_inc(shift_part, 1)
                pool.wait_ge(shift_part, 2 * i + 1)
                settle(pool, pool_settled)
                pool.tensor_scalar(shift[:], shift[:], -1.0, 0.0, ALU.mult, ALU.add).then_inc(shift_part, 1)
                pool.wait_ge(shift_part, 2 * i + 2)
                wait(pool, x1T_ready, 2 * i)
                wait(pool, mixed_ready, 2 * i)
                settle(pool, pool_settled)
                for c in range(CH):
                    pool.tensor_scalar(x1[:, c, :], att[:, c, :], rstd[:, c:c + 1], shift[:, c:c + 1],
                                       ALU.mult, ALU.add).then_inc(x1_ready, 1)

            def inverse_std2(b):
                inverse_std(b, mv2, mv2_ready, var_eps2, veps2_ready, rstd2, rstd2_ready, x2_ready)

            def iteration(i, attend, channel, later):
                if attend:
                    double(i)
                if later:
                    inverse_std2(i - 2)
                if channel:
                    mix_inputs(i - 1)
                if attend:
                    inverse_std(i, mv, mv_ready, var_eps, veps_ready, rstd, rstd_ready, x1_ready)
                    normalise_x1(i)

            iteration(0, True, False, False)
            iteration(1, True, True, False)
            with pool.Fori(2, BATCH) as i:
                iteration(i, True, True, True)
            iteration(BATCH, False, True, True)
            inverse_std2(BATCH - 1)

        @block.tensor
        def _(pe):
            def transpose_x(i):
                pe.wait_ge(x_in, 16 * i + 16)
                for h in range(2):
                    wait(pe, odd_copied if h else even_copied, GROUPS // 2 * i)
                    for c in range(HC):
                        mm = pe.transpose(turn[h][:, chunk(c)], xin[:, HC * h + c, :], ident[:])
                    mm.then_inc(xT_ready, 1)

            def keys_values(i):
                for h in range(2):
                    pe.wait_ge(xT_copied, 2 * i + h + 1)
                    if h == 0:
                        wait(pe, exp_done, CH * i - 1)
                    pe.matmul(score[0][:, half(h)], w_key[:], xT[:, half(h)], start=True, stop=True).then_inc(k_ready, 1)
                wait(pe, exp_done, CH * i)
                for h in range(2):
                    for c in range(HC):
                        mm = pe.matmul(score[1][:, chunk(HC * h + c)], xT[:, chunk(HC * h + c)], w_val[:],
                                       start=True, stop=True)
                    mm.then_inc(v_ready, 1)

            def scores(i, q):
                if q < 2:
                    pe.wait_ge(v_copied if q else k_copied, 2 * i + 2)
                else:
                    pe.wait_ge(exp_done, CH * i + q - 1)
                s = score[q % 2]
                for lo in range(0, q * P, HALF):
                    hi = min(lo + HALF, q * P)
                    pe.matmul(s[:, lo:hi], xT[:, chunk(q)], kT[:, lo:hi], start=True, stop=True)
                pe.matmul(s[:, chunk(q)], xT[:, chunk(q)], kT[:, chunk(q)], start=True, stop=False)
                pe.matmul(s[:, chunk(q)], ident16[:], mask[:], start=False, stop=True).then_inc(scored, 1)

            def transpose_probs(i, q):
                pe.wait_ge(exp_done, CH * i + q + 1)
                for g, first, blocks in groups(q):
                    if g < 2:
                        pe.wait_ge(xT_copied, 2 * i + 2)
                    else:
                        pe.wait_ge(odd_copied if g % 2 else even_copied, GROUPS // 2 * i + g // 2)
                    for k in range(blocks):
                        mm = pe.transpose(turn[g % 2][:, chunk(k)], probs[:, q % 2, chunk(first + k)], ident[:])
                    mm.then_inc(turned, 1)

            def weigh_values(i, q):
                for g, _, _ in groups(q):
                    pe.wait_ge(odd_copied if g % 2 else even_copied, GROUPS // 2 * i + g // 2 + 1)
                wait(pe, combined, CH * i + q)
                for k in range(q + 1):
                    mm = pe.matmul(pv[:, 0:P], probsT[:, q % 2, chunk(k)], val[:, k, :], start=k == 0, stop=k == q)
                mm.then_inc(pv_done, 1)

            def channel_piece(b, n):
                h = n % 2
                if n < 2:
                    if h:
                        pe.wait_ge(x1T_copied, 2 * b + 1)
                    else:
                        pe.wait_ge(x1_ready, CH * b + CH)
                        wait(pe, gated, 2 * b)
                    for c in range(HC):
                        mm = pe.transpose(mix[:, chunk(c)], x1[:, HC * h + c, :], ident[:])
                    mm.then_inc(x1T_ready, 1)
                elif n < 4:
                    pe.wait_ge(xk_ready, 2 * b + 1)
                    if h:
                        pe.wait_ge(relu_done, 2 * b + 1)
                    else:
                        pe.wait_ge(x1T_copied, 2 * b + 2)
                    pe.matmul(mix[:], w_k[:], xk[:, half(h)], start=True, stop=True).then_inc(km_ready, 1)
                elif n < 6:
                    pe.wait_ge(xk_ready, 2 * b + 2)
                    if h:
                        pe.wait_ge(gate_ready, 2 * b + 1)
                    else:
                        pe.wait_ge(relu_done, 2 * b + 2)
                    for c in range(HC):
                        mm = pe.matmul(mix[:, chunk(c)], xr[:, chunk(HC * h + c)], w_r[:], start=True, stop=True)
                    mm.then_inc(r_ready, 1)
                else:
                    pe.wait_ge(kact_ready, 2 * b + h + 1)
                    if h:
                        pe.wait_ge(gated, 2 * b + 1)
                    else:
                        pe.wait_ge(gate_ready, 2 * b + 2)
                    for c in range(HC):
                        mm = pe.matmul(mix[:, chunk(c)], kact[:, chunk(HC * h + c)], w_v[:], start=True, stop=True)
                    mm.then_inc(vm_ready, 1)

            def iteration(i, attend, channel):
                if attend:
                    transpose_x(i)
                    keys_values(i)
                for s in range(CH + 2):
                    if attend and s < CH:
                        scores(i, s)
                    if attend and s >= 2:
                        weigh_values(i, s - 2)
                    if attend and 1 <= s <= CH:
                        transpose_probs(i, s - 1)
                    if channel:
                        for n in {2: (0,), 3: (1,), 5: (2,), 6: (3, 4), 7: (5,), 8: (6,), 9: (7,)}.get(s, ()):
                            channel_piece(i - 1, n)

            pe.wait_ge(weights_in, 16 * len(weights))
            pe.wait_ge(consts, 2)
            iteration(0, True, False)
            iteration(1, True, True)
            with pe.Fori(2, BATCH) as i:
                iteration(i, True, True)
            iteration(BATCH, False, True)

        @block.scalar
        def _(act):
            def channel_piece(b, n):
                h = n % 2
                if n < 2:
                    act.wait_ge(x1T_ready, 2 * b + h + 1)
                    wait(act, xk_ready, 2 * b)
                    act.activation(x1T[:, 1 + h * HALF:1 + (h + 1) * HALF], mix[:], ACT.Copy).then_inc(x1T_copied, 1)
                elif n < 4:
                    act.wait_ge(km_ready, 2 * b + h + 1)
                    wait(act, kact_ready, 2 * b)
                    act.activation(relu[:, half(h)], mix[:], ACT.Relu).then_inc(relu_done, 1)
                else:
                    act.wait_ge(r_ready, 2 * b + h + 1)
                    wait(act, mixed_ready, 2 * b)
                    act.activation(gate[:, half(h)], mix[:], ACT.Tanh, scale=0.5).then_inc(gate_ready, 1)

            def iteration(i, attend, channel):
                b = i - 1
                if attend:
                    for h in range(2):
                        act.wait_ge(xT_ready, 2 * i + h + 1)
                        act.activation(xT[:, half(h)], turn[h][:], ACT.Copy).then_inc(xT_copied, 1)
                    for h in range(2):
                        act.wait_ge(k_ready, 2 * i + h + 1)
                        act.activation(kT[:, half(h)], score[0][:, half(h)], ACT.Copy).then_inc(k_copied, 1)
                for s in range(CH + 1):
                    if attend and s < CH:
                        act.wait_ge(max_found, CH * i + s + 1)
                        if s >= 2:
                            act.wait_ge(turned, GROUPS * i + groups(s - 2)[-1][0] + 1)
                        else:
                            wait(act, turned, GROUPS * (i - 1) + groups(CH - 2 + s)[-1][0] + 1)
                        wait(act, combined, CH * (i - 1) + s + 1)
                        act.activation(probs[:, s % 2, 0:(s + 1) * P], score[s % 2][:, 0:(s + 1) * P], ACT.Exp,
                                       bias=negmax[:, s % 2:s % 2 + 1],
                                       accum_out=rowsum[:, s:s + 1]).then_inc(exp_done, 1)
                    if attend and s >= 1:
                        for g, first, blocks in groups(s - 1):
                            if g % 2 == 0:
                                act.wait_ge(turned, GROUPS * i + g + 1)
                                wait(act, pv_done, CH * i + s - 2)
                                act.activation(probsT[:, (s - 1) % 2, first * P:(first + blocks) * P],
                                               turn[0][:, 0:blocks * P], ACT.Copy).then_inc(even_copied, 1)
                    if channel:
                        for n in {2: (0,), 3: (1,), 5: (2,), 6: (3, 4), 7: (5,)}.get(s, ()):
                            channel_piece(b, n)

            iteration(0, True, False)
            iteration(1, True, True)
            with act.Fori(2, BATCH) as i:
                iteration(i, True, True)
            iteration(BATCH, False, True)

        @block.vector
        def _(dve):
            def find_max(i, q):
                dve.wait_ge(scored, CH * i + q + 1)
                dve.tensor_reduce(negmax[:, q % 2:q % 2 + 1], score[q % 2][:, 0:(q + 1) * P], AX.X, ALU.max,
                                  negate=True).then_inc(max_found, 1)

            def combine(i, q):
                dve.wait_ge(pv_done, CH * i + q + 1)
                dve.wait_ge(inverted, CH * i + q + 1)
                dve.wait_ge(xx_made, i + 1)
                wait(dve, x1_ready, CH * i)
                dve.scalar_tensor_tensor(out=att[:, q, :], in0=pv[:, 0:P], scalar=rinv[:, q % 2:q % 2 + 1],
                                         in1=xx[:, q, :], op0=ALU.mult, op1=ALU.add).then_inc(combined, 1)

            def invert(i, q):
                dve.wait_ge(exp_done, CH * i + q + 1)
                dve.reciprocal(rinv[:, q % 2:q % 2 + 1], rowsum[:, q:q + 1]).then_inc(inverted, 1)

            def copy_odd(i, q):
                for g, first, blocks in groups(q):
                    if g % 2:
                        dve.wait_ge(turned, GROUPS * i + g + 1)
                        wait(dve, pv_done, CH * i + q - 1)
                        dve.tensor_copy(probsT[:, q % 2, first * P:(first + blocks) * P],
                                        turn[1][:, 0:blocks * P]).then_inc(odd_copied, 1)

            def sum_up(i, q):
                dve.wait_ge(combined, CH * i + q + 1)
                dve.bn_stats(stats[:, q, :], att[:, q, :]).then_inc(summed, 1)

            def mix_inputs(b, second):
                dve.wait_ge(diff_ready, b + 1)
                wait(dve, r_ready if second else km_ready, 2 * b)
                out, m = (xr, 0) if second else (xk, 1)
                dve.scalar_tensor_tensor(out=out[:], in0=diff[:], scalar=mu[:, m:m + 1], in1=x1T[:, 0:T],
                                         op0=ALU.mult, op1=ALU.add).then_inc(xk_ready, 1)

            def apply_gate(b, h):
                dve.wait_ge(gate_ready, 2 * b + h + 1)
                dve.wait_ge(vm_ready, 2 * b + h + 1)
                dve.scalar_tensor_tensor(out=gate[:, half(h)], in0=gate[:, half(h)], scalar=1.0, in1=mix[:],
                                         op0=ALU.add, op1=ALU.mult).then_inc(gated, 1)

            def add_x1(b, h):
                dve.wait_ge(gated, 2 * b + h + 1)
                cs = slice(HC * h, HC * h + HC)
                dve.scalar_tensor_tensor(out=mixed[:, cs, :].rearrange("p c d -> p (c d)"), in0=gate[:, half(h)],
                                         scalar=0.5, in1=x1[:, cs, :].rearrange("p c d -> p (c d)"),
                                         op0=ALU.mult, op1=ALU.add).then_inc(mixed_ready, 1)

            def sum_up2(b, cs):
                dve.wait_ge(mixed_ready, 2 * b + 2)
                for c in cs:
                    dve.bn_stats(stats2[:, c, :], mixed[:, c, :]).then_inc(summed2, 1)

            def aggregate(b, sums, done, out, ready):
                dve.wait_ge(done, CH * b + CH)
                settle(dve, dve_settled)
                for c in range(CH):
                    dve.bn_aggr(out[:, c, :], sums[:, c, :]).then_inc(ready, 1)

            def normalise_x2(b, cs):
                dve.wait_ge(rstd2_ready, b + 1)
                out = x_all[:, b] if isinstance(b, int) else \
                    x_all[:, bass.ds(b, 1)].rearrange("p b c d -> p (b c) d")
                for c in cs:
                    dve.tensor_scalar(out[:, c, :], mixed[:, c, :], mv2[:, c, 0:1], rstd2[:, c:c + 1],
                                      ALU.subtract, ALU.mult).then_inc(x2_ready, 1)

            def iteration(i, attend, channel, later):
                b = i - 1
                if attend:
                    for h in range(2):
                        dve.wait_ge(v_ready, 2 * i + h + 1)
                        dve.tensor_copy(val[:, HC * h:HC * h + HC, :].rearrange("p c d -> p (c d)"),
                                        score[1][:, half(h)]).then_inc(v_copied, 1)
                for s in range(CH + 2):
                    if attend:
                        if s < CH:
                            find_max(i, s)
                        if 1 <= s <= CH:
                            invert(i, s - 1)
                        if s >= 2:
                            combine(i, s - 2)
                        if 1 <= s <= CH:
                            copy_odd(i, s - 1)
                        if s >= 2:
                            sum_up(i, s - 2)
                    if later and s < 3:
                        sum_up2(b - 1, THIRDS[s])
                    if later and s == 3:
                        aggregate(b - 1, stats2, summed2, mv2, mv2_ready)
                    if later and 5 <= s < 8:
                        normalise_x2(b - 1, THIRDS[s - 5])
                    if channel and s in (4, 5):
                        mix_inputs(b, s == 5)
                    if channel and s == 8:
                        apply_gate(b, 0)
                        add_x1(b, 0)
                if attend:
                    aggregate(i, stats, summed, mv, mv_ready)
                if channel:
                    apply_gate(b, 1)
                    add_x1(b, 1)

            dve.wait_ge(weights_in, 16 * len(weights))
            dve.tensor_copy(mask[:], mask32[:]).then_inc(consts, 1)
            dve.tensor_copy(ident16[:], ident[:]).then_inc(consts, 1)
            iteration(0, True, False, False)
            iteration(1, True, True, False)
            with dve.Fori(2, BATCH) as i:
                iteration(i, True, True, True)
            iteration(BATCH, False, True, True)
            sum_up2(BATCH - 1, range(CH))
            aggregate(BATCH - 1, stats2, summed2, mv2, mv2_ready)
            normalise_x2(BATCH - 1, range(CH))


def at(i, n):
    return i + n // N, n % N


def step_count(i, n):
    return N * i + n


def ssm_phase(nc, d, keep):
    with ExitStack() as ctx:
        def sb(name, shape, dt=F32):
            return ctx.enter_context(nc.sbuf_tensor(name + "_sb", shape, dt))

        def ps(name, cols):
            return ctx.enter_context(nc.psum_tensor(name, [P, cols], F32))

        def sem(name):
            return ctx.enter_context(nc.semaphore(name))

        ident, x_all = keep["ident"], keep["x_all"]
        K3 = 3 * 2 * N
        w_dt, w_x, w_z, w_out = sb("w_dt", [P, P]), sb("w_x", [P, P]), sb("w_z", [P, P]), sb("w_out", [P, P])
        w_bc, b_bc = sb("w_bc", [P, K3]), sb("b_bc", [K3, 1])
        b_dt, b_x, a_log = sb("b_dt", [P, 1]), sb("b_x", [P, 1]), sb("a_log", [P, N])
        a_pos, a_neg = sb("a_pos", [P, N]), sb("a_neg", [P, N])
        pick32, pick = sb("pick32", [K3, 2 * N]), sb("pick", [K3, 2 * N, P], BF16)
        rows32 = sb("rows32", [K3, 2, P])
        rows, ones = sb("rows", [K3, 2, P], BF16), sb("ones", [K3, P], BF16)
        minus_half = sb("s_minus_half", [P, CH])
        x2, x2T = sb("x2", [P, CH, P]), sb("x2T", [P, T])
        dt, u, bc = sb("dt", [P, 2, T]), sb("u", [P, 2, T]), sb("bc", [K3, 2, T], BF16)
        mag, soft, bc32, rest = sb("mag", [P, T]), sb("soft", [P, T]), sb("bc32", [K3, T]), sb("rest", [K3, T])
        z = sb("z", [P, 2, T])
        a, bn, xb = sb("a", [P, 2, T]), sb("bn", [P, 2, T]), sb("xb", [P, 2, T])
        h, hc = sb("h", [P, 4, T]), sb("hc", [P, 2, T])
        yz, yzT, res = sb("yz", [P, T]), sb("yzT", [P, T]), sb("res", [P, CH, P])
        stats, mv = sb("s_stats", [P, CH, 6]), sb("s_mv", [P, CH, 2])
        var_eps, rstd = sb("s_var_eps", [P, CH]), sb("s_rstd", [P, CH])
        b_bank = [ps("b_bank0", HALF), ps("b_bank1", HALF)]
        c_bank = [ps("c_bank0", HALF), ps("c_bank1", HALF)]
        side = [ps("side0", HALF), ps("side1", HALF)]
        y = ps("y", T)

        weights_in = sem("weights_in2")
        a_made = sem("a_made")
        rows_made = sem("rows_made")
        pool_settled, dve_settled, act_settled = sem("s_pool_settled"), sem("s_dve_settled"), sem("s_act_settled")
        rows_clear = sem("rows_clear")
        pool_const = sem("pool_const")
        consts = sem("consts2")
        x2_in = sem("x2_in")
        x2T_ready = sem("x2T_ready")
        x2T_copied = sem("x2T_copied")
        dt_raw = sem("dt_raw")
        mag_done = sem("mag_done")
        relu_dt = sem("relu_dt")
        soft_exp = sem("soft_exp")
        soft_ln = sem("soft_ln")
        dt_ready = sem("dt_ready")
        xs_ready = sem("xs_ready")
        u_ready = sem("u_ready")
        bc_raw = sem("bc_raw")
        bc_high = sem("bc_high")
        bc_step = sem("bc_step")
        z_raw = sem("z_raw")
        z_ready = sem("z_ready")
        b_ready = sem("b_ready")
        b_copied = sem("b_copied")
        a_ready = sem("a_ready")
        xb_ready = sem("xb_ready")
        scanned = sem("scanned")
        c_ready = sem("c_ready")
        hc_ready = sem("hc_ready")
        summed_y = sem("summed_y")
        yz_ready = sem("yz_ready")
        yzT_ready = sem("yzT_ready")
        yzT_copied = sem("yzT_copied")
        out_ready = sem("out_ready")
        res_ready = sem("res_ready")
        summed = sem("s_summed")
        mv_ready = sem("s_mv_ready")
        veps_ready = sem("s_veps_ready")
        rstd_ready = sem("s_rstd_ready")
        x3_ready = sem("x3_ready")
        block = ctx.enter_context(nc.Block())

        def rows_of(b):
            if isinstance(b, int):
                return x_all[:, b]
            return x_all[:, bass.ds(b, 1)].rearrange("p b c d -> p (b c) d")

        def slot(buf, b):
            if isinstance(b, int):
                return buf[:, b % 2]
            return buf[:, bass.ds(b % 2, 1)].rearrange("p b t -> p (b t)")

        weights = [(w_dt[:], d["w_dt"]), (w_x[:], d["w_x"]), (w_z[:], d["w_z"]), (w_out[:], d["w_out"]),
                   (w_bc[:], d["w_bc"]), (b_bc[:], d["b_bc"]), (b_dt[:], d["b_dt"]), (b_x[:], d["b_x"]),
                   (a_log[:], d["a_log"]), (pick32[:], d["pick"])] + [
                       (rows32[32 * k:32 * k + 1], d["rows"]) for k in range(3)]

        @block.sync
        def _(sp):
            sp.dma_start(x2[:], x_all[:, 0]).then_inc(x2_in, 16)
            sp.wait_ge(rows_clear, 1)
            for dst, src in weights:
                sp.dma_start(dst, src).then_inc(weights_in, 16)
            with sp.Fori(1, BATCH) as i:
                wait(sp, x2T_ready, 2 * i)
                sp.dma_start(x2[:], rows_of(i)).then_inc(x2_in, 16)

        @block.gpsimd
        def _(pool):
            def scale_b(i, n):
                g = step_count(*at(i, n))
                b = at(i, n)[0]
                if at(i, n)[1] == 0:
                    pool.wait_ge(u_ready, 2 * b + 2)
                pool.wait_ge(b_copied, 2 * g + 2)
                wait(pool, scanned, g - 1)
                settle(pool, pool_settled)
                pool.tensor_tensor(xb[:, n % 2, :], slot(u, b), bn[:, n % 2, :], ALU.mult).then_inc(xb_ready, 1)

            def inverse_std(b):
                pool.wait_ge(mv_ready, CH * b + CH)
                settle(pool, pool_settled)
                pool.tensor_scalar(var_eps[:], mv[:, :, 1], 1.0, EPS, ALU.mult, ALU.add).then_inc(veps_ready, 1)
                pool.wait_ge(veps_ready, b + 1)
                wait(pool, x3_ready, CH * b)
                pool.tensor_tensor(rstd[:], var_eps[:], minus_half[:], ALU.pow).then_inc(rstd_ready, 1)

            def iteration(i, scan, finish, more):
                for n in range(N):
                    if scan and (more or n + 2 < N):
                        scale_b(i, n + 2)
                    if finish and n == 13:
                        inverse_std(i - 1)

            pool.memset(rows32[:], 0.0).then_inc(rows_clear, 1)
            pool.memset(minus_half[:], -0.5).then_inc(pool_const, 1)
            pool.wait_ge(pool_const, 1)
            for n in range(2):
                scale_b(0, n)
            iteration(0, True, False, True)
            iteration(1, True, True, True)
            with pool.Fori(2, BATCH - 1) as i:
                iteration(i, True, True, True)
            iteration(BATCH - 1, True, True, False)
            iteration(BATCH, False, True, False)

        @block.tensor
        def _(pe):
            def spread_b(i, n):
                b, k = at(i, n)
                g = step_count(b, k)
                if k == 0:
                    pe.wait_ge(bc_step, 4 * b + 4)
                for f in range(2):
                    wait(pe, b_copied, 2 * g + f - 1)
                    pe.matmul(b_bank[f][:], pick[:, k, :], slot(bc, b)[:, half(f)], start=True,
                              stop=True).then_inc(b_ready, 1)

            def spread_c(i, n):
                g = step_count(i, n)
                for f in range(2):
                    wait(pe, hc_ready, 2 * g + f - 1)
                    pe.matmul(c_bank[f][:], pick[:, N + n, :], slot(bc, i)[:, half(f)], start=True,
                              stop=True).then_inc(c_ready, 1)

            def sum_states(i, n):
                b, k = at(i, n)
                g = step_count(b, k)
                pe.wait_ge(hc_ready, 2 * g + 2)
                if k == 0:
                    wait(pe, yz_ready, 2 * b)
                for c in range(CH):
                    mm = pe.matmul(y[:, chunk(c)], hc[:, k % 2, chunk(c)], ident[:], is_transpose=True,
                                   start=k == 0 and c % HC == 0, stop=k == N - 1, skip_group_check=True)
                mm.then_inc(summed_y, 1)

            def prepare(b, n):
                if n == 0:
                    pe.wait_ge(x2_in, 16 * b + 16)
                    wait(pe, res_ready, 2 * (b - 2))
                    wait(pe, z_ready, 2 * b)
                    for f in range(2):
                        for c in range(HC):
                            mm = pe.transpose(side[f][:, chunk(c)], x2[:, HC * f + c, :], ident[:])
                        mm.then_inc(x2T_ready, 1)
                elif n in (1, 2):
                    f = n - 1
                    pe.wait_ge(x2T_copied, 2 * b + f + 1)
                    pe.matmul(side[f][:], w_dt[:], x2T[:, half(f)], start=True, stop=True).then_inc(dt_raw, 1)
                elif n in (3, 4):
                    f = n - 3
                    pe.wait_ge(mag_done, 2 * b + f + 1)
                    pe.wait_ge(relu_dt, 2 * b + f + 1)
                    pe.matmul(side[f][:], w_x[:], x2T[:, half(f)], start=True, stop=True).then_inc(xs_ready, 1)
                elif n in (5, 6):
                    f = n - 5
                    pe.wait_ge(u_ready, 2 * b + f + 1)
                    pe.matmul(side[f][0:K3, :], w_bc[:], x2T[:, half(f)], start=True, stop=True).then_inc(bc_raw, 1)
                elif n in (8, 9):
                    f = n - 8
                    if f == 0:
                        pe.wait_ge(bc_high, 4 * b + 4)
                    wait(pe, yzT_copied, 2 * (b - 2) + f + 1)
                    for c in range(HC):
                        pe.matmul(side[f][:, chunk(c)], x2T[:, chunk(HC * f + c)], w_z[:], start=True, stop=False)
                        mm = pe.matmul(side[f][:, chunk(c)], ones[:], rows[:, 0, :], start=False, stop=True)
                    mm.then_inc(z_raw, 1)

            def finish(b, n, last):
                if n == 7:
                    pe.wait_ge(yz_ready, 2 * b + 2)
                    wait(pe, res_ready, 2 * b)
                    if not last:
                        pe.wait_ge(bc_high, 4 * (b + 2) + 4)
                    for f in range(2):
                        for c in range(HC):
                            mm = pe.transpose(side[f][:, chunk(c)], yz[:, chunk(HC * f + c)], ident[:])
                        mm.then_inc(yzT_ready, 1)
                elif n in (10, 11):
                    f = n - 10
                    pe.wait_ge(yzT_copied, 2 * b + f + 1)
                    if not last:
                        pe.wait_ge(z_ready, 2 * (b + 2) + f + 1)
                    for c in range(HC):
                        pe.matmul(side[f][:, chunk(c)], yzT[:, chunk(HC * f + c)], w_out[:], start=True, stop=False)
                        mm = pe.matmul(side[f][:, chunk(c)], ones[:], rows[:, 1, :], start=False, stop=True)
                    mm.then_inc(out_ready, 1)

            def iteration(i, scan, done, more):
                for n in range(N):
                    if scan:
                        spread_c(i, n)
                        if more or n + 3 < N:
                            spread_b(i, n + 3)
                    if more:
                        prepare(i + 1, n)
                    if done:
                        finish(i - 1, n, not more)
                    if (scan and n >= 1) or (done and n == 0):
                        sum_states(i, n - 1)

            pe.wait_ge(weights_in, 16 * len(weights))
            pe.wait_ge(consts, 3)
            pe.wait_ge(rows_made, 5)
            for n in range(N):
                prepare(0, n)
            for n in range(3):
                spread_b(0, n)
            iteration(0, True, False, True)
            iteration(1, True, True, True)
            with pe.Fori(2, BATCH - 1) as i:
                iteration(i, True, True, True)
            iteration(BATCH - 1, True, True, False)
            iteration(BATCH, False, True, False)

        @block.scalar
        def _(act):
            def copy_b(i, n):
                g = step_count(*at(i, n))
                for f in range(2):
                    act.wait_ge(b_ready, 2 * g + f + 1)
                    if f == 0:
                        wait(act, xb_ready, g - 1)
                    act.activation(bn[:, n % 2, half(f)], b_bank[f][:], ACT.Copy).then_inc(b_copied, 1)

            def decay(i, n):
                b, k = at(i, n)
                g = step_count(b, k)
                if k == 0:
                    act.wait_ge(dt_ready, b + 1)
                wait(act, scanned, g - 1)
                settle(act, act_settled)
                act.activation(a[:, n % 2, :], slot(dt, b), ACT.Exp, scale=a_neg[:, k:k + 1]).then_inc(a_ready, 1)

            def prepare(b, n):
                if n == 0:
                    for f in range(2):
                        act.wait_ge(x2T_ready, 2 * b + f + 1)
                        wait(act, z_raw, 2 * b)
                        act.activation(x2T[:, half(f)], side[f][:], ACT.Copy).then_inc(x2T_copied, 1)
                elif n in (1, 2):
                    f = n - 1
                    act.wait_ge(dt_raw, 2 * b + f + 1)
                    act.activation(mag[:, half(f)], side[f][:], ACT.Abs, bias=b_dt[:]).then_inc(mag_done, 1)
                    if f:
                        act.wait_ge(mag_done, 2 * b + 2)
                        act.activation(soft[:], mag[:], ACT.Exp, scale=-1.0).then_inc(soft_exp, 1)
                        act.wait_ge(soft_exp, b + 1)
                        act.activation(mag[:], soft[:], ACT.Ln, bias=1.0).then_inc(soft_ln, 1)
                elif n in (5, 6):
                    f = n - 5
                    act.wait_ge(bc_raw, 2 * b + f + 1)
                    wait(act, bc_step, 4 * b)
                    act.activation(bc32[:, half(f)], side[f][0:K3, :], ACT.Identity,
                                   bias=b_bc[:]).then_inc(bc_high, 1)
                    act.activation(slot(bc, b)[:, half(f)], side[f][0:K3, :], ACT.Identity,
                                   bias=b_bc[:]).then_inc(bc_high, 1)
                elif n == 9:
                    act.wait_ge(z_raw, 2 * b + 2)
                    wait(act, yz_ready, 2 * (b - 1))
                    settle(act, act_settled)
                    for f in range(2):
                        act.activation(slot(z, b)[:, half(f)], side[f][:], ACT.Sigmoid).then_inc(z_ready, 1)
                    act.preload_act_table_set("natural_log_exp_and_others")

            def finish(b, n):
                if n == 7:
                    for f in range(2):
                        act.wait_ge(yzT_ready, 2 * b + f + 1)
                        wait(act, out_ready, 2 * b)
                        act.activation(yzT[:, half(f)], side[f][:], ACT.Copy).then_inc(yzT_copied, 1)

            def iteration(i, scan, done, more):
                for n in range(N):
                    if scan and (more or n + 3 < N):
                        copy_b(i, n + 3)
                    if scan and (more or n + 2 < N):
                        decay(i, n + 2)
                    if more:
                        prepare(i + 1, n)
                    if done:
                        finish(i - 1, n)

            act.preload_act_table_set("natural_log_exp_and_others")
            act.wait_ge(weights_in, 16 * len(weights))
            act.activation(a_pos[:], a_log[:], ACT.Exp).then_inc(a_made, 1)
            for n in range(N):
                prepare(0, n)
            act.wait_ge(a_made, 2)
            for n in range(3):
                copy_b(0, n)
                if n < 2:
                    decay(0, n)
            iteration(0, True, False, True)
            iteration(1, True, True, True)
            with act.Fori(2, BATCH - 1) as i:
                iteration(i, True, True, True)
            iteration(BATCH - 1, True, True, False)
            iteration(BATCH, False, True, False)

        @block.vector
        def _(dve):
            def scan_state(i, n):
                b, k = at(i, n)
                g = step_count(b, k)
                dve.wait_ge(a_ready, g + 1)
                dve.wait_ge(xb_ready, g + 1)
                wait(dve, hc_ready, 2 * (g - 3))
                dve.tensor_tensor_scan(h[:, n % 4, :], a[:, n % 2, :], xb[:, n % 2, :], 0.0, ALU.mult,
                                       ALU.add).then_inc(scanned, 1)

            def times_c(i, n):
                g = step_count(i, n)
                dve.wait_ge(scanned, g + 1)
                wait(dve, summed_y, g - 1)
                for f in range(2):
                    dve.wait_ge(c_ready, 2 * g + f + 1)
                    dve.tensor_tensor(hc[:, n % 2, half(f)], h[:, n % 4, half(f)], c_bank[f][:],
                                      ALU.mult).then_inc(hc_ready, 1)

            def prepare(b, n):
                if n in (1, 2):
                    f = n - 1
                    dve.wait_ge(mag_done, 2 * b + f + 1)
                    wait(dve, xb_ready, N * (b - 1))
                    dve.tensor_scalar(slot(dt, b)[:, half(f)], side[f][:], b_dt[:], 0.0, ALU.add,
                                      ALU.max).then_inc(relu_dt, 1)
                elif n == 3:
                    dve.wait_ge(soft_ln, b + 1)
                    dve.wait_ge(relu_dt, 2 * b + 2)
                    dve.tensor_tensor(slot(dt, b), slot(dt, b), mag[:], ALU.add).then_inc(dt_ready, 1)
                    dve.wait_ge(dt_ready, b + 1)
                if n in (3, 4):
                    f = n - 3
                    dve.wait_ge(xs_ready, 2 * b + f + 1)
                    dve.scalar_tensor_tensor(out=slot(u, b)[:, half(f)], in0=side[f][:], scalar=b_x[:],
                                             in1=slot(dt, b)[:, half(f)], op0=ALU.add,
                                             op1=ALU.mult).then_inc(u_ready, 1)
                elif n == 7:
                    dve.wait_ge(bc_high, 4 * b + 4)
                    dve.tensor_tensor(rest[:], bc32[:], slot(bc, b), ALU.subtract).then_inc(bc_step, 1)
                elif n == 8:
                    dve.wait_ge(bc_step, 4 * b + 1)
                    dve.tensor_copy(slot(bc, b)[32:64], rest[32:64]).then_inc(bc_step, 1)
                    dve.tensor_copy(slot(bc, b)[64:96], rest[64:96]).then_inc(bc_step, 1)
                elif n == 9:
                    dve.wait_ge(bc_step, 4 * b + 3)
                    dve.tensor_tensor(slot(bc, b)[64:96], rest[64:96], slot(bc, b)[64:96],
                                      ALU.subtract).then_inc(bc_step, 1)

            def finish(b, n):
                if n == 0:
                    dve.wait_ge(summed_y, N * b + N)
                    dve.wait_ge(z_ready, 2 * b + 2)
                    for f in range(2):
                        dve.tensor_tensor(yz[:, half(f)], y[:, half(f)], slot(z, b)[:, half(f)],
                                          ALU.mult).then_inc(yz_ready, 1)
                elif n in (10, 11):
                    f = n - 10
                    dve.wait_ge(out_ready, 2 * b + f + 1)
                    dve.tensor_tensor(res[:, HC * f:HC * f + HC, :].rearrange("p c d -> p (c d)"), side[f][:],
                                      rows_of(b)[:, HC * f:HC * f + HC, :].rearrange("p c d -> p (c d)"),
                                      ALU.add).then_inc(res_ready, 1)
                elif n == 12:
                    dve.wait_ge(res_ready, 2 * b + 2)
                    for c in range(CH):
                        dve.bn_stats(stats[:, c, :], res[:, c, :]).then_inc(summed, 1)
                elif n == 13:
                    dve.wait_ge(summed, CH * b + CH)
                    settle(dve, dve_settled)
                    for c in range(CH):
                        dve.bn_aggr(mv[:, c, :], stats[:, c, :]).then_inc(mv_ready, 1)
                elif n == 15:
                    dve.wait_ge(rstd_ready, b + 1)
                    for c in range(CH):
                        dve.tensor_scalar(rows_of(b)[:, c, :], res[:, c, :], mv[:, c, 0:1], rstd[:, c:c + 1],
                                          ALU.subtract, ALU.mult).then_inc(x3_ready, 1)

            def iteration(i, scan, done, more):
                for n in range(N):
                    if scan and (more or n + 1 < N):
                        scan_state(i, n + 1)
                    if scan:
                        times_c(i, n)
                    if more:
                        prepare(i + 1, n)
                    if done:
                        finish(i - 1, n)

            dve.memset(ones[:], 1.0).then_inc(consts, 1)
            dve.wait_ge(weights_in, 16 * len(weights))
            for r in range(2):
                dve.tensor_copy(pick[:, N * r:N * r + N, :],
                                pick32[:, N * r:N * r + N].unsqueeze(2).broadcast_to([K3, N, P])).then_inc(consts, 1)
            dve.wait_ge(a_made, 1)
            dve.tensor_scalar(a_neg[:], a_pos[:], -1.0, None, ALU.mult).then_inc(a_made, 1)
            dve.tensor_copy(rows[:], rows32[:]).then_inc(rows_made, 1)
            dve.wait_ge(rows_made, 1)
            dve.tensor_tensor(rows32[:], rows32[:], rows[:], ALU.subtract).then_inc(rows_made, 1)
            dve.wait_ge(rows_made, 2)
            dve.tensor_copy(rows[32:64], rows32[32:64]).then_inc(rows_made, 1)
            dve.tensor_copy(rows[64:96], rows32[64:96]).then_inc(rows_made, 1)
            dve.wait_ge(rows_made, 4)
            dve.tensor_tensor(rows[64:96], rows32[64:96], rows[64:96], ALU.subtract).then_inc(rows_made, 1)
            for n in range(N):
                prepare(0, n)
            scan_state(0, 0)
            iteration(0, True, False, True)
            iteration(1, True, True, True)
            with dve.Fori(2, BATCH - 1) as i:
                iteration(i, True, True, True)
            iteration(BATCH - 1, True, True, False)
            iteration(BATCH, False, True, False)


def ffn_phase(nc, d, keep):
    BLOCKS, LANES, RANK, LINEARS = 3, 4, 32, 6
    ON_ACT = 2
    ON_DVE = HC - ON_ACT
    PAIRS = BATCH // 2
    with ExitStack() as ctx:
        def sb(name, shape, dt=F32):
            return ctx.enter_context(nc.sbuf_tensor(name + "_sb", shape, dt))

        def ps(name, cols):
            return ctx.enter_context(nc.psum_tensor(name, [P, cols], F32))

        def sem(name):
            return ctx.enter_context(nc.semaphore(name))

        ident, x_all = keep["ident"], keep["x_all"]
        q, scale, w = sb("q", [P, LINEARS, P], I32), sb("scale", [P, LINEARS, P]), sb("w", [P, LINEARS, P])
        lora_a, lora_b = sb("lora_a", [RANK, LINEARS, P]), sb("lora_b", [RANK, LINEARS, P])
        gamma, beta = sb("gamma", [P, BLOCKS]), sb("beta", [P, BLOCKS])
        rows32 = sb("f_rows32", [96, LINEARS, P])
        rows, ones = sb("f_rows", [96, LINEARS, P], BF16), sb("f_ones", [96, P], BF16)
        minus_half = sb("f_minus_half", [P, HC])

        def lanes(name, *shape):
            return [sb(f"{name}{n}", [P, *shape]) for n in range(LANES)]

        h_in, h_a, h_b, hx = lanes("h_in", HC, P), lanes("h_a", HC, P), lanes("h_b", HC, P), lanes("hx", HC, P)
        hT, yn, gT = lanes("hT", HALF), lanes("yn", HC, P), lanes("gT", HALF)
        fin, out = lanes("fin", HC, P), lanes("out", HC, P)
        stats, mv = lanes("f_stats", HC, 6), lanes("f_mv", HC, 2)
        var_eps, rstd = lanes("f_var_eps", HC), lanes("f_rstd", HC)
        shift = lanes("f_shift", ON_ACT)
        stats2, mv2 = lanes("g_stats", HC, 6), lanes("g_mv", HC, 2)
        var_eps2, rstd2 = lanes("g_var_eps", HC), lanes("g_rstd", HC)
        turn = [ps(f"f_turn{n}", HALF) for n in range(LANES)]
        lin = [ps(f"lin{n}", HALF) for n in range(LANES)]

        weights_in = sem("weights_in3")
        pool_settled, dve_settled = sem("f_pool_settled"), sem("f_dve_settled")
        act_settled = sem("f_act_settled")
        rows_clear = sem("f_rows_clear")
        pool_const = sem("f_pool_const")
        consts = sem("f_consts")
        dequant = sem("dequant")
        lora = sem("lora")
        rows_made = sem("f_rows_made")
        h_loaded = sem("h_loaded")
        hT_ready = sem("hT_ready")
        hT_copied = sem("hT_copied")
        lin0_ready = sem("lin0_ready")
        summed = sem("f_summed")
        mv_ready = sem("f_mv_ready")
        veps_ready = sem("f_veps_ready")
        rstd_ready = sem("f_rstd_ready")
        shift_part = sem("f_shift_part")
        normed = sem("normed")
        act_normed = sem("act_normed")
        ynT_ready = sem("ynT_ready")
        gelu_done = sem("gelu_done")
        lin1_ready = sem("lin1_ready")
        res_ready = sem("f_res_ready")
        hx_ready = sem("hx_ready")
        summed2 = sem("g_summed")
        mv2_ready = sem("g_mv_ready")
        veps2_ready = sem("g_veps_ready")
        rstd2_ready = sem("g_rstd_ready")
        out_ready = sem("f_out_ready")
        stored = sem("stored")
        block = ctx.enter_context(nc.Block())

        def batches(j):
            if isinstance(j, int):
                return x_all[:, 2 * j:2 * j + 2]
            return x_all[:, bass.ds(2 * j, 2)]

        def lane_rows(j, n):
            return batches(j)[:, n // 2, HC * (n % 2):HC * (n % 2) + HC, :]

        TURNS = BLOCKS * LANES

        def turn_at(j, s, lag, first):
            if s >= lag:
                return j, (s - lag) // LANES, (s - lag) % LANES
            return None if first else (j - 1, (s - lag + TURNS) // LANES, (s - lag) % LANES)

        LAST_SUMS = {0: 0, 3: 1, 6: 2, 9: 3}
        LAST_NORMS = {2: 0, 5: 1, 8: 2, 11: 3}

        def count(j, k, n):
            return TURNS * j + LANES * k + n + 1

        weights = [(q[:], d["q"]), (scale[:], d["scale"]), (lora_a[:], d["lora_a"]), (lora_b[:], d["lora_b"]),
                   (gamma[:], d["gamma"]), (beta[:], d["beta"])] + [
                       (rows32[32 * r:32 * r + 1], d["biases"]) for r in range(3)]
        out_dram = d["out"].rearrange("(j e) (f c p) d -> j e f p c d", e=2, f=2, p=P)

        @block.sync
        def _(sp):
            def load(j):
                for n in range(LANES):
                    sp.dma_start(h_in[n][:], lane_rows(j, n)).then_inc(h_loaded, 16)

            load(0)
            sp.wait_ge(rows_clear, 1)
            for dst, src in weights:
                sp.dma_start(dst, src).then_inc(weights_in, 16)

            def store(j, n):
                sp.wait_ge(out_ready, HC * (LANES * j + n + 1))
                dst = out_dram[j:j + 1] if isinstance(j, int) else out_dram[bass.ds(j, 1)]
                sp.dma_start(dst[:, n // 2, n % 2].rearrange("j p c d -> (j p) c d"), out[n][:]).then_inc(stored, 16)

            def pair(j, more):
                for n in range(LANES):
                    store(j - 1, n)
                    if more and n == 1:
                        sp.wait_ge(res_ready, count(j, 0, LANES - 1))
                        load(j + 1)

            sp.wait_ge(res_ready, count(0, 0, LANES - 1))
            load(1)
            with sp.Fori(1, PAIRS - 1) as j:
                pair(j, True)
            pair(PAIRS - 1, False)
            for n in range(LANES):
                store(PAIRS - 1, n)
            sp.wait_ge(stored, 16 * LANES * PAIRS)

        @block.gpsimd
        def _(pool):
            pool.memset(rows32[:], 0.0).then_inc(rows_clear, 1)
            pool.memset(minus_half[:], -0.5).then_inc(pool_const, 1)
            pool.wait_ge(pool_const, 1)

            def inverse_std(j, k, n):
                c = count(j, k, n)
                pool.wait_ge(mv_ready, HC * c)
                settle(pool, pool_settled)
                pool.tensor_scalar(var_eps[n][:], mv[n][:, :, 1], 1.0, EPS, ALU.mult, ALU.add).then_inc(veps_ready, 1)
                pool.wait_ge(veps_ready, c)
                pool.tensor_tensor(rstd[n][:], var_eps[n][:], minus_half[:], ALU.pow).then_inc(rstd_ready, 1)
                pool.wait_ge(rstd_ready, c)
                pool.tensor_tensor(shift[n][:], mv[n][:, ON_DVE:, 0], rstd[n][:, ON_DVE:], ALU.mult).then_inc(shift_part, 1)
                pool.wait_ge(shift_part, 2 * c - 1)
                settle(pool, pool_settled)
                pool.tensor_scalar(shift[n][:], shift[n][:], -1.0, 0.0, ALU.mult, ALU.add).then_inc(shift_part, 1)

            def add_x3(j, n):
                pool.wait_ge(res_ready, count(j, 1, n))
                settle(pool, pool_settled)
                pool.tensor_tensor(hx[n][:], h_b[n][:], lane_rows(j, n), ALU.add).then_inc(hx_ready, 1)

            def inverse_std2(j, n):
                c = LANES * j + n + 1
                pool.wait_ge(mv2_ready, HC * c)
                settle(pool, pool_settled)
                pool.tensor_scalar(var_eps2[n][:], mv2[n][:, :, 1], 1.0, EPS, ALU.mult,
                                   ALU.add).then_inc(veps2_ready, 1)
                pool.wait_ge(veps2_ready, c)
                pool.tensor_tensor(rstd2[n][:], var_eps2[n][:], minus_half[:], ALU.pow).then_inc(rstd2_ready, 1)

            def pair(j, first):
                for s in range(TURNS):
                    turn1 = turn_at(j, s, 1, first)
                    if turn1:
                        inverse_std(*turn1)
                    turn4 = turn_at(j, s, 4, first)
                    if turn4 and turn4[1] == 1:
                        add_x3(turn4[0], turn4[2])
                    if not first and s in LAST_SUMS:
                        inverse_std2(j - 1, LAST_SUMS[s])

            pair(0, True)
            with pool.Fori(1, PAIRS) as j:
                pair(j, False)
            inverse_std(PAIRS - 1, BLOCKS - 1, LANES - 1)
            for n in range(LANES):
                inverse_std2(PAIRS - 1, n)

        @block.tensor
        def _(pe):
            def linear(n, src, i):
                for c in range(HC):
                    mm = pe.matmul(lin[n][:, chunk(c)], src[n][:, chunk(c)], w[:, i, :], start=False, stop=c == HC - 1,
                                   skip_group_check=True)
                return mm

            def bias(n, i):
                pe.matmul(lin[n][:], ones[:], rows[:, i, :].unsqueeze(1).broadcast_to([96, HC, P]), start=True,
                          stop=False, skip_group_check=True)

            def turn_normed(j, k, n):
                pe.wait_ge(normed, ON_DVE * count(j, k, n))
                pe.wait_ge(act_normed, ON_ACT * count(j, k, n))
                for c in range(HC):
                    mm = pe.transpose(turn[n][:, chunk(c)], yn[n][:, c, :], ident[:])
                mm.then_inc(ynT_ready, 1)

            def turn_h(j, k, n):
                if k:
                    pe.wait_ge(res_ready, count(j, k - 1, n))
                else:
                    pe.wait_ge(h_loaded, 16 * LANES * (j + 1))
                for c in range(HC):
                    mm = pe.transpose(turn[n][:, chunk(c)], (h_in, h_a, h_b)[k][n][:, c, :], ident[:])
                mm.then_inc(hT_ready, 1)

            def second_bias(j, k, n):
                bias(n, 2 * k + 1)

            def first_bias(j, k, n):
                wait(pe, res_ready, count(j, k - 1, n))
                bias(n, 2 * k)

            def second_linear(j, k, n):
                pe.wait_ge(gelu_done, count(j, k, n))
                linear(n, gT, 2 * k + 1).then_inc(lin1_ready, 1)

            def first_linear(j, k, n):
                pe.wait_ge(hT_copied, count(j, k, n))
                linear(n, hT, 2 * k).then_inc(lin0_ready, 1)

            def pair(j, first):
                for s in range(TURNS):
                    turn0, turn3 = turn_at(j, s, 0, first), turn_at(j, s, 3, first)
                    if turn3:
                        turn_normed(*turn3)
                    turn_h(*turn0)
                    if turn3:
                        second_bias(*turn3)
                    first_bias(*turn0)
                    if turn3:
                        second_linear(*turn3)
                    first_linear(*turn0)

            pe.wait_ge(weights_in, 16 * len(weights))
            for i in range(LINEARS):
                mm = pe.matmul(turn[i // HC][:, chunk(i % HC)], lora_a[:, i, :], lora_b[:, i, :], start=True, stop=True)
                if i in (HC - 1, LINEARS - 1):
                    mm.then_inc(lora, 1)
            pe.wait_ge(consts, 1)
            pe.wait_ge(rows_made, 5)
            pe.wait_ge(dequant, 4)
            pair(0, True)
            with pe.Fori(1, PAIRS) as j:
                pair(j, False)
            for n in range(1, LANES):
                turn_normed(PAIRS - 1, BLOCKS - 1, n)
                second_bias(PAIRS - 1, BLOCKS - 1, n)
                second_linear(PAIRS - 1, BLOCKS - 1, n)

        @block.scalar
        def _(act):
            def activate(j, k, n):
                act.wait_ge(ynT_ready, count(j, k, n))
                act.activation(gT[n][:], turn[n][:], ACT.Gelu, bias=beta[:, k:k + 1],
                               scale=gamma[:, k:k + 1]).then_inc(gelu_done, 1)

            def normalise(j, k, n):
                act.wait_ge(shift_part, 2 * count(j, k, n))
                act.wait_ge(normed, ON_DVE * count(j, k, n))
                settle(act, act_settled)
                for s in range(ON_DVE, HC):
                    act.activation(yn[n][:, s, :], lin[n][:, chunk(s)], ACT.Identity,
                                   bias=shift[n][:, s - ON_DVE:s - ON_DVE + 1],
                                   scale=rstd[n][:, s:s + 1]).then_inc(act_normed, 1)

            def copy_h(j, k, n):
                act.wait_ge(hT_ready, count(j, k, n))
                act.activation(hT[n][:], turn[n][:], ACT.Copy).then_inc(hT_copied, 1)

            def pair(j, first):
                for s in range(TURNS):
                    turn3 = turn_at(j, s, 3, first)
                    if turn3:
                        activate(*turn3)
                    copy_h(*turn_at(j, s, 0, first))
                    turn2 = turn_at(j, s, 2, first)
                    if turn2:
                        normalise(*turn2)

            act.preload_act_table_set("gelu_and_others")
            act.wait_ge(weights_in, 16 * len(weights))
            pair(0, True)
            with act.Fori(1, PAIRS) as j:
                pair(j, False)
            for n in range(1, LANES):
                activate(PAIRS - 1, BLOCKS - 1, n)
                if n < LANES - 1:
                    normalise(PAIRS - 1, BLOCKS - 1, n + 1)

        @block.vector
        def _(dve):
            def flat(x):
                return x[:].rearrange("p c d -> p (c d)")

            def sum_up(j, k, n):
                dve.wait_ge(lin0_ready, count(j, k, n))
                for s in range(HC):
                    dve.bn_stats(stats[n][:, s, :], lin[n][:, chunk(s)]).then_inc(summed, 1)

            def aggregate(c, sums, done, out, ready):
                dve.wait_ge(done, HC * c)
                settle(dve, dve_settled)
                for s in range(HC):
                    dve.bn_aggr(out[:, s, :], sums[:, s, :]).then_inc(ready, 1)

            def normalise(j, k, n):
                dve.wait_ge(rstd_ready, count(j, k, n))
                for s in range(ON_DVE):
                    dve.tensor_scalar(yn[n][:, s, :], lin[n][:, chunk(s)], mv[n][:, s, 0:1], rstd[n][:, s:s + 1],
                                      ALU.subtract, ALU.mult).then_inc(normed, 1)

            def add_h(j, k, n):
                dve.wait_ge(lin1_ready, count(j, k, n))
                if k == 1:
                    wait(dve, hx_ready, LANES * (j - 1) + n + 1)
                if k == 2:
                    dve.wait_ge(hx_ready, LANES * j + n + 1)
                dve.tensor_tensor(flat((h_a, h_b, fin)[k][n]), lin[n][:], flat((h_in, h_a, hx)[k][n]),
                                  ALU.add).then_inc(res_ready, 1)

            def last_statistics(j, n):
                dve.wait_ge(res_ready, count(j, BLOCKS - 1, n))
                for s in range(HC):
                    dve.bn_stats(stats2[n][:, s, :], fin[n][:, s, :]).then_inc(summed2, 1)
                aggregate(LANES * j + n + 1, stats2[n], summed2, mv2[n], mv2_ready)

            def last_normalise(j, n):
                dve.wait_ge(rstd2_ready, LANES * j + n + 1)
                wait(dve, stored, 16 * LANES * j)
                for s in range(HC):
                    dve.tensor_scalar(out[n][:, s, :], fin[n][:, s, :], mv2[n][:, s, 0:1], rstd2[n][:, s:s + 1],
                                      ALU.subtract, ALU.mult).then_inc(out_ready, 1)

            def pair(j, first):
                for s in range(TURNS):
                    turn1, turn2, turn4 = (turn_at(j, s, lag, first) for lag in (1, 2, 4))
                    if turn4:
                        add_h(*turn4)
                    if turn1:
                        sum_up(*turn1)
                    if not first and s in LAST_NORMS:
                        last_normalise(j - 1, LAST_NORMS[s])
                    if turn1:
                        aggregate(count(*turn1), stats[turn1[2]], summed, mv[turn1[2]], mv_ready)
                    if turn2:
                        normalise(*turn2)
                    if not first and s in LAST_SUMS:
                        last_statistics(j - 1, LAST_SUMS[s])

            dve.memset(ones[:], 1.0).then_inc(consts, 1)
            dve.wait_ge(weights_in, 16 * len(weights))
            dve.tensor_scalar(w[:], q[:], 1.0 / 7.5, -1.0, ALU.mult, ALU.add).then_inc(dequant, 1)
            dve.wait_ge(dequant, 1)
            dve.tensor_tensor(w[:], w[:], scale[:], ALU.mult).then_inc(dequant, 1)
            dve.wait_ge(dequant, 2)
            for r, cols in enumerate((slice(0, HC), slice(HC, LINEARS))):
                dve.wait_ge(lora, r + 1)
                size = (cols.stop - cols.start) * P
                dve.tensor_tensor(w[:, cols, :].rearrange("p c d -> p (c d)"), turn[r][:, 0:size],
                                  w[:, cols, :].rearrange("p c d -> p (c d)"), ALU.add).then_inc(dequant, 1)
            dve.tensor_copy(rows[:], rows32[:]).then_inc(rows_made, 1)
            dve.wait_ge(rows_made, 1)
            dve.tensor_tensor(rows32[:], rows32[:], rows[:], ALU.subtract).then_inc(rows_made, 1)
            dve.wait_ge(rows_made, 2)
            dve.tensor_copy(rows[32:64], rows32[32:64]).then_inc(rows_made, 1)
            dve.tensor_copy(rows[64:96], rows32[64:96]).then_inc(rows_made, 1)
            dve.wait_ge(rows_made, 4)
            dve.tensor_tensor(rows[64:96], rows32[64:96], rows[64:96], ALU.subtract).then_inc(rows_made, 1)
            pair(0, True)
            with dve.Fori(1, PAIRS) as j:
                pair(j, False)
            for n in range(LANES):
                add_h(PAIRS - 1, BLOCKS - 1, n)
                if n == 0:
                    sum_up(PAIRS - 1, BLOCKS - 1, LANES - 1)
                    aggregate(PAIRS * TURNS, stats[LANES - 1], summed, mv[LANES - 1], mv_ready)
                if n < 2:
                    normalise(PAIRS - 1, BLOCKS - 1, LANES - 2 + n)
                last_statistics(PAIRS - 1, n)
                if n:
                    last_normalise(PAIRS - 1, n - 1)
            last_normalise(PAIRS - 1, LANES - 1)


def build(nc, d):
    with ExitStack() as ctx:
        keep = {
            "ident": ctx.enter_context(nc.sbuf_tensor("ident_sb", [P, P], F32)),
            "x_all": ctx.enter_context(nc.sbuf_tensor("x_all", [P, BATCH, CH, P], F32)),
        }
        attention_phase(nc, d, keep)
        ssm_phase(nc, d, keep)
        ffn_phase(nc, d, keep)


def lay_out(np, inputs):
    tr = np.ascontiguousarray
    w = inputs["L0_attn_W"]
    return {
        "L0_attn_x": tr(inputs["L0_attn_x"]),
        "ident": np.eye(P, dtype=np.float32),
        "mask": np.triu(np.full((P, P), MASKED, np.float32), 1),
        "w_key": tr(w[:P].T), "w_val": tr(w[P:].T),
        "w_r": tr(inputs["L0_ffn_W_r"].T), "w_k": tr(inputs["L0_ffn_W_k"].T), "w_v": tr(inputs["L0_ffn_W_v"].T),
        "w_dt": tr(inputs["L1_attn_Wdt"]), "w_x": tr(inputs["L1_attn_Wx"]), "w_z": tr(inputs["L1_attn_Wz"]),
        "w_out": tr(inputs["L1_attn_Wout"]),
        "w_bc": tr(np.concatenate([inputs["L1_attn_WB"], inputs["L1_attn_WC"]] * 3, 1)),
        "b_bc": tr(np.concatenate([inputs["L1_attn_bB"], inputs["L1_attn_bC"]] * 3)[:, None]),
        "b_dt": tr(inputs["L1_attn_bdt"][:, None]), "b_x": tr(inputs["L1_attn_bx"][:, None]),
        "a_log": tr(inputs["L1_attn_A_log"]),
        "pick": np.concatenate([np.eye(2 * N, dtype=np.float32)] * 3),
        "rows": tr(np.stack([inputs["L1_attn_bz"], inputs["L1_attn_bout"]])[None]),
        "q": tr(inputs["L1_ffn_qweights"].transpose(2, 0, 1)),
        "scale": tr(np.repeat(inputs["L1_ffn_scales"], P // inputs["L1_ffn_scales"].shape[2], axis=2).transpose(2, 0, 1)),
        "lora_a": tr(inputs["L1_ffn_lora_a"].transpose(1, 0, 2)),
        "lora_b": tr(inputs["L1_ffn_lora_b"].transpose(2, 0, 1)),
        "biases": tr(inputs["L1_ffn_biases"][None]),
        "gamma": tr(inputs["L1_ffn_ln_gamma"].T), "beta": tr(inputs["L1_ffn_ln_beta"].T),
        "mu": tr(np.stack([inputs["L0_ffn_mu_r"], inputs["L0_ffn_mu_k"]], 1)),
    }


def kernel(**inputs):
    import numpy as np
    import concourse.bacc as bacc
    from concourse.bass_utils import run_bass_kernel_spmd

    nc = bacc.Bacc("TRN2", target_bir_lowering=False, num_devices=1)
    arrays = lay_out(np, {name: np.asarray(a) for name, a in inputs.items()})
    dram = {name: nc.dram_tensor(name, a.shape, mybir.dt.from_np(a.dtype), kind="ExternalInput").ap()
            for name, a in arrays.items()}
    dram["out"] = nc.dram_tensor("out", (BATCH, T, P), F32, kind="ExternalOutput").ap()
    build(nc, dram)
    r = run_bass_kernel_spmd(nc, [arrays], core_ids=[0])
    return r.results[0]["out"]
```

```python
from contextlib import ExitStack

import concourse.bass as bass
from concourse import mybir

F32 = mybir.dt.float32
BF16 = mybir.dt.bfloat16
I32 = mybir.dt.int32
ALU = mybir.AluOpType
ACT = mybir.ActivationFunctionType
AX = mybir.AxisListType

P = 128
BATCH = 8
T = 1024
CH = T // P
HALF = 512
HC = HALF // P
N = 16
EPS = 1e-5
MASKED = -1e30


def wait(eng, sem, value):
    if not (isinstance(value, int) and value <= 0):
        eng.wait_ge(sem, value)


def settle(eng, settled):
    eng.sem_inc(settled, 1)


def chunk(c):
    return slice(c * P, (c + 1) * P)


def rows_of(x, b):
    if isinstance(b, int):
        return x[:, b]
    return x[:, bass.ds(b, 1)].rearrange("p b c d -> p (b c) d")


def half(h):
    return slice(h * HALF, (h + 1) * HALF)


def groups(q):
    first = q if q < HC else HC + 2 * (q - HC)
    return [(first + g, g * HC, min(HC, q + 1 - g * HC)) for g in range(1 + (q >= HC))]


EARLY = {3: (0,), 6: (3,)}
LATE = {3: (1,), 5: (2,), 6: (4,), 7: (5,), 8: (6,), 9: (7,)}
PIECES = {0: (4, 5, 6), 1: (7, 8), 2: (9,), 4: (10,), 5: (11, 12), 7: (13, 14)}
ACT_PIECES = {0: (4, 6), 1: (7, 8), 2: (9,), 4: (10,), 8: (14,)}
DVE_PIECES = {2: (10,), 6: (12,)}
THIRDS = (range(0, 3), range(3, 6), range(6, 8))
GROUPS = groups(CH - 1)[-1][0] + 1


BLOCKS, RANK, LINEARS = 3, 32, 6
K3 = 3 * 2 * N


def keep_on_chip(nc, ctx):
    def sb(name, shape, dt=F32):
        return ctx.enter_context(nc.sbuf_tensor(name + "_sb", shape, dt))

    keep = {"ident": sb("ident", [P, P]), "x_all": sb("x_all", [P, BATCH, CH, P])}
    for name in ("w_dt", "w_x", "w_z", "w_out"):
        keep[name] = sb(name, [P, P])
    keep.update(
        w_bc=sb("w_bc", [P, K3]), b_bc=sb("b_bc", [K3, 1]), b_dt=sb("b_dt", [P, 1]), b_x=sb("b_x", [P, 1]),
        a_neg=sb("a_neg", [P, N]),
        pick=sb("pick", [K3, 2 * N, P], BF16),
        minus_one=sb("minus_one", [K3, 2, K3], BF16),
        rows=sb("rows", [K3, 2, P], BF16), ones=sb("ones", [96, P], BF16))
    keep.update(
        w=sb("w", [P, LINEARS, P]), gamma=sb("gamma", [P, BLOCKS]), beta=sb("beta", [P, BLOCKS]),
        f_rows=sb("f_rows", [96, LINEARS, P], BF16))
    keep["mixed"] = sb("mixed", [P, CH, P])
    keep["projections"] = Projections(nc, ctx, keep)
    return keep


def project(pe, out, f, xT, w, bias, ones):
    pe.matmul(out[:, half(f)], ones[:], bias.unsqueeze(1).broadcast_to([K3, HC, P]), start=True, stop=False,
              skip_group_check=True)
    for c in range(HC * f, HC * f + HC):
        mm = pe.matmul(out[:, chunk(c)], xT[:, chunk(c)], w[:], start=False, stop=c % HC == HC - 1,
                       skip_group_check=True)
    return mm


def turn_tokens(pe, out, x, ident):
    for c in range(CH):
        mm = pe.transpose(out[:, chunk(c)], x[:, chunk(c)], ident[:])
    return mm


class Projections:

    def __init__(self, nc, ctx, keep):
        def sb(name, shape, dt=F32):
            return ctx.enter_context(nc.sbuf_tensor(name + "_sb", shape, dt))

        def sem(name):
            return ctx.enter_context(nc.semaphore(name))

        self.keep = keep
        self.x2T, self.mag, self.soft = sb("x2T", [P, T]), sb("mag", [P, T]), sb("soft", [P, T])
        self.dt, self.u, self.z = sb("dt", [P, 2, T]), sb("u", [P, 2, T]), sb("z", [P, 2, T])
        self.bc = sb("bc", [K3, 2, T], BF16)
        self.x2T_ready = sem("x2T_ready")
        self.x2T_copied = sem("x2T_copied")
        self.dt_raw = sem("dt_raw")
        self.mag_done = sem("mag_done")
        self.soft_exp = sem("soft_exp")
        self.soft_ln = sem("soft_ln")
        self.dt_ready = sem("dt_ready")
        self.bc_raw = sem("bc_raw")
        self.bc_part = sem("bc_part")
        self.xs_ready = sem("xs_ready")
        self.u_ready = sem("u_ready")
        self.z_raw = sem("z_raw")
        self.z_ready = sem("z_ready")
        self.a_ready = sem("a_ready")
        self.xb_ready = sem("xb_ready")
        self.yz_ready = sem("yz_ready")

    @staticmethod
    def slot(buf, b):
        if isinstance(b, int):
            return buf[:, b % 2]
        return buf[:, bass.ds(b % 2, 1)].rearrange("p b t -> p (b t)")

    def on_tensor(self, pe, side, x2, b, n):
        keep = self.keep
        if n == 4:
            turn_tokens(pe, side, x2.rearrange("p c d -> p (c d)"), keep["ident"]).then_inc(self.x2T_ready, 1)
        elif n in (5, 6):
            f = n - 5
            if f == 0:
                pe.wait_ge(self.x2T_copied, b + 1)
            mm = pe.matmul(side[:, half(f)], keep["w_dt"][:], self.x2T[:, half(f)], start=True, stop=True)
            if f:
                mm.then_inc(self.dt_raw, 1)
        elif n in (7, 8):
            f = n - 7
            if f == 0:
                pe.wait_ge(self.mag_done, 2 * b + 2)
            mm = pe.matmul(side[0:K3, half(f)], keep["w_bc"][:], self.x2T[:, half(f)], start=True, stop=False,
                           skip_group_check=True)
            if f:
                mm.then_inc(self.bc_raw, 1)
        elif n in (9, 10):
            pe.wait_ge(self.bc_part, 3 * b + n - 8)
            for f in range(2):
                mm = pe.matmul(side[0:K3, half(f)], keep["minus_one"][:, n - 9, :], self.slot(self.bc, b)[:, half(f)],
                               start=False, stop=n == 10, skip_group_check=True)
            mm.then_inc(self.bc_raw, 1)
        elif n in (11, 12):
            f = n - 11
            if f == 0:
                pe.wait_ge(self.bc_part, 3 * b + 3)
            mm = pe.matmul(side[:, half(f)], keep["w_x"][:], self.x2T[:, half(f)], start=True, stop=True)
            if f:
                mm.then_inc(self.xs_ready, 1)
        elif n in (13, 14):
            f = n - 13
            if f == 0:
                pe.wait_ge(self.u_ready, b + 1)
            mm = project(pe, side, f, self.x2T, keep["w_z"], keep["rows"][:, 0, :], keep["ones"])
            if f:
                mm.then_inc(self.z_raw, 1)

    def on_scalar(self, act, settled, side, b, n):
        keep = self.keep
        if n == 4:
            act.wait_ge(self.x2T_ready, b + 1)
            wait(act, self.z_raw, b)
            act.activation(self.x2T[:], side[:], ACT.Copy).then_inc(self.x2T_copied, 1)
        elif n == 6:
            act.wait_ge(self.dt_raw, b + 1)
            act.activation(self.mag[:], side[:], ACT.Abs, bias=keep["b_dt"][:]).then_inc(self.mag_done, 1)
            wait(act, self.a_ready, N * (b - 1))
            settle(act, settled)
            act.activation(self.slot(self.dt, b), side[:], ACT.Relu, bias=keep["b_dt"][:]).then_inc(self.mag_done, 1)
        elif n == 7:
            act.wait_ge(self.mag_done, 2 * b + 2)
            act.activation(self.soft[:], self.mag[:], ACT.Exp, scale=-1.0).then_inc(self.soft_exp, 1)
        if n == 8:
            act.wait_ge(self.bc_raw, 3 * b + 1)
            settle(act, settled)
            act.activation(self.slot(self.bc, b), side[0:K3, :], ACT.Identity,
                           bias=keep["b_bc"][:]).then_inc(self.bc_part, 1)
            act.wait_ge(self.soft_exp, b + 1)
            act.activation(self.mag[:], self.soft[:], ACT.Ln, bias=1.0).then_inc(self.soft_ln, 1)
        elif n == 9:
            act.wait_ge(self.bc_raw, 3 * b + 2)
            settle(act, settled)
            act.activation(self.slot(self.bc, b)[0:64], side[0:64, :], ACT.Identity,
                           bias=keep["b_bc"][0:64]).then_inc(self.bc_part, 1)
        elif n == 10:
            act.wait_ge(self.bc_raw, 3 * b + 3)
            settle(act, settled)
            act.activation(self.slot(self.bc, b)[0:32], side[0:32, :], ACT.Identity,
                           bias=keep["b_bc"][0:32]).then_inc(self.bc_part, 1)
        elif n == 14:
            act.wait_ge(self.z_raw, b + 1)
            wait(act, self.yz_ready, b - 1)
            settle(act, settled)
            act.activation(self.slot(self.z, b), side[:], ACT.Sigmoid).then_inc(self.z_ready, 1)
            act.preload_act_table_set("natural_log_exp_and_others")

    def on_vector(self, dve, side, b, n):
        keep = self.keep
        if n == 10:
            dve.wait_ge(self.soft_ln, b + 1)
            dve.wait_ge(self.mag_done, 2 * b + 2)
            dve.tensor_tensor(self.slot(self.dt, b), self.slot(self.dt, b), self.mag[:],
                              ALU.add).then_inc(self.dt_ready, 1)
        elif n == 12:
            dve.wait_ge(self.dt_ready, b + 1)
            dve.wait_ge(self.xs_ready, b + 1)
            wait(dve, self.xb_ready, N * (b - 1))
            dve.scalar_tensor_tensor(out=self.slot(self.u, b), in0=side[:], scalar=keep["b_x"][:],
                                     in1=self.slot(self.dt, b), op0=ALU.add, op1=ALU.mult).then_inc(self.u_ready, 1)


class Output:

    def __init__(self, nc, ctx, keep):
        def sb(name, shape, dt=F32):
            return ctx.enter_context(nc.sbuf_tensor(name + "_sb", shape, dt))

        def sem(name):
            return ctx.enter_context(nc.semaphore(name))

        self.keep = keep
        self.y = ctx.enter_context(nc.psum_tensor("y", [P, T], F32))
        self.side = ctx.enter_context(nc.psum_tensor("side", [P, T], F32))
        self.yz, self.yzT, self.res = sb("yz", [P, T]), sb("yzT", [P, T]), sb("res", [P, CH, P])
        self.stats, self.mv = sb("s_stats", [P, CH, 6]), sb("s_mv", [P, CH, 2])
        self.var_eps, self.rstd = sb("s_var_eps", [P, CH]), sb("s_rstd", [P, CH])
        self.minus_half = sb("s_minus_half", [P, CH])
        self.summed_y = sem("summed_y")
        self.yz_ready = keep["projections"].yz_ready
        self.yzT_ready = sem("yzT_ready")
        self.yzT_copied = sem("yzT_copied")
        self.out_ready = sem("out_ready")
        self.res_ready = sem("res_ready")
        self.summed = sem("s_summed")
        self.mv_ready = sem("s_mv_ready")
        self.veps_ready = sem("s_veps_ready")
        self.rstd_ready = sem("s_rstd_ready")
        self.x3_ready = sem("x3_ready")

    def on_tensor(self, pe, b, n):
        keep, side = self.keep, self.side
        if n == 1:
            pe.wait_ge(self.yz_ready, b + 1)
            last = isinstance(b, int) and b == BATCH - 1
            pe.wait_ge(keep["projections"].z_ready, b + (1 if last else 2))
            turn_tokens(pe, side, self.yz, keep["ident"]).then_inc(self.yzT_ready, 1)
        elif n in (2, 3):
            f = n - 2
            if f == 0:
                pe.wait_ge(self.yzT_copied, b + 1)
            mm = project(pe, side, f, self.yzT, keep["w_out"], keep["rows"][:, 1, :], keep["ones"])
            if f:
                mm.then_inc(self.out_ready, 1)

    def on_scalar(self, act, b, n):
        if n == 1:
            act.wait_ge(self.yzT_ready, b + 1)
            wait(act, self.out_ready, b)
            act.activation(self.yzT[:], self.side[:], ACT.Copy).then_inc(self.yzT_copied, 1)

    def on_vector(self, dve, settled, b, n):
        pr, rows = self.keep["projections"], rows_of(self.keep["x_all"], b)
        if n == 0:
            dve.wait_ge(self.summed_y, N * b + N)
            dve.wait_ge(pr.z_ready, b + 1)
            dve.tensor_tensor(self.yz[:], self.y[:], pr.slot(pr.z, b), ALU.mult).then_inc(self.yz_ready, 1)
        elif n == 4:
            dve.wait_ge(self.out_ready, b + 1)
            dve.tensor_tensor(self.res[:].rearrange("p c d -> p (c d)"), self.side[:],
                              rows.rearrange("p c d -> p (c d)"), ALU.add).then_inc(self.res_ready, 1)
        elif n in (5, 6):
            dve.wait_ge(self.res_ready, b + 1)
            for c in range(HC * (n - 5), HC * (n - 5) + HC):
                dve.bn_stats(self.stats[:, c, :], self.res[:, c, :]).then_inc(self.summed, 1)
        elif n == 7:
            dve.wait_ge(self.summed, CH * b + CH)
            settle(dve, settled)
            for c in range(CH):
                dve.bn_aggr(self.mv[:, c, :], self.stats[:, c, :]).then_inc(self.mv_ready, 1)
        elif n in (11, 13):
            dve.wait_ge(self.rstd_ready, b + 1)
            for c in range(HC * (n == 13), HC * (n == 13) + HC):
                dve.tensor_scalar(rows[:, c, :], self.res[:, c, :], self.mv[:, c, 0:1], self.rstd[:, c:c + 1],
                                  ALU.subtract, ALU.mult).then_inc(self.x3_ready, 1)

    def on_pool(self, pool, settled, b, n):
        if n == 8:
            pool.wait_ge(self.mv_ready, CH * b + CH)
            settle(pool, settled)
            pool.tensor_scalar(self.var_eps[:], self.mv[:, :, 1], 1.0, EPS, ALU.mult, ALU.add).then_inc(self.veps_ready, 1)
            pool.wait_ge(self.veps_ready, b + 1)
            wait(pool, self.x3_ready, CH * b)
            pool.tensor_tensor(self.rstd[:], self.var_eps[:], self.minus_half[:], ALU.pow).then_inc(self.rstd_ready, 1)


def attention_phase(nc, d, keep):
    with ExitStack() as ctx:
        def sb(name, shape, dt=F32):
            return ctx.enter_context(nc.sbuf_tensor(name + "_sb", shape, dt))

        def ps(name, cols):
            return ctx.enter_context(nc.psum_tensor(name, [P, cols], F32))

        def sem(name):
            return ctx.enter_context(nc.semaphore(name))

        ident, x_all, pr = keep["ident"], keep["x_all"], keep["projections"]
        a_log, a_pos, pick32 = sb("a_log", [P, N]), sb("a_pos", [P, N]), sb("pick32", [K3, 2 * N])
        rows32, f_rows32 = sb("rows32", [96, 2, P]), sb("f_rows32", [96, LINEARS, P])
        q, scale = sb("q", [P, LINEARS, P], I32), sb("scale", [P, LINEARS, P])
        lora_a, lora_b = sb("lora_a", [RANK, LINEARS, P]), sb("lora_b", [RANK, LINEARS, P])
        w_key, w_val = sb("w_key", [P, P]), sb("w_val", [P, P])
        w_r, w_k, w_v = sb("w_r", [P, P]), sb("w_k", [P, P]), sb("w_v", [P, P])
        mu = sb("mu", [P, 2])
        mask32, mask, ident16 = sb("mask32", [P, P]), sb("mask", [P, P], BF16), sb("ident16", [P, P], BF16)
        minus_half = sb("a_minus_half", [P, CH])
        xin, xx = sb("xin", [P, CH, P]), sb("xx", [P, CH, P])
        xT, kT, val = sb("xT", [P, T]), sb("kT", [P, T]), sb("val", [P, CH, P])
        probs, probsT = sb("probs", [P, 2, T]), sb("probsT", [P, 2, T])
        negmax, rowsum, rinv = sb("negmax", [P, 2]), sb("rowsum", [P, CH]), sb("rinv", [P, 2])
        att, stats, mv = sb("att", [P, CH, P]), sb("stats", [P, CH, 6]), sb("mv", [P, CH, 2])
        var_eps, rstd, shift = sb("var_eps", [P, CH]), sb("rstd", [P, CH]), sb("shift", [P, CH])
        x1 = sb("x1", [P, CH, P])
        x1T, diff = sb("x1T", [P, 1 + T]), sb("diff", [P, T])
        xk, xr = sb("xk", [P, T]), sb("xr", [P, T])
        relu, kact = sb("relu", [P, T]), sb("kact", [P, T])
        gate, mixed = sb("gate", [P, T]), keep["mixed"]
        stats2, mv2 = sb("stats2", [P, CH, 6]), sb("mv2", [P, CH, 2])
        var_eps2, rstd2 = sb("var_eps2", [P, CH]), sb("rstd2", [P, CH])
        score = [ps("score0", T), ps("score1", T)]
        turn = [ps("turn0", HALF), ps("turn1", HALF)]
        pv, mix = ps("pv", HALF), ps("mix", HALF)

        weights_in = sem("weights_in")
        pool_settled, dve_settled = sem("a_pool_settled"), sem("a_dve_settled")
        minus_made = sem("minus_made")
        act_settled = sem("a_act_settled")
        zero_made = sem("zero_made")
        consts = sem("consts")
        x_in = sem("x_in")
        xx_made = sem("xx_made")
        xT_ready = sem("xT_ready")
        xT_copied = sem("xT_copied")
        k_ready = sem("k_ready")
        k_copied = sem("k_copied")
        v_ready = sem("v_ready")
        v_copied = sem("v_copied")
        scored = sem("scored")
        max_found = sem("max_found")
        exp_done = sem("exp_done")
        turned = sem("turned")
        even_copied = sem("even_copied")
        odd_copied = sem("odd_copied")
        pv_done = sem("pv_done")
        inverted = sem("inverted")
        combined = sem("combined")
        summed = sem("summed")
        mv_ready = sem("mv_ready")
        veps_ready = sem("veps_ready")
        rstd_ready = sem("rstd_ready")
        shift_part = sem("shift_part")
        x1_ready = sem("x1_ready")
        x1T_ready = sem("x1T_ready")
        x1T_copied = sem("x1T_copied")
        diff_ready = sem("diff_ready")
        xk_ready = sem("xk_ready")
        km_ready = sem("km_ready")
        relu_done = sem("relu_done")
        kact_ready = sem("kact_ready")
        r_ready = sem("r_ready")
        gate_ready = sem("gate_ready")
        vm_ready = sem("vm_ready")
        gated = sem("gated")
        mixed_ready = sem("mixed_ready")
        summed2 = sem("summed2")
        mv2_ready = sem("mv2_ready")
        veps2_ready = sem("veps2_ready")
        rstd2_ready = sem("rstd2_ready")
        x2_ready = sem("x2_ready")
        rows_clear = sem("rows_clear")
        later_in = sem("later_in")
        a_made = sem("a_made")
        lora = sem("lora")
        dequant = sem("dequant")
        picks = sem("picks")
        rows_made = sem("rows_made")
        block = ctx.enter_context(nc.Block())

        x_dram = d["L0_attn_x"].rearrange("b (c p) d -> p b c d", p=P)
        weights = [(ident[:], d["ident"]), (w_key[:], d["w_key"]), (w_val[:], d["w_val"]), (mask32[:], d["mask"]),
                   (w_r[:], d["w_r"]), (w_k[:], d["w_k"]), (w_v[:], d["w_v"]), (mu[:], d["mu"])]
        later = [(keep[name][:], d[name]) for name in
                 ("w_dt", "w_x", "w_z", "w_out", "w_bc", "b_bc", "b_dt", "b_x", "gamma", "beta")] + [
                     (a_log[:], d["a_log"]), (pick32[:], d["pick"]), (q[:], d["q"]), (scale[:], d["scale"]),
                     (lora_a[:], d["lora_a"]), (lora_b[:], d["lora_b"])] + [
                         (rows32[32 * r:32 * r + 1], d["rows"]) for r in range(3)] + [
                             (f_rows32[32 * r:32 * r + 1], d["biases"]) for r in range(3)]

        @block.sync
        def _(sp):
            sp.dma_start(xin[:], x_dram[:, 0]).then_inc(x_in, 16)
            for dst, src in weights:
                sp.dma_start(dst, src).then_inc(weights_in, 16)
            sp.wait_ge(rows_clear, 2)
            for dst, src in later:
                sp.dma_start(dst, src).then_inc(later_in, 16)
            with sp.Fori(1, BATCH) as i:
                wait(sp, xT_ready, 2 * i)
                wait(sp, xx_made, i)
                sp.dma_start(xin[:], x_dram[:, bass.ds(i, 1)].rearrange("p b c d -> p (b c) d")).then_inc(x_in, 16)

        @block.gpsimd
        def _(pool):
            pool.memset(minus_half[:], -0.5).then_inc(minus_made, 1)
            pool.memset(x1T[:, 0:1], 0.0).then_inc(zero_made, 1)
            pool.memset(rows32[:], 0.0).then_inc(rows_clear, 1)
            pool.memset(f_rows32[:], 0.0).then_inc(rows_clear, 1)
            pool.wait_ge(minus_made, 1)
            pool.wait_ge(zero_made, 1)

            def double(i):
                pool.wait_ge(x_in, 16 * i + 16)
                wait(pool, combined, CH * i)
                settle(pool, pool_settled)
                pool.tensor_scalar(xx[:], xin[:], 2.0, 0.0, ALU.mult, ALU.add).then_inc(xx_made, 1)

            def take_difference(b):
                pool.wait_ge(x1T_copied, 2 * b + 2)
                wait(pool, xk_ready, 2 * b)
                pool.tensor_tensor(diff[:], x1T[:, 1:1 + T], x1T[:, 0:T], ALU.subtract).then_inc(diff_ready, 1)

            def square(b):
                for h in range(2):
                    pool.wait_ge(relu_done, 2 * b + h + 1)
                    wait(pool, vm_ready, 2 * b)
                    pool.tensor_tensor(kact[:, half(h)], relu[:, half(h)], relu[:, half(h)],
                                       ALU.mult).then_inc(kact_ready, 1)

            def inverse_std(b, mean_var, ready, ve, made, out, done, used):
                pool.wait_ge(ready, CH * b + CH)
                settle(pool, pool_settled)
                pool.tensor_scalar(ve[:], mean_var[:, :, 1], 1.0, EPS, ALU.mult, ALU.add).then_inc(made, 1)
                pool.wait_ge(made, b + 1)
                wait(pool, used, CH * b)
                pool.tensor_tensor(out[:], ve[:], minus_half[:], ALU.pow).then_inc(done, 1)

            def normalise_x1(i):
                pool.wait_ge(rstd_ready, i + 1)
                pool.tensor_tensor(shift[:], mv[:, :, 0], rstd[:], ALU.mult).then_inc(shift_part, 1)
                pool.wait_ge(shift_part, 2 * i + 1)
                settle(pool, pool_settled)
                pool.tensor_scalar(shift[:], shift[:], -1.0, 0.0, ALU.mult, ALU.add).then_inc(shift_part, 1)
                pool.wait_ge(shift_part, 2 * i + 2)
                wait(pool, x1T_ready, 2 * i)
                wait(pool, mixed_ready, 2 * i)
                settle(pool, pool_settled)
                for c in range(CH):
                    pool.tensor_scalar(x1[:, c, :], att[:, c, :], rstd[:, c:c + 1], shift[:, c:c + 1],
                                       ALU.mult, ALU.add).then_inc(x1_ready, 1)

            def inverse_std2(b):
                inverse_std(b, mv2, mv2_ready, var_eps2, veps2_ready, rstd2, rstd2_ready, x2_ready)

            def iteration(i, attend, channel, older):
                if attend:
                    double(i)
                if channel:
                    take_difference(i - 1)
                if older:
                    inverse_std2(i - 2)
                if channel:
                    square(i - 1)
                if attend:
                    inverse_std(i, mv, mv_ready, var_eps, veps_ready, rstd, rstd_ready, x1_ready)
                    normalise_x1(i)

            iteration(0, True, False, False)
            iteration(1, True, True, False)
            with pool.Fori(2, BATCH) as i:
                iteration(i, True, True, True)
            iteration(BATCH, False, True, True)

        @block.tensor
        def _(pe):
            def transpose_x(i):
                pe.wait_ge(x_in, 16 * i + 16)
                for h in range(2):
                    wait(pe, odd_copied if h else even_copied, GROUPS // 2 * i)
                    for c in range(HC):
                        mm = pe.transpose(turn[h][:, chunk(c)], xin[:, HC * h + c, :], ident[:])
                    mm.then_inc(xT_ready, 1)

            def keys_values(i):
                for h in range(2):
                    pe.wait_ge(xT_copied, 2 * i + h + 1)
                    if h == 0:
                        wait(pe, exp_done, CH * i - 1)
                    pe.matmul(score[0][:, half(h)], w_key[:], xT[:, half(h)], start=True, stop=True).then_inc(k_ready, 1)
                wait(pe, exp_done, CH * i)
                for h in range(2):
                    for c in range(HC):
                        mm = pe.matmul(score[1][:, chunk(HC * h + c)], xT[:, chunk(HC * h + c)], w_val[:],
                                       start=True, stop=True)
                    mm.then_inc(v_ready, 1)

            def scores(i, q):
                if q < 2:
                    pe.wait_ge(v_copied if q else k_copied, 2 * i + 2)
                else:
                    pe.wait_ge(exp_done, CH * i + q - 1)
                s = score[q % 2]
                for lo in range(0, q * P, HALF):
                    hi = min(lo + HALF, q * P)
                    pe.matmul(s[:, lo:hi], xT[:, chunk(q)], kT[:, lo:hi], start=True, stop=True)
                pe.matmul(s[:, chunk(q)], xT[:, chunk(q)], kT[:, chunk(q)], start=True, stop=False)
                pe.matmul(s[:, chunk(q)], ident16[:], mask[:], start=False, stop=True).then_inc(scored, 1)

            def transpose_probs(i, q):
                pe.wait_ge(exp_done, CH * i + q + 1)
                for g, first, blocks in groups(q):
                    if g < 2:
                        pe.wait_ge(xT_copied, 2 * i + 2)
                    else:
                        pe.wait_ge(odd_copied if g % 2 else even_copied, GROUPS // 2 * i + g // 2)
                    for k in range(blocks):
                        mm = pe.transpose(turn[g % 2][:, chunk(k)], probs[:, q % 2, chunk(first + k)], ident[:])
                    mm.then_inc(turned, 1)

            def weigh_values(i, q):
                for g, _, _ in groups(q):
                    pe.wait_ge(odd_copied if g % 2 else even_copied, GROUPS // 2 * i + g // 2 + 1)
                wait(pe, combined, CH * i + q)
                for k in range(q + 1):
                    mm = pe.matmul(pv[:, 0:P], probsT[:, q % 2, chunk(k)], val[:, k, :], start=k == 0, stop=k == q)
                mm.then_inc(pv_done, 1)

            def channel_piece(b, n):
                h = n % 2
                if n < 2:
                    if h:
                        pe.wait_ge(x1T_copied, 2 * b + 1)
                    else:
                        pe.wait_ge(x1_ready, CH * b + CH)
                        wait(pe, gated, 2 * b)
                    for c in range(HC):
                        mm = pe.transpose(mix[:, chunk(c)], x1[:, HC * h + c, :], ident[:])
                    mm.then_inc(x1T_ready, 1)
                elif n < 4:
                    pe.wait_ge(xk_ready, 2 * b + 1)
                    if h:
                        pe.wait_ge(relu_done, 2 * b + 1)
                    else:
                        pe.wait_ge(x1T_copied, 2 * b + 2)
                    pe.matmul(mix[:], w_k[:], xk[:, half(h)], start=True, stop=True).then_inc(km_ready, 1)
                elif n < 6:
                    pe.wait_ge(xk_ready, 2 * b + 2)
                    if h:
                        pe.wait_ge(gate_ready, 2 * b + 1)
                    else:
                        pe.wait_ge(relu_done, 2 * b + 2)
                    for c in range(HC):
                        mm = pe.matmul(mix[:, chunk(c)], xr[:, chunk(HC * h + c)], w_r[:], start=True, stop=True)
                    mm.then_inc(r_ready, 1)
                else:
                    pe.wait_ge(kact_ready, 2 * b + h + 1)
                    if h:
                        pe.wait_ge(gated, 2 * b + 1)
                    else:
                        pe.wait_ge(gate_ready, 2 * b + 2)
                    for c in range(HC):
                        mm = pe.matmul(mix[:, chunk(c)], kact[:, chunk(HC * h + c)], w_v[:], start=True, stop=True)
                    mm.then_inc(vm_ready, 1)

            def iteration(i, attend, channel):
                if attend:
                    transpose_x(i)
                    keys_values(i)
                for s in range(CH + 2):
                    if attend and s < CH:
                        scores(i, s)
                    if channel:
                        for n in EARLY.get(s, ()):
                            channel_piece(i - 1, n)
                    if attend and s >= 2:
                        weigh_values(i, s - 2)
                    if attend and 1 <= s <= CH:
                        transpose_probs(i, s - 1)
                    if channel:
                        for n in LATE.get(s, ()):
                            channel_piece(i - 1, n)
                    if not attend:
                        for n in PIECES.get(s, ()):
                            if n == 4:
                                pe.wait_ge(later_in, 16 * len(later))
                                pe.wait_ge(x2_ready, CH)
                                pe.wait_ge(exp_done, CH * BATCH)
                            if n == 9:
                                pe.wait_ge(picks, 4)
                                pe.wait_ge(rows_made, 5)
                            pr.on_tensor(pe, score[1], x_all[:, 0], 0, n)

            pe.wait_ge(weights_in, 16 * len(weights))
            pe.wait_ge(consts, 2)
            iteration(0, True, False)
            iteration(1, True, True)
            with pe.Fori(2, BATCH) as i:
                iteration(i, True, True)
            pe.wait_ge(later_in, 16 * len(later))
            pe.wait_ge(exp_done, CH * BATCH)
            for k in range(LINEARS):
                mm = pe.matmul(score[0][:, chunk(k)], lora_a[:, k, :], lora_b[:, k, :], start=True, stop=True)
            mm.then_inc(lora, 1)
            iteration(BATCH, False, True)

        @block.scalar
        def _(act):
            def channel_piece(b, n):
                h = n % 2
                if n < 2:
                    act.wait_ge(x1T_ready, 2 * b + h + 1)
                    wait(act, xk_ready, 2 * b)
                    act.activation(x1T[:, 1 + h * HALF:1 + (h + 1) * HALF], mix[:], ACT.Copy).then_inc(x1T_copied, 1)
                elif n < 4:
                    act.wait_ge(km_ready, 2 * b + h + 1)
                    wait(act, kact_ready, 2 * b)
                    act.activation(relu[:, half(h)], mix[:], ACT.Relu).then_inc(relu_done, 1)
                else:
                    act.wait_ge(r_ready, 2 * b + h + 1)
                    wait(act, mixed_ready, 2 * b)
                    act.activation(gate[:, half(h)], mix[:], ACT.Tanh, scale=0.5).then_inc(gate_ready, 1)

            def iteration(i, attend, channel):
                b = i - 1
                if attend:
                    for h in range(2):
                        act.wait_ge(xT_ready, 2 * i + h + 1)
                        act.activation(xT[:, half(h)], turn[h][:], ACT.Copy).then_inc(xT_copied, 1)
                    for h in range(2):
                        act.wait_ge(k_ready, 2 * i + h + 1)
                        act.activation(kT[:, half(h)], score[0][:, half(h)], ACT.Copy).then_inc(k_copied, 1)
                for s in range(CH + 1):
                    if channel:
                        for n in EARLY.get(s, ()):
                            if n < 6:
                                channel_piece(b, n)
                    if attend and s < CH:
                        act.wait_ge(max_found, CH * i + s + 1)
                        if s >= 2:
                            act.wait_ge(turned, GROUPS * i + groups(s - 2)[-1][0] + 1)
                        else:
                            wait(act, turned, GROUPS * (i - 1) + groups(CH - 2 + s)[-1][0] + 1)
                        wait(act, combined, CH * (i - 1) + s + 1)
                        act.activation(probs[:, s % 2, 0:(s + 1) * P], score[s % 2][:, 0:(s + 1) * P], ACT.Exp,
                                       bias=negmax[:, s % 2:s % 2 + 1],
                                       accum_out=rowsum[:, s:s + 1]).then_inc(exp_done, 1)
                    if attend and s >= 1:
                        for g, first, blocks in groups(s - 1):
                            if g % 2 == 0:
                                act.wait_ge(turned, GROUPS * i + g + 1)
                                wait(act, pv_done, CH * i + s - 2)
                                act.activation(probsT[:, (s - 1) % 2, first * P:(first + blocks) * P],
                                               turn[0][:, 0:blocks * P], ACT.Copy).then_inc(even_copied, 1)
                    if channel:
                        for n in LATE.get(s, ()):
                            if n < 6:
                                channel_piece(b, n)
                    if not attend:
                        for n in ACT_PIECES.get(s, ()):
                            pr.on_scalar(act, act_settled, score[1], 0, n)

            iteration(0, True, False)
            iteration(1, True, True)
            with act.Fori(2, BATCH) as i:
                iteration(i, True, True)
            act.wait_ge(later_in, 16 * len(later))
            act.activation(a_pos[:], a_log[:], ACT.Exp).then_inc(a_made, 1)
            iteration(BATCH, False, True)

        @block.vector
        def _(dve):
            def find_max(i, q):
                dve.wait_ge(scored, CH * i + q + 1)
                dve.tensor_reduce(negmax[:, q % 2:q % 2 + 1], score[q % 2][:, 0:(q + 1) * P], AX.X, ALU.max,
                                  negate=True).then_inc(max_found, 1)

            def combine(i, q):
                dve.wait_ge(pv_done, CH * i + q + 1)
                dve.wait_ge(inverted, CH * i + q + 1)
                dve.wait_ge(xx_made, i + 1)
                wait(dve, x1_ready, CH * i)
                dve.scalar_tensor_tensor(out=att[:, q, :], in0=pv[:, 0:P], scalar=rinv[:, q % 2:q % 2 + 1],
                                         in1=xx[:, q, :], op0=ALU.mult, op1=ALU.add).then_inc(combined, 1)

            def invert(i, q):
                dve.wait_ge(exp_done, CH * i + q + 1)
                dve.reciprocal(rinv[:, q % 2:q % 2 + 1], rowsum[:, q:q + 1]).then_inc(inverted, 1)

            def copy_odd(i, q):
                for g, first, blocks in groups(q):
                    if g % 2:
                        dve.wait_ge(turned, GROUPS * i + g + 1)
                        wait(dve, pv_done, CH * i + q - 1)
                        dve.tensor_copy(probsT[:, q % 2, first * P:(first + blocks) * P],
                                        turn[1][:, 0:blocks * P]).then_inc(odd_copied, 1)

            def sum_up(i, q):
                dve.wait_ge(combined, CH * i + q + 1)
                dve.bn_stats(stats[:, q, :], att[:, q, :]).then_inc(summed, 1)

            def mix_inputs(b, second):
                dve.wait_ge(diff_ready, b + 1)
                wait(dve, r_ready if second else km_ready, 2 * b)
                out, m = (xr, 0) if second else (xk, 1)
                dve.scalar_tensor_tensor(out=out[:], in0=diff[:], scalar=mu[:, m:m + 1], in1=x1T[:, 0:T],
                                         op0=ALU.mult, op1=ALU.add).then_inc(xk_ready, 1)

            def apply_gate(b, h):
                dve.wait_ge(gate_ready, 2 * b + h + 1)
                dve.wait_ge(vm_ready, 2 * b + h + 1)
                dve.scalar_tensor_tensor(out=gate[:, half(h)], in0=gate[:, half(h)], scalar=1.0, in1=mix[:],
                                         op0=ALU.add, op1=ALU.mult).then_inc(gated, 1)

            def add_x1(b, h):
                dve.wait_ge(gated, 2 * b + h + 1)
                cs = slice(HC * h, HC * h + HC)
                dve.scalar_tensor_tensor(out=mixed[:, cs, :].rearrange("p c d -> p (c d)"), in0=gate[:, half(h)],
                                         scalar=0.5, in1=x1[:, cs, :].rearrange("p c d -> p (c d)"),
                                         op0=ALU.mult, op1=ALU.add).then_inc(mixed_ready, 1)

            def sum_up2(b, cs):
                dve.wait_ge(mixed_ready, 2 * b + 2)
                for c in cs:
                    dve.bn_stats(stats2[:, c, :], mixed[:, c, :]).then_inc(summed2, 1)

            def aggregate(b, sums, done, out, ready):
                dve.wait_ge(done, CH * b + CH)
                settle(dve, dve_settled)
                for c in range(CH):
                    dve.bn_aggr(out[:, c, :], sums[:, c, :]).then_inc(ready, 1)

            def normalise_x2(b, cs):
                dve.wait_ge(rstd2_ready, b + 1)
                out = x_all[:, b] if isinstance(b, int) else \
                    x_all[:, bass.ds(b, 1)].rearrange("p b c d -> p (b c) d")
                for c in cs:
                    dve.tensor_scalar(out[:, c, :], mixed[:, c, :], mv2[:, c, 0:1], rstd2[:, c:c + 1],
                                      ALU.subtract, ALU.mult).then_inc(x2_ready, 1)

            def split_rows(rows, rows32, done):
                dve.tensor_copy(rows[:], rows32[:]).then_inc(rows_made, 1)
                dve.wait_ge(rows_made, done + 1)
                dve.tensor_tensor(rows32[:], rows32[:], rows[:], ALU.subtract).then_inc(rows_made, 1)
                dve.wait_ge(rows_made, done + 2)
                dve.tensor_copy(rows[32:64], rows32[32:64]).then_inc(rows_made, 1)
                dve.tensor_copy(rows[64:96], rows32[64:96]).then_inc(rows_made, 1)
                dve.wait_ge(rows_made, done + 4)
                dve.tensor_tensor(rows[64:96], rows32[64:96], rows[64:96], ALU.subtract).then_inc(rows_made, 1)

            def later_weights(second):
                minus_one, pick, w = keep["minus_one"], keep["pick"], keep["w"]
                if not second:
                    dve.wait_ge(later_in, 16 * len(later))
                    dve.tensor_scalar(w[:], q[:], 1.0 / 7.5, -1.0, ALU.mult, ALU.add).then_inc(dequant, 1)
                    dve.memset(keep["ones"][:], 1.0).then_inc(picks, 1)
                    dve.memset(minus_one[:], 0.0).then_inc(picks, 1)
                    dve.wait_ge(dequant, 1)
                    dve.tensor_tensor(w[:], w[:], scale[:], ALU.mult).then_inc(dequant, 1)
                    dve.wait_ge(picks, 2)
                    dve.tensor_scalar(minus_one[:, 0, :], ident[0:K3, 0:K3], -1.0, None, ALU.mult).then_inc(picks, 1)
                    dve.tensor_scalar(minus_one[0:32, 1, :], ident[0:32, 0:K3], -1.0, None, ALU.mult).then_inc(picks, 1)
                    split_rows(keep["rows"], rows32, 0)
                else:
                    dve.wait_ge(dequant, 2)
                    dve.wait_ge(lora, 1)
                    flat_w = w[:].rearrange("p c d -> p (c d)")
                    dve.tensor_tensor(flat_w, score[0][:, 0:LINEARS * P], flat_w, ALU.add).then_inc(dequant, 1)
                    dve.wait_ge(a_made, 1)
                    dve.tensor_scalar(keep["a_neg"][:], a_pos[:], -1.0, None, ALU.mult).then_inc(picks, 1)
                    split_rows(keep["f_rows"], f_rows32, 5)
                    for r in range(2):
                        dve.tensor_copy(pick[:, N * r:N * r + N, :],
                                        pick32[:, N * r:N * r + N].unsqueeze(2).broadcast_to([K3, N, P])
                                        ).then_inc(picks, 1)

            def iteration(i, attend, channel, older):
                b = i - 1
                if attend:
                    for h in range(2):
                        dve.wait_ge(v_ready, 2 * i + h + 1)
                        dve.tensor_copy(val[:, HC * h:HC * h + HC, :].rearrange("p c d -> p (c d)"),
                                        score[1][:, half(h)]).then_inc(v_copied, 1)
                for s in range(CH + 2):
                    if attend:
                        if s < CH:
                            find_max(i, s)
                        if 1 <= s <= CH:
                            invert(i, s - 1)
                        if s >= 2:
                            combine(i, s - 2)
                        if 1 <= s <= CH:
                            copy_odd(i, s - 1)
                        if s >= 2:
                            sum_up(i, s - 2)
                    if older and s < 3:
                        sum_up2(b - 1, THIRDS[s])
                    if older and s == 3:
                        aggregate(b - 1, stats2, summed2, mv2, mv2_ready)
                    if older and 5 <= s < 8:
                        normalise_x2(b - 1, THIRDS[s - 5])
                    if channel and s in (4, 5):
                        mix_inputs(b, s == 5)
                    if channel and s == 8:
                        apply_gate(b, 0)
                        add_x1(b, 0)
                    if not attend and s in (0, 7):
                        later_weights(s == 7)
                    if not attend:
                        for n in DVE_PIECES.get(s, ()):
                            pr.on_vector(dve, score[1], 0, n)
                if attend:
                    aggregate(i, stats, summed, mv, mv_ready)
                if channel:
                    apply_gate(b, 1)
                    add_x1(b, 1)

            dve.wait_ge(weights_in, 16 * len(weights))
            dve.tensor_copy(mask[:], mask32[:]).then_inc(consts, 1)
            dve.tensor_copy(ident16[:], ident[:]).then_inc(consts, 1)
            iteration(0, True, False, False)
            iteration(1, True, True, False)
            with dve.Fori(2, BATCH) as i:
                iteration(i, True, True, True)
            iteration(BATCH, False, True, True)


def at(i, n):
    return i + n // N, n % N


def step_count(i, n):
    return N * i + n


def ssm_phase(nc, d, keep):
    with ExitStack() as ctx:
        def sb(name, shape, dt=F32):
            return ctx.enter_context(nc.sbuf_tensor(name + "_sb", shape, dt))

        def ps(name, cols):
            return ctx.enter_context(nc.psum_tensor(name, [P, cols], F32))

        def sem(name):
            return ctx.enter_context(nc.semaphore(name))

        ident, x_all = keep["ident"], keep["x_all"]
        DEEP = 4
        LEAD = 4
        a_neg, pick, pr, out = keep["a_neg"], keep["pick"], keep["projections"], keep["output"]
        side, y, summed_y, res_ready = out.side, out.y, out.summed_y, out.res_ready
        mixed = keep["mixed"]
        dt, u, z, bc, slot = pr.dt, pr.u, pr.z, pr.bc, pr.slot
        x2T_ready, dt_ready, bc_part, u_ready, z_ready = pr.x2T_ready, pr.dt_ready, pr.bc_part, pr.u_ready, pr.z_ready
        a_ready, xb_ready, yz_ready = pr.a_ready, pr.xb_ready, pr.yz_ready
        x2 = sb("x2", [P, CH, P])
        a, bn, xb = sb("a", [P, DEEP, T]), sb("bn", [P, DEEP, T]), sb("xb", [P, DEEP, T])
        h, hc = sb("h", [P, 4, T]), sb("hc", [P, 2, T])
        l_stats, l_mv = sb("l_stats", [P, CH, 6]), sb("l_mv", [P, CH, 2])
        l_var_eps, l_rstd = sb("l_var_eps", [P, CH]), sb("l_rstd", [P, CH])
        b_bank, c_bank = ps("b_bank", T), ps("c_bank", T)

        pool_settled, dve_settled, act_settled = sem("s_pool_settled"), sem("s_dve_settled"), sem("s_act_settled")
        pool_const = sem("pool_const")
        x2_in = sem("x2_in")
        b_ready = sem("b_ready")
        b_copied = sem("b_copied")
        scanned = sem("scanned")
        c_ready = sem("c_ready")
        hc_ready = sem("hc_ready")
        l_summed = sem("l_summed")
        l_mv_ready = sem("l_mv_ready")
        l_veps_ready = sem("l_veps_ready")
        l_rstd_ready = sem("l_rstd_ready")
        l_x2_ready = sem("l_x2_ready")
        block = ctx.enter_context(nc.Block())

        @block.sync
        def _(sp):
            sp.dma_start(x2[:], rows_of(x_all, 1)).then_inc(x2_in, 16)
            sp.wait_ge(l_x2_ready, CH)
            with sp.Fori(2, BATCH) as i:
                wait(sp, x2T_ready, i)
                sp.dma_start(x2[:], rows_of(x_all, i)).then_inc(x2_in, 16)

        @block.gpsimd
        def _(pool):
            def scale_b(i, n):
                g = step_count(*at(i, n))
                b = at(i, n)[0]
                if at(i, n)[1] == 0:
                    pool.wait_ge(u_ready, b + 1)
                pool.wait_ge(b_copied, g + 1)
                wait(pool, scanned, g - DEEP + 1)
                settle(pool, pool_settled)
                pool.tensor_tensor(xb[:, n % DEEP, :], slot(u, b), bn[:, n % DEEP, :], ALU.mult).then_inc(xb_ready, 1)

            def inverse_std_x2():
                pool.wait_ge(l_mv_ready, CH)
                pool.tensor_scalar(l_var_eps[:], l_mv[:, :, 1], 1.0, EPS, ALU.mult, ALU.add).then_inc(l_veps_ready, 1)
                pool.wait_ge(l_veps_ready, 1)
                pool.tensor_tensor(l_rstd[:], l_var_eps[:], out.minus_half[:], ALU.pow).then_inc(l_rstd_ready, 1)

            def iteration(i, finish, more):
                for n in range(N):
                    if more or n + LEAD - 1 < N:
                        scale_b(i, n + LEAD - 1)
                    if finish:
                        out.on_pool(pool, pool_settled, i - 1, n)
                    elif n == 8:
                        inverse_std_x2()

            pool.memset(out.minus_half[:], -0.5).then_inc(pool_const, 1)
            pool.wait_ge(pool_const, 1)
            for n in range(LEAD - 1):
                scale_b(0, n)
            iteration(0, False, True)
            iteration(1, True, True)
            with pool.Fori(2, BATCH - 1) as i:
                iteration(i, True, True)
            iteration(BATCH - 1, True, False)

        @block.tensor
        def _(pe):
            def spread_b(i, n):
                b, k = at(i, n)
                g = step_count(b, k)
                if k == 0:
                    pe.wait_ge(bc_part, 3 * b + 3)
                wait(pe, b_copied, g)
                for f in range(2):
                    mm = pe.matmul(b_bank[:, half(f)], pick[:, k, :], slot(bc, b)[:, half(f)], start=True, stop=True)
                mm.then_inc(b_ready, 1)

            def spread_c(i, n):
                wait(pe, hc_ready, step_count(i, n))
                for f in range(2):
                    mm = pe.matmul(c_bank[:, half(f)], pick[:, N + n, :], slot(bc, i)[:, half(f)], start=True, stop=True)
                mm.then_inc(c_ready, 1)

            def sum_states(i, n):
                b, k = at(i, n)
                g = step_count(b, k)
                pe.wait_ge(hc_ready, g + 1)
                if k == 0:
                    wait(pe, yz_ready, b)
                for c in range(CH):
                    mm = pe.matmul(y[:, chunk(c)], hc[:, k % 2, chunk(c)], ident[:], is_transpose=True,
                                   start=k == 0 and c % HC == 0, stop=k == N - 1, skip_group_check=True)
                mm.then_inc(summed_y, 1)

            def iteration(i, done, more):
                for n in range(N):
                    spread_c(i, n)
                    if n == 0 and done:
                        sum_states(i, -1)
                    if more or n + LEAD < N:
                        spread_b(i, n + LEAD)
                    if n:
                        sum_states(i, n - 1)
                    if done:
                        out.on_tensor(pe, i - 1, n)
                    if more:
                        if n == 4:
                            wait(pe, x2_in, 16 * (i + 1))
                            wait(pe, res_ready, i)
                            wait(pe, z_ready, i + 1)
                        pr.on_tensor(pe, side, x2[:], i + 1, n)

            for n in range(LEAD):
                spread_b(0, n)
            iteration(0, False, True)
            iteration(1, True, True)
            with pe.Fori(2, BATCH - 1) as i:
                iteration(i, True, True)
            iteration(BATCH - 1, True, False)
            sum_states(BATCH - 1, N - 1)

        @block.scalar
        def _(act):
            def copy_b(i, n):
                g = step_count(*at(i, n))
                act.wait_ge(b_ready, g + 1)
                wait(act, xb_ready, g - DEEP + 1)
                act.activation(bn[:, n % DEEP, :], b_bank[:], ACT.Copy).then_inc(b_copied, 1)

            def decay(i, n):
                b, k = at(i, n)
                g = step_count(b, k)
                if k == 0:
                    act.wait_ge(dt_ready, b + 1)
                wait(act, scanned, g - DEEP + 1)
                settle(act, act_settled)
                act.activation(a[:, n % DEEP, :], slot(dt, b), ACT.Exp, scale=a_neg[:, k:k + 1]).then_inc(a_ready, 1)

            def iteration(i, done, more):
                for n in range(N):
                    if more or n + LEAD < N:
                        copy_b(i, n + LEAD)
                    if more or n + LEAD - 1 < N:
                        decay(i, n + LEAD - 1)
                    if more:
                        pr.on_scalar(act, act_settled, side, i + 1, n)
                    if done:
                        out.on_scalar(act, i - 1, n)

            act.preload_act_table_set("natural_log_exp_and_others")
            for n in range(LEAD):
                copy_b(0, n)
                if n < LEAD - 1:
                    decay(0, n)
            iteration(0, False, True)
            iteration(1, True, True)
            with act.Fori(2, BATCH - 1) as i:
                iteration(i, True, True)
            iteration(BATCH - 1, True, False)

        @block.vector
        def _(dve):
            def scan_state(i, n):
                b, k = at(i, n)
                g = step_count(b, k)
                dve.wait_ge(a_ready, g + 1)
                dve.wait_ge(xb_ready, g + 1)
                wait(dve, hc_ready, g - 3)
                dve.tensor_tensor_scan(h[:, n % 4, :], a[:, n % DEEP, :], xb[:, n % DEEP, :], 0.0, ALU.mult,
                                       ALU.add).then_inc(scanned, 1)

            def times_c(i, n):
                g = step_count(i, n)
                dve.wait_ge(scanned, g + 1)
                wait(dve, summed_y, g - 1)
                dve.wait_ge(c_ready, g + 1)
                dve.tensor_tensor(hc[:, n % 2, :], h[:, n % 4, :], c_bank[:], ALU.mult).then_inc(hc_ready, 1)

            def normalise_x2(n):
                if n in (5, 6):
                    for c in range(HC * (n - 5), HC * (n - 5) + HC):
                        dve.bn_stats(l_stats[:, c, :], mixed[:, c, :]).then_inc(l_summed, 1)
                elif n == 7:
                    dve.wait_ge(l_summed, CH)
                    for c in range(CH):
                        dve.bn_aggr(l_mv[:, c, :], l_stats[:, c, :]).then_inc(l_mv_ready, 1)
                elif n in (11, 13):
                    dve.wait_ge(l_rstd_ready, 1)
                    for c in range(HC * (n == 13), HC * (n == 13) + HC):
                        dve.tensor_scalar(x_all[:, BATCH - 1, c, :], mixed[:, c, :], l_mv[:, c, 0:1], l_rstd[:, c:c + 1],
                                          ALU.subtract, ALU.mult).then_inc(l_x2_ready, 1)

            def iteration(i, done, more):
                for n in range(N):
                    if more or n + 1 < N:
                        scan_state(i, n + 1)
                    times_c(i, n)
                    if more:
                        pr.on_vector(dve, side, i + 1, n)
                    if done:
                        out.on_vector(dve, dve_settled, i - 1, n)
                    else:
                        normalise_x2(n)

            scan_state(0, 0)
            iteration(0, False, True)
            iteration(1, True, True)
            with dve.Fori(2, BATCH - 1) as i:
                iteration(i, True, True)
            iteration(BATCH - 1, True, False)


def ffn_phase(nc, d, keep):
    LANES = 4
    ON_ACT = 2
    ON_DVE = HC - ON_ACT
    PAIRS = BATCH // 2
    with ExitStack() as ctx:
        def sb(name, shape, dt=F32):
            return ctx.enter_context(nc.sbuf_tensor(name + "_sb", shape, dt))

        def ps(name, cols):
            return ctx.enter_context(nc.psum_tensor(name, [P, cols], F32))

        def sem(name):
            return ctx.enter_context(nc.semaphore(name))

        ident, x_all = keep["ident"], keep["x_all"]
        w, gamma, beta = keep["w"], keep["gamma"], keep["beta"]
        rows, ones = keep["f_rows"], keep["ones"]
        minus_half = sb("f_minus_half", [P, HC])

        def lanes(name, *shape):
            return [sb(f"{name}{n}", [P, *shape]) for n in range(LANES)]

        h_in, h_a, h_b, hx = lanes("h_in", HC, P), lanes("h_a", HC, P), lanes("h_b", HC, P), lanes("hx", HC, P)
        hT, yn, gT = lanes("hT", HALF), lanes("yn", HC, P), lanes("gT", HALF)
        fin, out = lanes("fin", HC, P), lanes("out", HC, P)
        stats, mv = lanes("f_stats", HC, 6), lanes("f_mv", HC, 2)
        var_eps, rstd = lanes("f_var_eps", HC), lanes("f_rstd", HC)
        shift = lanes("f_shift", ON_ACT)
        stats2, mv2 = lanes("g_stats", HC, 6), lanes("g_mv", HC, 2)
        var_eps2, rstd2 = lanes("g_var_eps", HC), lanes("g_rstd", HC)
        output = keep["output"]
        turn = [ps("f_turn0", HALF), ps("f_turn1", HALF), output.y[:, half(0)], output.y[:, half(1)]]
        lin = [ps("lin0", HALF), ps("lin1", HALF), output.side[:, half(0)], output.side[:, half(1)]]

        pool_settled, dve_settled = sem("f_pool_settled"), sem("f_dve_settled")
        act_settled = sem("f_act_settled")
        pool_const = sem("f_pool_const")
        h_loaded = sem("h_loaded")
        hT_ready = sem("hT_ready")
        hT_copied = sem("hT_copied")
        lin0_ready = sem("lin0_ready")
        summed = sem("f_summed")
        mv_ready = sem("f_mv_ready")
        veps_ready = sem("f_veps_ready")
        rstd_ready = sem("f_rstd_ready")
        shift_part = sem("f_shift_part")
        normed = sem("normed")
        act_normed = sem("act_normed")
        ynT_ready = sem("ynT_ready")
        gelu_done = sem("gelu_done")
        lin1_ready = sem("lin1_ready")
        res_ready = sem("f_res_ready")
        hx_ready = sem("hx_ready")
        summed2 = sem("g_summed")
        mv2_ready = sem("g_mv_ready")
        veps2_ready = sem("g_veps_ready")
        rstd2_ready = sem("g_rstd_ready")
        out_ready = sem("f_out_ready")
        stored = sem("stored")
        block = ctx.enter_context(nc.Block())

        def batches(j):
            if isinstance(j, int):
                return x_all[:, 2 * j:2 * j + 2]
            return x_all[:, bass.ds(2 * j, 2)]

        def lane_rows(j, n):
            return batches(j)[:, n // 2, HC * (n % 2):HC * (n % 2) + HC, :]

        TURNS = BLOCKS * LANES

        PE_PIECES = {0: (1,), 1: (2, 3)}
        ACT_PIECES = {0: (1,)}
        DVE_PIECES = {1: (4,), 2: (5, 6), 3: (7,), 5: (11,), 6: (13,)}
        POOL_PIECES = {3: (8,)}

        def turn_at(j, s, lag, first):
            if s >= lag:
                return j, (s - lag) // LANES, (s - lag) % LANES
            return None if first else (j - 1, (s - lag + TURNS) // LANES, (s - lag) % LANES)

        LAST_SUMS = {0: 0, 3: 1, 6: 2, 9: 3}
        LAST_NORMS = {2: 0, 5: 1, 8: 2, 11: 3}

        def entering(j, n):
            return lane_rows(0, n) if isinstance(j, int) and j == 0 else h_in[n]

        def count(j, k, n):
            return TURNS * j + LANES * k + n + 1

        out_dram = d["out"].rearrange("(j e) (f c p) d -> j e f p c d", e=2, f=2, p=P)

        @block.sync
        def _(sp):
            def load(j):
                for n in range(LANES):
                    sp.dma_start(h_in[n][:], lane_rows(j, n)).then_inc(h_loaded, 16)

            def store(j, n):
                sp.wait_ge(out_ready, HC * (LANES * j + n + 1))
                dst = out_dram[j:j + 1] if isinstance(j, int) else out_dram[bass.ds(j, 1)]
                sp.dma_start(dst[:, n // 2, n % 2].rearrange("j p c d -> (j p) c d"), out[n][:]).then_inc(stored, 16)

            def pair(j, more):
                for n in range(LANES):
                    store(j - 1, n)
                    if more and n == 1:
                        sp.wait_ge(res_ready, count(j, 0, LANES - 1))
                        load(j + 1)

            load(1)
            sp.wait_ge(output.x3_ready, CH * BATCH)
            with sp.Fori(1, PAIRS - 1) as j:
                pair(j, True)
            pair(PAIRS - 1, False)
            for n in range(LANES):
                store(PAIRS - 1, n)
            sp.wait_ge(stored, 16 * LANES * PAIRS)

        @block.gpsimd
        def _(pool):
            pool.memset(minus_half[:], -0.5).then_inc(pool_const, 1)
            pool.wait_ge(pool_const, 1)

            def inverse_std(j, k, n):
                c = count(j, k, n)
                pool.wait_ge(mv_ready, HC * c)
                settle(pool, pool_settled)
                pool.tensor_scalar(var_eps[n][:], mv[n][:, :, 1], 1.0, EPS, ALU.mult, ALU.add).then_inc(veps_ready, 1)
                pool.wait_ge(veps_ready, c)
                pool.tensor_tensor(rstd[n][:], var_eps[n][:], minus_half[:], ALU.pow).then_inc(rstd_ready, 1)
                pool.wait_ge(rstd_ready, c)
                pool.tensor_tensor(shift[n][:], mv[n][:, ON_DVE:, 0], rstd[n][:, ON_DVE:], ALU.mult).then_inc(shift_part, 1)
                pool.wait_ge(shift_part, 2 * c - 1)
                settle(pool, pool_settled)
                pool.tensor_scalar(shift[n][:], shift[n][:], -1.0, 0.0, ALU.mult, ALU.add).then_inc(shift_part, 1)

            def add_x3(j, n):
                pool.wait_ge(res_ready, count(j, 1, n))
                settle(pool, pool_settled)
                pool.tensor_tensor(hx[n][:], h_b[n][:], lane_rows(j, n), ALU.add).then_inc(hx_ready, 1)

            def inverse_std2(j, n):
                c = LANES * j + n + 1
                pool.wait_ge(mv2_ready, HC * c)
                settle(pool, pool_settled)
                pool.tensor_scalar(var_eps2[n][:], mv2[n][:, :, 1], 1.0, EPS, ALU.mult,
                                   ALU.add).then_inc(veps2_ready, 1)
                pool.wait_ge(veps2_ready, c)
                pool.tensor_tensor(rstd2[n][:], var_eps2[n][:], minus_half[:], ALU.pow).then_inc(rstd2_ready, 1)

            def pair(j, first):
                for s in range(TURNS):
                    turn1 = turn_at(j, s, 1, first)
                    if turn1:
                        inverse_std(*turn1)
                    turn4 = turn_at(j, s, 4, first)
                    if turn4 and turn4[1] == 1:
                        add_x3(turn4[0], turn4[2])
                    if not first and s in LAST_SUMS:
                        inverse_std2(j - 1, LAST_SUMS[s])
                    if first:
                        for n in POOL_PIECES.get(s, ()):
                            output.on_pool(pool, pool_settled, BATCH - 1, n)

            pair(0, True)
            with pool.Fori(1, PAIRS) as j:
                pair(j, False)
            inverse_std(PAIRS - 1, BLOCKS - 1, LANES - 1)
            for n in range(LANES):
                inverse_std2(PAIRS - 1, n)

        @block.tensor
        def _(pe):
            def linear(n, src, i):
                for c in range(HC):
                    mm = pe.matmul(lin[n][:, chunk(c)], src[n][:, chunk(c)], w[:, i, :], start=False, stop=c == HC - 1,
                                   skip_group_check=True)
                return mm

            def bias(n, i):
                pe.matmul(lin[n][:], ones[:], rows[:, i, :].unsqueeze(1).broadcast_to([96, HC, P]), start=True,
                          stop=False, skip_group_check=True)

            def turn_normed(j, k, n):
                pe.wait_ge(normed, ON_DVE * count(j, k, n))
                pe.wait_ge(act_normed, ON_ACT * count(j, k, n))
                for c in range(HC):
                    mm = pe.transpose(turn[n][:, chunk(c)], yn[n][:, c, :], ident[:])
                mm.then_inc(ynT_ready, 1)

            def turn_h(j, k, n):
                if k:
                    pe.wait_ge(res_ready, count(j, k - 1, n))
                else:
                    wait(pe, h_loaded, 16 * LANES * j)
                h = (entering(j, n), h_a[n], h_b[n])[k]
                for c in range(HC):
                    mm = pe.transpose(turn[n][:, chunk(c)], h[:, c, :], ident[:])
                mm.then_inc(hT_ready, 1)

            def second_bias(j, k, n):
                bias(n, 2 * k + 1)

            def first_bias(j, k, n):
                wait(pe, res_ready, count(j, k - 1, n))
                bias(n, 2 * k)

            def second_linear(j, k, n):
                pe.wait_ge(gelu_done, count(j, k, n))
                linear(n, gT, 2 * k + 1).then_inc(lin1_ready, 1)

            def first_linear(j, k, n):
                pe.wait_ge(hT_copied, count(j, k, n))
                linear(n, hT, 2 * k).then_inc(lin0_ready, 1)

            def pair(j, first):
                for s in range(TURNS):
                    turn0, turn3 = turn_at(j, s, 0, first), turn_at(j, s, 3, first)
                    if first and s == 2:
                        pe.wait_ge(output.res_ready, BATCH)
                    if turn3:
                        turn_normed(*turn3)
                    turn_h(*turn0)
                    if turn3:
                        second_bias(*turn3)
                    first_bias(*turn0)
                    if turn3:
                        second_linear(*turn3)
                    first_linear(*turn0)
                    if first:
                        for n in PE_PIECES.get(s, ()):
                            output.on_tensor(pe, BATCH - 1, n)

            pair(0, True)
            with pe.Fori(1, PAIRS) as j:
                pair(j, False)
            for n in range(1, LANES):
                turn_normed(PAIRS - 1, BLOCKS - 1, n)
                second_bias(PAIRS - 1, BLOCKS - 1, n)
                second_linear(PAIRS - 1, BLOCKS - 1, n)

        @block.scalar
        def _(act):
            def activate(j, k, n):
                act.wait_ge(ynT_ready, count(j, k, n))
                act.activation(gT[n][:], turn[n][:], ACT.Gelu, bias=beta[:, k:k + 1],
                               scale=gamma[:, k:k + 1]).then_inc(gelu_done, 1)

            def normalise(j, k, n):
                act.wait_ge(shift_part, 2 * count(j, k, n))
                act.wait_ge(normed, ON_DVE * count(j, k, n))
                settle(act, act_settled)
                for s in range(ON_DVE, HC):
                    act.activation(yn[n][:, s, :], lin[n][:, chunk(s)], ACT.Identity,
                                   bias=shift[n][:, s - ON_DVE:s - ON_DVE + 1],
                                   scale=rstd[n][:, s:s + 1]).then_inc(act_normed, 1)

            def copy_h(j, k, n):
                act.wait_ge(hT_ready, count(j, k, n))
                act.activation(hT[n][:], turn[n][:], ACT.Copy).then_inc(hT_copied, 1)

            def pair(j, first):
                for s in range(TURNS):
                    turn3 = turn_at(j, s, 3, first)
                    if turn3:
                        activate(*turn3)
                    copy_h(*turn_at(j, s, 0, first))
                    turn2 = turn_at(j, s, 2, first)
                    if turn2:
                        normalise(*turn2)
                    if first:
                        for n in ACT_PIECES.get(s, ()):
                            output.on_scalar(act, BATCH - 1, n)

            act.preload_act_table_set("gelu_and_others")
            pair(0, True)
            with act.Fori(1, PAIRS) as j:
                pair(j, False)
            for n in range(1, LANES):
                activate(PAIRS - 1, BLOCKS - 1, n)
                if n < LANES - 1:
                    normalise(PAIRS - 1, BLOCKS - 1, n + 1)

        @block.vector
        def _(dve):
            def flat(x):
                return x[:, :, :].rearrange("p c d -> p (c d)")

            def sum_up(j, k, n):
                dve.wait_ge(lin0_ready, count(j, k, n))
                for s in range(HC):
                    dve.bn_stats(stats[n][:, s, :], lin[n][:, chunk(s)]).then_inc(summed, 1)

            def aggregate(c, sums, done, out, ready):
                dve.wait_ge(done, HC * c)
                settle(dve, dve_settled)
                for s in range(HC):
                    dve.bn_aggr(out[:, s, :], sums[:, s, :]).then_inc(ready, 1)

            def normalise(j, k, n):
                dve.wait_ge(rstd_ready, count(j, k, n))
                for s in range(ON_DVE):
                    dve.tensor_scalar(yn[n][:, s, :], lin[n][:, chunk(s)], mv[n][:, s, 0:1], rstd[n][:, s:s + 1],
                                      ALU.subtract, ALU.mult).then_inc(normed, 1)

            def add_h(j, k, n):
                dve.wait_ge(lin1_ready, count(j, k, n))
                if k == 1:
                    wait(dve, hx_ready, LANES * (j - 1) + n + 1)
                if k == 2:
                    dve.wait_ge(hx_ready, LANES * j + n + 1)
                dve.tensor_tensor(flat((h_a, h_b, fin)[k][n]), lin[n][:], flat((entering(j, n), h_a[n], hx[n])[k]),
                                  ALU.add).then_inc(res_ready, 1)

            def last_statistics(j, n):
                dve.wait_ge(res_ready, count(j, BLOCKS - 1, n))
                for s in range(HC):
                    dve.bn_stats(stats2[n][:, s, :], fin[n][:, s, :]).then_inc(summed2, 1)
                aggregate(LANES * j + n + 1, stats2[n], summed2, mv2[n], mv2_ready)

            def last_normalise(j, n):
                dve.wait_ge(rstd2_ready, LANES * j + n + 1)
                wait(dve, stored, 16 * LANES * j)
                for s in range(HC):
                    dve.tensor_scalar(out[n][:, s, :], fin[n][:, s, :], mv2[n][:, s, 0:1], rstd2[n][:, s:s + 1],
                                      ALU.subtract, ALU.mult).then_inc(out_ready, 1)

            def pair(j, first):
                if first:
                    output.on_vector(dve, dve_settled, BATCH - 1, 0)
                for s in range(TURNS):
                    turn1, turn2, turn4 = (turn_at(j, s, lag, first) for lag in (1, 2, 4))
                    if turn4:
                        add_h(*turn4)
                    if turn1:
                        sum_up(*turn1)
                    if not first and s in LAST_NORMS:
                        last_normalise(j - 1, LAST_NORMS[s])
                    if turn1:
                        aggregate(count(*turn1), stats[turn1[2]], summed, mv[turn1[2]], mv_ready)
                    if turn2:
                        normalise(*turn2)
                    if not first and s in LAST_SUMS:
                        last_statistics(j - 1, LAST_SUMS[s])
                    if first:
                        for n in DVE_PIECES.get(s, ()):
                            output.on_vector(dve, dve_settled, BATCH - 1, n)

            pair(0, True)
            with dve.Fori(1, PAIRS) as j:
                pair(j, False)
            for n in range(LANES):
                add_h(PAIRS - 1, BLOCKS - 1, n)
                if n == 0:
                    sum_up(PAIRS - 1, BLOCKS - 1, LANES - 1)
                    aggregate(PAIRS * TURNS, stats[LANES - 1], summed, mv[LANES - 1], mv_ready)
                if n < 2:
                    normalise(PAIRS - 1, BLOCKS - 1, LANES - 2 + n)
                last_statistics(PAIRS - 1, n)
                if n:
                    last_normalise(PAIRS - 1, n - 1)
            last_normalise(PAIRS - 1, LANES - 1)


def build(nc, d):
    with ExitStack() as ctx:
        keep = keep_on_chip(nc, ctx)
        attention_phase(nc, d, keep)
        keep["output"] = Output(nc, ctx, keep)
        ssm_phase(nc, d, keep)
        ffn_phase(nc, d, keep)


def lay_out(np, inputs):
    tr = np.ascontiguousarray
    w = inputs["L0_attn_W"]
    return {
        "L0_attn_x": tr(inputs["L0_attn_x"]),
        "ident": np.eye(P, dtype=np.float32),
        "mask": np.triu(np.full((P, P), MASKED, np.float32), 1),
        "w_key": tr(w[:P].T), "w_val": tr(w[P:].T),
        "w_r": tr(inputs["L0_ffn_W_r"].T), "w_k": tr(inputs["L0_ffn_W_k"].T), "w_v": tr(inputs["L0_ffn_W_v"].T),
        "w_dt": tr(inputs["L1_attn_Wdt"]), "w_x": tr(inputs["L1_attn_Wx"]), "w_z": tr(inputs["L1_attn_Wz"]),
        "w_out": tr(inputs["L1_attn_Wout"]),
        "w_bc": tr(np.concatenate([inputs["L1_attn_WB"], inputs["L1_attn_WC"]] * 3, 1)),
        "b_bc": tr(np.concatenate([inputs["L1_attn_bB"], inputs["L1_attn_bC"]] * 3)[:, None]),
        "b_dt": tr(inputs["L1_attn_bdt"][:, None]), "b_x": tr(inputs["L1_attn_bx"][:, None]),
        "a_log": tr(inputs["L1_attn_A_log"]),
        "pick": np.concatenate([np.eye(2 * N, dtype=np.float32)] * 3),
        "rows": tr(np.stack([inputs["L1_attn_bz"], inputs["L1_attn_bout"]])[None]),
        "q": tr(inputs["L1_ffn_qweights"].transpose(2, 0, 1)),
        "scale": tr(np.repeat(inputs["L1_ffn_scales"], P // inputs["L1_ffn_scales"].shape[2], axis=2).transpose(2, 0, 1)),
        "lora_a": tr(inputs["L1_ffn_lora_a"].transpose(1, 0, 2)),
        "lora_b": tr(inputs["L1_ffn_lora_b"].transpose(2, 0, 1)),
        "biases": tr(inputs["L1_ffn_biases"][None]),
        "gamma": tr(inputs["L1_ffn_ln_gamma"].T), "beta": tr(inputs["L1_ffn_ln_beta"].T),
        "mu": tr(np.stack([inputs["L0_ffn_mu_r"], inputs["L0_ffn_mu_k"]], 1)),
    }


def kernel(**inputs):
    import numpy as np
    import concourse.bacc as bacc
    from concourse.bass_utils import run_bass_kernel_spmd

    nc = bacc.Bacc("TRN2", target_bir_lowering=False, num_devices=1)
    arrays = lay_out(np, {name: np.asarray(a) for name, a in inputs.items()})
    dram = {name: nc.dram_tensor(name, a.shape, mybir.dt.from_np(a.dtype), kind="ExternalInput").ap()
            for name, a in arrays.items()}
    dram["out"] = nc.dram_tensor("out", (BATCH, T, P), F32, kind="ExternalOutput").ap()
    build(nc, dram)
    r = run_bass_kernel_spmd(nc, [arrays], core_ids=[0])
    return r.results[0]["out"]
```
